# Optimizing a Trainium2 kernel written in Bass

```python
import numpy as np
import jax
import jax.numpy as jnp

def _softmax(x, axis=-1):
    return jax.nn.softmax(x, axis=axis)

def _gelu(x):
    return jax.nn.gelu(x, approximate=True)

def _silu(x):
    return jax.nn.silu(x)

def _sigmoid(x):
    return jax.nn.sigmoid(x)

def _layernorm(x, axis=-1, eps=1e-05):
    m = jnp.mean(x, axis=axis, keepdims=True)
    v = jnp.var(x, axis=axis, keepdims=True)
    return (x - m) / jnp.sqrt(v + eps)

def _scatter_add(tgt, idx, src, axis=0):
    return tgt.at[idx].add(src)

def _segment_sum(src, seg, n):
    return jax.ops.segment_sum(src, seg, n)
kernel_name = 'mk_flamingo_gated_d2_seqx_r4_373877'

def setup_inputs(seed: int=0):
    np.random.seed(seed)
    _w = jnp.asarray

    def _rec_inputs():
        import jax
        import jax.numpy as jnp
        _rk = jax.random.key(seed)
        x = 7.22e-05 + 1 * jax.random.normal(jax.random.fold_in(_rk, 1), (2, 1024, 256), jnp.float32)
        _lenS = 1024 - jax.random.randint(jax.random.fold_in(_rk, 7), (2,), 0, max(1, 1024 // 4) + 1, jnp.int32)
        _lenS2 = 77 - jax.random.randint(jax.random.fold_in(_rk, 8), (2,), 0, max(1, 77 // 4) + 1, jnp.int32)
        _ctx_1024P = jax.random.normal(jax.random.fold_in(_rk, 11), (2, 16, 256), jnp.float32)
        _ctx_1024c = jax.random.dirichlet(jax.random.fold_in(_rk, 511), 0.3 * jnp.ones((16,), jnp.float32), (2, 77))
        _ctx_1024t = jnp.einsum('bsk,bkd->bsd', _ctx_1024c, _ctx_1024P)
        _ctx_1024t = _ctx_1024t * jax.lax.rsqrt(jnp.mean(jnp.square(_ctx_1024t)) + 1e-12) * 0.953939
        ctx_1024 = 4.13588e-05 + 0.999923 * (_ctx_1024t + 0.3 * jax.random.normal(jax.random.fold_in(_rk, 611), (2, 77, 256), jnp.float32))
        _validS = jnp.arange(1024)[None, :] < _lenS[:, None]
        _validS2 = jnp.arange(77)[None, :] < _lenS2[:, None]
        _causal = jnp.tril(jnp.ones((1024, 1024), dtype=bool))
        mask_Bx1xS2_bk0 = jnp.logical_not(jnp.broadcast_to(_validS2[:, None, :], (2, 1, 77)))
        mask_BxSxS2_ik0 = jnp.where(jnp.broadcast_to(_validS2[:, None, :], (2, 1024, 77)), 0, 1).astype(jnp.int32)
        _g = jax.random.normal(jax.random.fold_in(_rk, 9001), (2, 2), jnp.float32)
        _g = jnp.sign(_g) * jnp.maximum(jnp.abs(_g), 1.0) + (_g == 0) * 1.0
        g_xattn = _g[0]
        g_ffn = _g[1]
        return (x, ctx_1024, mask_Bx1xS2_bk0, mask_BxSxS2_ik0, g_xattn, g_ffn)
    x, ctx_1024, mask_Bx1xS2_bk0, mask_BxSxS2_ik0, g_xattn, g_ffn = _rec_inputs()

    def _L0_xattn_setup():
        import jax, jax.numpy as jnp
        import numpy as np
        B, S, E, H = (4, 512, 256, 16)
        DH = E // H

        def _make_heads(v, n_heads):
            b, n, e = v.shape
            return jnp.moveaxis(v.reshape(b, n, n_heads, e // n_heads), -2, 0)
        key = jax.random.key(seed)
        k1, k2, k3, k4, k5 = jax.random.split(key, 5)
        return {'query': jax.random.normal(k1, (B, S, E), dtype=jnp.float32), 'key': jax.random.normal(k2, (B, S, E), dtype=jnp.float32), 'value': jax.random.normal(k3, (B, S, E), dtype=jnp.float32), 'mask': jax.random.randint(k4, (B, 1, S), 0, 2).astype(bool), 'W_out': jax.random.normal(k5, (E, E), dtype=jnp.float32) / np.sqrt(E), 'scale': jnp.asarray(1.0, dtype=jnp.float32), 'log_C': jnp.asarray(np.log(10.0), dtype=jnp.float32)}
    _L0_xattn_all = _L0_xattn_setup()
    _L0_xattn_in = {k: v for k, v in _L0_xattn_all.items() if k in ('W_out', 'scale', 'log_C')}
    del _L0_xattn_all

    def _L0_ffn_setup():
        import jax, jax.numpy as jnp
        import numpy as np
        N_EMBD = 256
        EXPERT_SIZES = [(4, 256), (4, 512)]
        TOP_K = 2
        B, S = (1, 512)
        WIDTHS = []
        for count, size in EXPERT_SIZES:
            WIDTHS += [size] * count
        OFFSETS = np.concatenate([[0], np.cumsum(WIDTHS)]).astype(np.int64)
        E = len(WIDTHS)
        TOTAL_W = int(OFFSETS[-1])
        MAX_W = max(WIDTHS)

        def _stack_experts(w1, w2):
            W1e, W2e = ([], [])
            for e in range(E):
                off, wd = (int(OFFSETS[e]), WIDTHS[e])
                pad = MAX_W - wd
                W1e.append(jnp.pad(w1[:, off:off + wd], ((0, 0), (0, pad))))
                W2e.append(jnp.pad(w2[off:off + wd, :], ((0, pad), (0, 0))))
            return (jnp.stack(W1e), jnp.stack(W2e))
        key = jax.random.key(seed)
        k1, k2, k3, k4 = jax.random.split(key, 4)
        x = jax.random.normal(k1, (B, S, N_EMBD), jnp.float32)
        router_w = jax.random.normal(k2, (E, N_EMBD), jnp.float32) * 0.02
        w1 = jax.random.truncated_normal(k3, -3.0, 3.0, (N_EMBD, TOTAL_W), jnp.float32) * 0.02
        w2 = jax.random.truncated_normal(k4, -3.0, 3.0, (TOTAL_W, N_EMBD), jnp.float32) * 0.02
        return {'x': x, 'router_w': router_w, 'w1': w1, 'w2': w2}
    _L0_ffn_all = _L0_ffn_setup()
    _L0_ffn_in = {k: v for k, v in _L0_ffn_all.items() if k in ('router_w', 'w1', 'w2')}
    del _L0_ffn_all

    def _L1_xattn_setup():
        import jax, jax.numpy as jnp
        import numpy as np
        B, NKV, NQ, D, H = (4, 512, 256, 256, 16)
        HD = D // H
        key = jax.random.key(seed)
        ks = jax.random.split(key, 9)
        s = 0.02
        return {'x': jax.random.normal(ks[0], (B, NKV, D), jnp.float32), 'y': jax.random.normal(ks[1], (B, NQ, D), jnp.float32), 'mask': jax.random.randint(ks[2], (B, NQ, NKV), 0, 2, jnp.int32), 'W_kv': jax.random.normal(ks[3], (D, 2 * D), jnp.float32) * s, 'b_kv': jnp.zeros((2 * D,), jnp.float32), 'W_q': jax.random.normal(ks[4], (D, D), jnp.float32) * s, 'b_q': jnp.zeros((D,), jnp.float32), 'W_o': jax.random.normal(ks[5], (D, D), jnp.float32) * s, 'b_o': jnp.zeros((D,), jnp.float32)}
    _L1_xattn_all = _L1_xattn_setup()
    _L1_xattn_in = {k: v for k, v in _L1_xattn_all.items() if k in ('W_kv', 'b_kv', 'W_q', 'b_q', 'W_o', 'b_o')}
    del _L1_xattn_all

    def _L1_ffn_setup():
        import jax, jax.numpy as jnp
        import numpy as np
        D_MODEL, D_FF, RANK = (256, 1024, 64)
        B, S = (4, 1024)
        key = jax.random.key(seed)
        ks = jax.random.split(key, 7)
        return {'x': jax.random.normal(ks[0], (B, S, D_MODEL), dtype=jnp.float32), 'U1': jax.random.normal(ks[1], (D_MODEL, RANK), dtype=jnp.float32) * 0.02, 'V1': jax.random.normal(ks[2], (RANK, D_FF), dtype=jnp.float32) * 0.02, 'b1': jnp.zeros((D_FF,), dtype=jnp.float32), 'U2': jax.random.normal(ks[3], (D_FF, RANK), dtype=jnp.float32) * 0.02, 'V2': jax.random.normal(ks[4], (RANK, D_MODEL), dtype=jnp.float32) * 0.02, 'b2': jnp.zeros((D_MODEL,), dtype=jnp.float32)}
    _L1_ffn_all = _L1_ffn_setup()
    _L1_ffn_in = {k: v for k, v in _L1_ffn_all.items() if k in ('U1', 'V1', 'b1', 'U2', 'V2', 'b2')}
    del _L1_ffn_all
    return {'x': x, 'ctx_1024': ctx_1024, 'mask_Bx1xS2_bk0': mask_Bx1xS2_bk0, 'mask_BxSxS2_ik0': mask_BxSxS2_ik0, 'g_xattn': g_xattn, 'g_ffn': g_ffn, 'L0_xattn_W_out': _L0_xattn_in['W_out'], 'L0_xattn_scale': _L0_xattn_in['scale'], 'L0_xattn_log_C': _L0_xattn_in['log_C'], 'L0_ffn_router_w': _L0_ffn_in['router_w'], 'L0_ffn_w1': _L0_ffn_in['w1'], 'L0_ffn_w2': _L0_ffn_in['w2'], 'L1_xattn_W_kv': _L1_xattn_in['W_kv'], 'L1_xattn_b_kv': _L1_xattn_in['b_kv'], 'L1_xattn_W_q': _L1_xattn_in['W_q'], 'L1_xattn_b_q': _L1_xattn_in['b_q'], 'L1_xattn_W_o': _L1_xattn_in['W_o'], 'L1_xattn_b_o': _L1_xattn_in['b_o'], 'L1_ffn_U1': _L1_ffn_in['U1'], 'L1_ffn_V1': _L1_ffn_in['V1'], 'L1_ffn_b1': _L1_ffn_in['b1'], 'L1_ffn_U2': _L1_ffn_in['U2'], 'L1_ffn_V2': _L1_ffn_in['V2'], 'L1_ffn_b2': _L1_ffn_in['b2']}

def reference(x, ctx_1024, mask_Bx1xS2_bk0, mask_BxSxS2_ik0, g_xattn, g_ffn, L0_xattn_W_out, L0_xattn_scale, L0_xattn_log_C, L0_ffn_router_w, L0_ffn_w1, L0_ffn_w2, L1_xattn_W_kv, L1_xattn_b_kv, L1_xattn_W_q, L1_xattn_b_q, L1_xattn_W_o, L1_xattn_b_o, L1_ffn_U1, L1_ffn_V1, L1_ffn_b1, L1_ffn_U2, L1_ffn_V2, L1_ffn_b2):
    import jax
    import jax.numpy as jnp

    def _L0_xattn_ref(query, key, value, mask, W_out, scale, log_C):
        import jax, jax.numpy as jnp
        import numpy as np
        B, S, E, H = (4, 512, 256, 16)
        DH = E // H

        def _make_heads(v, n_heads):
            b, n, e = v.shape
            return jnp.moveaxis(v.reshape(b, n, n_heads, e // n_heads), -2, 0)
        q = _make_heads(query, H)
        k = _make_heads(key, H)
        v = _make_heads(value, H)
        d_k = q.shape[-1]
        u = jnp.einsum('hbqd,hbkd->hbqk', q, k) * scale / np.sqrt(d_k)
        logits = jnp.tanh(u) * jnp.exp(log_C)
        logits = jnp.where(mask, -jnp.inf, logits)
        attn = jax.nn.softmax(logits, axis=-1)
        out_heads = jnp.einsum('hbqk,hbkd->hbqd', attn, v)
        out = jnp.moveaxis(out_heads, 0, -2).reshape(query.shape)
        return out @ W_out.T

    def _L0_ffn_ref(x, router_w, w1, w2):
        import jax, jax.numpy as jnp
        import numpy as np
        N_EMBD = 256
        EXPERT_SIZES = [(4, 256), (4, 512)]
        TOP_K = 2
        B, S = (1, 512)
        WIDTHS = []
        for count, size in EXPERT_SIZES:
            WIDTHS += [size] * count
        OFFSETS = np.concatenate([[0], np.cumsum(WIDTHS)]).astype(np.int64)
        E = len(WIDTHS)
        TOTAL_W = int(OFFSETS[-1])
        MAX_W = max(WIDTHS)

        def _stack_experts(w1, w2):
            W1e, W2e = ([], [])
            for e in range(E):
                off, wd = (int(OFFSETS[e]), WIDTHS[e])
                pad = MAX_W - wd
                W1e.append(jnp.pad(w1[:, off:off + wd], ((0, 0), (0, pad))))
                W2e.append(jnp.pad(w2[off:off + wd, :], ((0, pad), (0, 0))))
            return (jnp.stack(W1e), jnp.stack(W2e))
        b, s, d = x.shape
        xf = x.reshape(-1, d)
        logits = xf @ router_w.T
        probs = jax.nn.sigmoid(logits.astype(jnp.float32))
        topw, sel = jax.lax.top_k(probs, TOP_K)
        topw = topw / (topw.sum(-1, keepdims=True) + 1e-20)
        topw = topw.astype(x.dtype)
        onehot = sel[:, :, None] == jnp.arange(E)[None, None, :]
        combine = jnp.sum(topw[:, :, None] * onehot, axis=1)
        W1e, W2e = _stack_experts(w1, w2)
        h = jnp.einsum('td,edw->tew', xf, W1e)
        h = jnp.square(jax.nn.relu(h))
        y = jnp.einsum('tew,ewd->ted', h, W2e)
        out = jnp.einsum('ted,te->td', y, combine)
        return out.reshape(b, s, d)

    def _L1_xattn_ref(x, y, mask, W_kv, b_kv, W_q, b_q, W_o, b_o):
        import jax, jax.numpy as jnp
        import numpy as np
        B, NKV, NQ, D, H = (4, 512, 256, 256, 16)
        HD = D // H
        b, nkv, _ = x.shape
        nq = y.shape[1]
        kv = x @ W_kv + b_kv
        q = y @ W_q + b_q
        kv = kv.reshape(b, nkv, H, 2 * HD).transpose(0, 2, 1, 3)
        q = q.reshape(b, nq, H, HD).transpose(0, 2, 1, 3)
        k, v = (kv[..., :HD], kv[..., HD:])
        scores = jnp.einsum('bhqd,bhkd->bhqk', q, k) / jnp.sqrt(jnp.float32(HD))
        scores = jnp.where(mask[:, None, :, :] == 0, jnp.float32(-1e+20), scores)
        attn = jax.nn.softmax(scores, axis=-1)
        vals = jnp.einsum('bhqk,bhkd->bhqd', attn, v)
        vals = vals.transpose(0, 2, 1, 3).reshape(b, nq, D)
        return vals @ W_o + b_o

    def _L1_ffn_ref(x, U1, V1, b1, U2, V2, b2):
        import jax, jax.numpy as jnp
        import numpy as np
        D_MODEL, D_FF, RANK = (256, 1024, 64)
        B, S = (4, 1024)
        P = jnp.einsum('bsd,dr->bsr', x, U1)
        H = jax.nn.gelu(jnp.einsum('bsr,rf->bsf', P, V1) + b1)
        Q = jnp.einsum('bsf,fr->bsr', H, U2)
        return jnp.einsum('bsr,rd->bsd', Q, V2) + b2
    x = x + jnp.tanh(g_xattn[0]) * _L0_xattn_ref(_layernorm(x, axis=-1), ctx_1024, ctx_1024, mask_Bx1xS2_bk0, L0_xattn_W_out, L0_xattn_scale, L0_xattn_log_C)
    x = x + jnp.tanh(g_ffn[0]) * _L0_ffn_ref(_layernorm(x, axis=-1), L0_ffn_router_w, L0_ffn_w1, L0_ffn_w2)
    x = x + jnp.tanh(g_xattn[1]) * _L1_xattn_ref(ctx_1024, _layernorm(x, axis=-1), mask_BxSxS2_ik0, L1_xattn_W_kv, L1_xattn_b_kv, L1_xattn_W_q, L1_xattn_b_q, L1_xattn_W_o, L1_xattn_b_o)
    x = x + jnp.tanh(g_ffn[1]) * _L1_ffn_ref(_layernorm(x, axis=-1), L1_ffn_U1, L1_ffn_V1, L1_ffn_b1, L1_ffn_U2, L1_ffn_V2, L1_ffn_b2)
    return x

_drawn_inputs = setup_inputs


def setup_inputs(seed=0):
    import zlib

    import numpy as np

    out = dict(_drawn_inputs(seed))
    spreads = {'g_ffn': (-1.0, 0.6),
     'L1_xattn_b_kv': (0.0, 0.324),
     'L1_xattn_b_q': (0.0, 2.0),
     'L1_xattn_b_o': (0.0, 0.1),
     'L1_ffn_b1': (0.0, 0.8),
     'L1_ffn_b2': (0.0, 0.8)}
    factors = {'L0_ffn_router_w': 3.059,
     'L0_ffn_w1': 2.904,
     'L1_xattn_W_q': 8.0,
     'L1_ffn_U1': 8.0,
     'L1_ffn_V1': 8.0,
     'L1_ffn_U2': 8.0,
     'L1_ffn_V2': 8.0}
    for name, (base, spread) in spreads.items():
        noise = np.random.default_rng([zlib.crc32(name.encode()), seed]).standard_normal(out[name].shape)
        drawn = base * np.exp(spread * noise) if base else spread * noise
        out[name] = jnp.asarray(drawn.astype(out[name].dtype))
    for name, factor in factors.items():
        out[name] = (out[name] * factor).astype(out[name].dtype)
    return out
```

```python
from contextlib import ExitStack

import concourse.bass as bass
from concourse import mybir

F32 = mybir.dt.float32
F32R = mybir.dt.float32r
BF16 = mybir.dt.bfloat16
I32 = mybir.dt.int32
U8 = mybir.dt.uint8
ALU = mybir.AluOpType
ACT = mybir.ActivationFunctionType
AX = mybir.AxisListType

P = 128
B, S, E = 2, 1024, 256
H, DH = 16, 16
KEYS = 77
G = 2
HG = H // G
KC = P // HG
NC = -(-KEYS // KC)
T = 512
NT = T // P
NB = S // T
KE = E // P
HALF = (KEYS + 1) // 2
WIDTHS = [256] * 4 + [512] * 4
NX = len(WIDTHS)
TOTAL = sum(WIDTHS)
CH = [(e, j == 0, j == w // P - 1) for e, w in enumerate(WIDTHS) for j in range(w // P)]
NH = len(CH)
RANK = 64
NF = 1024 // P
MASKED = -1e20
REMOVED = -1e30
EPS = 1e-5
NP = 3
ROUTE = 19


C_MINUS = 2 * P + 2 * HG
C_ROWS = C_MINUS + G * P


def rows_of(c):
    return HG * (min(KEYS, KC * (c + 1)) - KC * c)


def flamingo(nc, x, ctx_rows, ctx_t, mask0, mask1, gates, logc, scale0, w_out_t, router_t, w1, w2, wk, wv, bk, bv,
             wq, bq, wo, bo, u1, v1, b1, u2, v2, b2, consts, out):
    stack = ExitStack()
    with stack:
        def sb(name, shape, dt=F32):
            return stack.enter_context(nc.sbuf_tensor(name, shape, dt))

        def ps(name):
            return stack.enter_context(nc.psum_tensor(name, [P, 2, 512], F32))

        def sem(name):
            return stack.enter_context(nc.semaphore(name))

        cst = sb("cst", [P, 2 * P + 2 * HG])
        ident, same_head = cst[:, 0:P], cst[:, P:2 * P]
        head_of_feature, rank_of_expert = cst[:, 2 * P:2 * P + HG], cst[:, 2 * P + HG:2 * P + 2 * HG]
        minus_head = sb("minus_head", [32, G, P], F32R)
        ident_b = sb("ident_b", [P, P], BF16)
        rows_of_key = sb("rows_of_key", [KEYS, KEYS * HG], BF16)
        minus_half, eps_sb, aside = sb("minus_half", [P, NT]), sb("eps_sb", [P, NT]), sb("aside", [P, 1])
        w1h, w1l = sb("w1h", [P, KE, TOTAL], F32R), sb("w1l", [P, KE, TOTAL], F32R)
        w2h, w2l = sb("w2h", [P, NH, E], F32R), sb("w2l", [P, NH, E], F32R)
        rth, rtl = sb("rth", [P, KE, NX], F32R), sb("rtl", [P, KE, NX], F32R)
        rt_raw = sb("rt_raw", [P, KE, NX])
        w_out_sb, wk_sb, wv_sb, wq_sb, wo_sb = (sb(n, [P, KE, E]) for n in ("w_out_sb", "wk_sb", "wv_sb", "wq_sb", "wo_sb"))
        u1_sb, u2_sb = sb("u1_sb", [P, KE, RANK]), sb("u2_sb", [P, NF, RANK])
        v1_sb, v2_sb = sb("v1_sb", [RANK, NF * P]), sb("v2_sb", [RANK, E])
        bk_sb, bq_sb, b1_sb = sb("bk_sb", [P, G]), sb("bq_sb", [P, G]), sb("b1_sb", [P, NF])
        bv_rows, bo_rows, b2_rows = sb("bv_rows", [P, E]), sb("bo_rows", [P, E]), sb("b2_rows", [P, E])
        gate_raw, gate = sb("gate_raw", [P, 4]), sb("gate", [P, 4])
        cap, scale_raw, scale_q = sb("cap", [P, 3]), sb("scale_raw", [P, 1]), sb("scale_q", [P, 1])
        cT = sb("cT", [P, KE, KEYS])
        mask0_sb = sb("mask0_sb", [P, NC], U8)
        mask1_sb = sb("mask1_sb", [P, NB * NT, KEYS], I32)
        mbias = sb("mbias", [P, NB * NT, KEYS], BF16)
        mbT = sb("mbT", [KEYS, S], BF16)
        ebias = sb("ebias", [P, NC])
        k1T = sb("k1T", [P, G, KEYS])
        kd = [sb("kd0", [P, G, KEYS * HG]), sb("kd1", [P, G, KEYS * HG])]
        kd1h = sb("kd1h", [P, G, KEYS * HG], F32R)
        vd = [sb("vd0", [P, NC, E]), sb("vd1", [P, NC, E])]
        xin = sb("xin", [P, NB * NT, E])
        xs = sb("xs", [P, NB * NT, E])
        xT = sb("xT", [P, KE, T])
        xTh, xTl = sb("xTh", [P, KE, T], F32R), sb("xTl", [P, KE, T], F32R)
        bstat, mv = sb("bstat", [P, NT, 6]), sb("mv", [P, NT, 2])
        veps, rstd = sb("veps", [P, NT]), sb("rstd", [P, NT])
        work = sb("work", [P, 7, T])
        th, pr, psm = work[:, 0:2], work[:, 2:2 + NP], work[:, 5:7]
        qT = th
        ur, hf, gl = work[:, 0:2], work[:, 2:4], work[:, 0:2]
        xn = sb("xn", [P, NT, E])
        at = xn[:, :, :].rearrange("p t e -> p (t e)").rearrange("p (g n) -> p g n", g=G)
        hh, hl = sb("hh", [P, 2, T], F32R), sb("hl", [P, 2, T], F32R)
        qTh = hh
        mx, mxs = sb("mx", [P, NT, H]), sb("mxs", [P, NT, 2, H])
        mxT = hl[0:32, 0, :]
        route = work[:, 6, 0:12 * NT * NX].rearrange("p (i t e) -> p i t e", t=NT, e=NX)
        rone = sb("rone", [P, 8, NT])
        comb = sb("comb", [P, NT, NX])
        pT, qq = at[0:RANK, 0], at[0:RANK, 1]

        Sb, Ob, Yb, Tb = ps("Sb"), ps("Ob"), ps("Yb"), ps("Tb")
        Y2 = [Yb, Ob]

        def tiles(bank_pair):
            return bank_pair[:, :, :].rearrange("p a (b n) -> p (a b) n", n=E)

        minus_head_raw = work[0:32, 6, 0:G * P].rearrange("p (g n) -> p g n", g=G)
        sel_raw = xn[0:KEYS, :, :].rearrange("p t e -> p (t e)")[:, 0:KEYS * HG]
        ctx_wide = work[:, 0:3, :].rearrange("p a n -> p (a n)")[:, 0:KE * KEYS * HG].rearrange("p (k n) -> p k n", k=KE)
        raw = work[:, 0:6, :].rearrange("p a n -> p (a n)").rearrange("p (r n) -> p r n", r=2)

        carried = sem("carried")
        weights_loaded = sem("weights_loaded")
        gates_loaded = sem("gates_loaded")
        raw_loaded = [sem("raw_loaded0"), sem("raw_loaded1")]
        raw_high = sem("raw_high")
        raw_low = sem("raw_low")
        ready, pool_ready, cleared = sem("ready"), sem("pool_ready"), sem("cleared")
        gates_ready = sem("gates_ready")
        ctx_loaded, ctx_used = sem("ctx_loaded"), sem("ctx_used")
        vd0_loaded = sem("vd0_loaded")
        xin_loaded = sem("xin_loaded")
        prep = sem("prep")
        kv_done = sem("kv_done")
        stat, aggr, vare, rstd_done = sem("stat"), sem("aggr"), sem("vare"), sem("rstd_done")
        xn_done, turned, xT_act, xT_dve = sem("xn_done"), sem("turned"), sem("xT_act"), sem("xT_dve")
        scored = [sem("scored0"), sem("scored1")]
        capped = sem("capped")
        prob = [sem("prob0"), sem("prob1")]
        summed = [sem("summed0"), sem("summed1")]
        weighed = [sem("weighed0"), sem("weighed1")]
        total = [sem("total0"), sem("total1")]
        inverse = [sem("inverse0"), sem("inverse1")]
        normed = [sem("normed0"), sem("normed1")]
        projected = [sem("projected0"), sem("projected1")]
        added = [sem("added0"), sem("added1")]
        routed, odds, route_step, comb_done = sem("routed"), sem("odds"), sem("route_step"), sem("comb_done")
        hidden, rectified, squared = sem("hidden"), sem("rectified"), sem("squared")
        high, low, down, mixed = sem("high"), sem("low"), sem("down"), sem("mixed")
        q_done, q_act = sem("q_done"), sem("q_act")
        rowscores, rowmax, split_max, max_turned, max_ready = (
            sem("rowscores"), sem("rowmax"), sem("split_max"), sem("max_turned"), sem("max_ready"))
        biased = sem("biased")
        low1, low1_copied, inner, gelu_done, low2, low2_copied = (
            sem("low1"), sem("low1_copied"), sem("inner"), sem("gelu_done"), sem("low2"), sem("low2_copied"))
        ffn_done, res_done, stored = sem("ffn_done"), sem("res_done"), [sem("stored0"), sem("stored1")]

        PREP = 1 + 1 + 1 + 2 + 1 + 1 + 2 + 2 + 1 + NC + 1

        def per_batch(b, n, k):
            return b * n + k

        def per_block(b, j, n, k):
            return b * (NB * n) + (j * n + k)

        w1_pieces = [(k, s) for k in range(KE) for s in range(0, TOTAL, 1536)]
        w2_pieces = list(range(0, NH, 6))
        w2_v = w2.rearrange("(j p) d -> p j d", p=P)
        NPIECE = len(w1_pieces) + len(w2_pieces)

        def piece(t, i):
            if i < len(w1_pieces):
                k, s = w1_pieces[i]
                return t[0][:, k, s:s + 1536]
            j = w2_pieces[i - len(w1_pieces)]
            return t[1][:, j:j + 6, :].rearrange("p j d -> p (j d)")

        NW = 25
        block = stack.enter_context(nc.Block())

        @block.sync
        def _(sp):
            def carry():
                sp.sem_inc(carried, 1)

            def load_ctx(b):
                sp.dma_start(cT[:], ctx_t[b].rearrange("(k p) n -> p k n", p=P)).then_inc(ctx_loaded, 16)
                sp.dma_start(mask1_sb[:], mask1[b].rearrange("(t p) n -> p t n", p=P)).then_inc(ctx_loaded, 16)
                for c in range(NC):
                    n = rows_of(c) // HG
                    src = mask0[b, KC * c:KC * c + n].unsqueeze(1).unsqueeze(1).to_broadcast([n, HG, 1])
                    sp.dma_start(mask0_sb[0:n * HG, c:c + 1], src).then_inc(ctx_loaded, 16)

            def load_vd0(b):
                for c in range(NC):
                    n = rows_of(c) // HG
                    src = ctx_rows[b, KC * c:KC * c + n, :].unsqueeze(1).to_broadcast([n, HG, E])
                    sp.dma_start(vd[0][0:n * HG, c, :], src).then_inc(vd0_loaded, 16)

            def load_x(b):
                sp.dma_start(xin[:], x[b].rearrange("(t p) e -> p t e", p=P)).then_inc(xin_loaded, 16)

            def store(b, j):
                sp.wait_ge(res_done, per_block(b, j, NT, NT))
                carry()
                sp.dma_start(out[b, j * T:(j + 1) * T, :].rearrange("(t p) e -> p t e", p=P),
                             xs[:, j * NT:(j + 1) * NT, :]).then_inc(stored[j], 16)

            sp.dma_start(gate_raw[:], gates.partition_broadcast(P)).then_inc(gates_loaded, 16)
            sp.dma_start(cap[:, 0:1], logc.partition_broadcast(P)).then_inc(gates_loaded, 16)
            sp.dma_start(scale_raw[:], scale0.partition_broadcast(P)).then_inc(gates_loaded, 16)
            sp.dma_start(cst[:], consts[:, 0:2 * P + 2 * HG]).then_inc(weights_loaded, 16)
            sp.dma_start(work[0:32, 6, 0:G * P],
                         consts[0:32, C_MINUS:C_ROWS]).then_inc(weights_loaded, 16)
            sp.dma_start(sel_raw, consts[0:KEYS, C_ROWS:]).then_inc(weights_loaded, 16)
            sp.wait_ge(cleared, 2)
            load_ctx(0)
            load_vd0(0)
            load_x(0)
            for dst, src in ((w_out_sb, w_out_t), (wk_sb, wk), (wv_sb, wv), (wq_sb, wq), (wo_sb, wo)):
                sp.dma_start(dst[:], src.rearrange("(k p) n -> p k n", p=P)).then_inc(weights_loaded, 16)
            for dst, src in ((rt_raw, router_t), (u1_sb, u1), (u2_sb, u2)):
                sp.dma_start(dst[:], src.rearrange("(k p) n -> p k n", p=P)).then_inc(weights_loaded, 16)
            for dst, src in ((v1_sb, v1), (v2_sb, v2), (bk_sb, bk), (bq_sb, bq), (b1_sb, b1)):
                sp.dma_start(dst[:], src).then_inc(weights_loaded, 16)
            for dst, src in ((bv_rows, bv), (bo_rows, bo), (b2_rows, b2)):
                sp.dma_start(dst[:], src.partition_broadcast(P)).then_inc(weights_loaded, 16)
            for i in range(NPIECE):
                if i >= 2:
                    sp.wait_ge(raw_low, i - 1)
                src = piece((w1.rearrange("(k p) n -> p k n", p=P), None), i) if i < len(w1_pieces) else \
                    w2_v[:, w2_pieces[i - len(w1_pieces)]:w2_pieces[i - len(w1_pieces)] + 6, :]
                dst = raw[:, i % 2, :]
                if i >= len(w1_pieces):
                    dst = dst.rearrange("p (j d) -> p j d", d=E)
                sp.dma_start(dst, src).then_inc(raw_loaded[i % 2], 16)
            with sp.Fori(0, B) as b:
                other = sp.snap(1 - b)
                sp.wait_ge(prep, per_batch(b, PREP, PREP))
                sp.wait_ge(kv_done, per_batch(b, 3, 3))
                carry()
                load_ctx(other)
                store(b, 0)
                sp.wait_ge(weighed[0], per_block(b, NB - 1, G * NC, G * NC))
                carry()
                load_vd0(other)
                sp.wait_ge(added[0], per_block(b, NB - 1, NT, NT))
                carry()
                load_x(other)
                store(b, 1)
            for j in range(NB):
                sp.wait_ge(stored[j], 16 * (B + 1))
            sp.wait_ge(ctx_loaded, 16 * (2 + NC) * (B + 1))
            sp.wait_ge(vd0_loaded, 16 * NC * (B + 1))
            sp.wait_ge(xin_loaded, 16 * (B + 1))

        @block.tensor
        def _(pe):
            def split3(o, ah, al, bh, bl, first, last):
                pe.matmul(o, ah, bl, start=first, stop=False, skip_group_check=True)
                pe.matmul(o, al, bh, start=False, stop=False, skip_group_check=True)
                return pe.matmul(o, ah, bh, start=False, stop=last, skip_group_check=True)

            def turn(b, j, s):
                pe.wait_ge(xn_done, per_block(b, j, 4 * NT, NT * (s + 1)))
                for k in range(KE):
                    for t in range(NT):
                        ins = pe.transpose(Tb[:, k, t * P:(t + 1) * P], xn[:, t, k * P:(k + 1) * P], ident)
                    ins.then_inc(turned, 1)

            def xT_ready(b, j, upto):
                pe.wait_ge(xT_act, per_block(b, j, 5, upto))
                pe.wait_ge(xT_dve, per_block(b, j, 5, upto))

            def attend(b, j, a):
                for n in range(G * NC + 1):
                    if n < G * NC:
                        g, c = divmod(n, NC)
                        r = rows_of(c)
                        s = Sb[0:r, n % 2, :]
                        if n >= 2:
                            pe.wait_ge(capped if a == 0 else prob[1], per_block(b, j, G * NC, n - 1))
                        kk = kd[a][:, g, KC * HG * c:KC * HG * c + r]
                        if a == 0:
                            ins = pe.matmul(s, kk, xT[:, g, :], start=True, stop=True)
                        else:
                            pe.matmul(s, rows_of_key[:, KC * HG * c:KC * HG * c + r], mbT[:, j * T:(j + 1) * T],
                                      start=True, stop=False, skip_group_check=True)
                            pe.matmul(s, kk, qT[:, g, :], start=False, stop=False, skip_group_check=True)
                            ins = pe.matmul(s, minus_head[:, g, 0:r], mxT, start=False, stop=True,
                                            skip_group_check=True)
                        ins.then_inc(scored[a], 1)
                    if n >= 1:
                        m = n - 1
                        g, c = divmod(m, NC)
                        r = rows_of(c)
                        pe.wait_ge(prob[a], per_block(b, j, G * NC, m + 1))
                        pe.matmul(Ob[:, g, :], vd[a][0:r, c, g * P:(g + 1) * P], pr[0:r, m % NP, :],
                                  start=(c == 0), stop=(c == NC - 1)).then_inc(weighed[a], 1)
                    for g in range(G):
                        if n == min(NC * (g + 1) + 1, G * NC):
                            pe.wait_ge(summed[a], per_block(b, j, G * (NC - 1), (g + 1) * (NC - 1)))
                            pe.matmul(Tb[:, g, :], same_head, psm[:, g, :], start=True, stop=True).then_inc(total[a], 1)
                w = w_out_sb if a == 0 else wo_sb
                pe.wait_ge(normed[a], per_block(b, j, G, G))
                for t in range(NT):
                    for g in range(G):
                        ins = pe.matmul(tiles(Yb)[:, t, :], at[:, g, t * P:(t + 1) * P], w[:, g, :],
                                        start=(g == 0), stop=(g == G - 1))
                    if t % 2:
                        ins.then_inc(projected[a], 1)

            def prepare(b):
                pe.wait_ge(prep, per_batch(b, PREP, 1))
                for g in range(G):
                    for k in range(KE):
                        ins = pe.matmul(Tb[:, g, 0:KEYS], wk_sb[:, k, g * P:(g + 1) * P], cT[:, k, :],
                                        start=(k == 0), stop=(k == KE - 1))
                ins.then_inc(kv_done, 1)
                for t in range(NB * NT):
                    ins = pe.transpose(Yb[:, 0, :].bitcast(BF16)[0:KEYS, t * P:(t + 1) * P], mbias[:, t, :], ident_b[:])
                ins.then_inc(kv_done, 1)
                pe.wait_ge(prep, per_batch(b, PREP, 3))
                for c in range(NC):
                    r = rows_of(c)
                    o = tiles(Sb)[0:r, c, :] if c < 4 else tiles(Ob)[0:r, 0, :]
                    for k in range(KE):
                        keys = ctx_wide[:, k, KC * HG * c:KC * HG * c + r]
                        ins = pe.matmul(o, keys, wv_sb[:, k, :], start=(k == 0), stop=(k == KE - 1))
                ins.then_inc(kv_done, 1)

            def experts(b, j):
                xT_ready(b, j, 3)
                for t in range(NT):
                    o = Tb[:, 0, t * NX:(t + 1) * NX]
                    for k in range(KE):
                        ts = slice(t * P, (t + 1) * P)
                        ins = split3(o, xTh[:, k, ts], xTl[:, k, ts], rth[:, k, :], rtl[:, k, :], k == 0, k == KE - 1)
                ins.then_inc(routed, 1)
                for n in range(NH + 1):
                    if n < NH:
                        if n >= 2:
                            pe.wait_ge(squared, per_block(b, j, NH, n - 1))
                        for k in range(KE):
                            ws = slice(n * P, (n + 1) * P)
                            ins = split3(Sb[:, n % 2, :], w1h[:, k, ws], w1l[:, k, ws], xTh[:, k, :], xTl[:, k, :],
                                         k == 0, k == KE - 1)
                        ins.then_inc(hidden, 1)
                    if n >= 1:
                        m = n - 1
                        e, first, last = CH[m]
                        pe.wait_ge(low, per_block(b, j, NH, m + 1))
                        if first and e >= 2:
                            pe.wait_ge(mixed, per_block(b, j, NX * NT, (e - 1) * NT))
                        y = tiles(Y2[e % 2])
                        for t in range(NT):
                            ts = slice(t * P, (t + 1) * P)
                            ins = split3(y[:, t, :], hh[:, m % 2, ts], hl[:, m % 2, ts], w2h[:, m, :], w2l[:, m, :],
                                         first and t % 2 == 0, last)
                        ins.then_inc(down, 1)

            def queries(b, j):
                xT_ready(b, j, 4)
                for g in range(G):
                    for k in range(KE):
                        ins = pe.matmul(Ob[:, g, :], wq_sb[:, k, g * P:(g + 1) * P], xT[:, k, :],
                                        start=(k == 0), stop=(k == KE - 1))
                    ins.then_inc(q_done, 1)
                pe.wait_ge(q_act, per_block(b, j, 2 * G, 2 * G))
                for t in range(NT):
                    for g in range(G):
                        n = t * G + g
                        bank = (Sb, Tb)[n % 2]
                        if n >= 2:
                            pe.wait_ge(rowmax, per_block(b, j, NT * G, n - 1))
                        for i in range(2):
                            k0 = (0, KEYS - HALF)[i]
                            o = bank[:, i, 0:HALF * HG].rearrange("p (k h) -> p k h", h=HG)
                            m = mbias[:, j * NT + t, k0:k0 + HALF].unsqueeze(2).to_broadcast([P, HALF, HG])
                            pe.matmul(o, ident_b[:], m, start=True, stop=False)
                            ins = pe.matmul(bank[:, i, 0:HALF * HG], qTh[:, g, t * P:(t + 1) * P],
                                            kd1h[:, g, k0 * HG:(k0 + HALF) * HG], start=False, stop=True)
                        ins.then_inc(rowscores, 1)
                pe.wait_ge(split_max, per_block(b, j, 2, 2))
                for t in range(NT):
                    ins = pe.transpose(Yb[0:32, 0, t * P:(t + 1) * P],
                                       mxs[:, t, :, :].rearrange("p a h -> p (a h)"), ident)
                ins.then_inc(max_turned, 1)
                pe.wait_ge(max_ready, per_block(b, j, 1, 1))

            def low_rank(b, j):
                xT_ready(b, j, 5)
                for k in range(KE):
                    ins = pe.matmul(Ob[0:RANK, 0, :], u1_sb[:, k, :], xT[:, k, :], start=(k == 0), stop=(k == KE - 1))
                ins.then_inc(low1, 1)
                pe.wait_ge(low1_copied, per_block(b, j, 1, 1))
                for n in range(NF + 1):
                    if n < NF:
                        if n >= 2:
                            pe.wait_ge(gelu_done, per_block(b, j, NF, n - 1))
                        pe.matmul(Sb[:, n % 2, :], v1_sb[:, n * P:(n + 1) * P], pT,
                                  start=True, stop=True).then_inc(inner, 1)
                    if n >= 1:
                        m = n - 1
                        pe.wait_ge(gelu_done, per_block(b, j, NF, m + 1))
                        pe.matmul(Ob[0:RANK, 1, :], u2_sb[:, m, :], gl[:, m % 2, :],
                                  start=(m == 0), stop=(m == NF - 1)).then_inc(low2, 1)
                pe.wait_ge(low2_copied, per_block(b, j, 1, 1))
                for t in range(NT):
                    ins = pe.matmul(tiles(Yb)[:, t, :], qq[:, t * P:(t + 1) * P], v2_sb[:], start=True, stop=True)
                    if t % 2:
                        ins.then_inc(ffn_done, 1)

            pe.wait_ge(weights_loaded, 16 * 19)
            pe.wait_ge(ready, 9)
            pe.wait_ge(raw_low, NPIECE)
            with pe.Fori(0, B) as b:
                prepare(b)
                for j in range(NB):
                    turn(b, j, 0)
                    xT_ready(b, j, 1)
                    if j == 0:
                        pe.wait_ge(prep, per_batch(b, PREP, PREP))
                    attend(b, j, 0)
                    turn(b, j, 1)
                    experts(b, j)
                    turn(b, j, 2)
                    queries(b, j)
                    attend(b, j, 1)
                    turn(b, j, 3)
                    low_rank(b, j)

        @block.scalar
        def _(act):
            def turned_copy(b, j, s, split):
                for k in range(KE if split else 1):
                    act.wait_ge(turned, per_block(b, j, 4 * KE, KE * s + k + 1))
                    dst = xTh[:, k, :] if split else xT[:, 0, :]
                    nc.scalar.activation(dst, Tb[:, k, :], ACT.Copy).then_inc(xT_act, 1)

            def probs(b, j, a):
                for n in range(G * NC + 1):
                    if a == 0 and n < G * NC:
                        r = rows_of(n % NC)
                        act.wait_ge(scored[0], per_block(b, j, G * NC, n + 1))
                        nc.scalar.activation(th[0:r, n % 2, :], Sb[0:r, n % 2, :], ACT.Tanh,
                                             scale=scale_q[0:r, :]).then_inc(capped, 1)
                    if n >= 1:
                        m = n - 1
                        c = m % NC
                        r = rows_of(c)
                        if m >= NP:
                            act.wait_ge(weighed[a], per_block(b, j, G * NC, m - NP + 1))
                            g0, c0 = divmod(m - NP, NC)
                            act.wait_ge(summed[a], per_block(b, j, G * (NC - 1), g0 * (NC - 1) + max(c0, 1)))
                        if a == 0:
                            act.wait_ge(capped, per_block(b, j, G * NC, m + 1))
                            nc.scalar.activation(pr[0:r, m % NP, :], th[0:r, m % 2, :], ACT.Exp, scale=cap[0:r, 1:2],
                                                 bias=ebias[0:r, c:c + 1]).then_inc(prob[0], 1)
                        else:
                            act.wait_ge(scored[1], per_block(b, j, G * NC, m + 1))
                            nc.scalar.activation(pr[0:r, m % NP, :], Sb[0:r, m % 2, :], ACT.Exp,
                                                 scale=DH ** -0.5).then_inc(prob[1], 1)

            act.wait_ge(gates_loaded, 48)
            nc.scalar.activation(gate[:], gate_raw[:], ACT.Tanh).then_inc(gates_ready, 1)
            nc.scalar.activation(cap[:, 1:2], cap[:, 0:1], ACT.Exp).then_inc(gates_ready, 1)
            act.wait_ge(gates_ready, 2)
            nc.scalar.mul(cap[:, 2:3], cap[:, 1:2], -1.0).then_inc(gates_ready, 1)
            nc.scalar.mul(scale_q[:], scale_raw[:], DH ** -0.5).then_inc(gates_ready, 1)
            act.wait_ge(gates_ready, 4)
            for i in range(NPIECE):
                act.wait_ge(raw_loaded[i % 2], 16 * (i // 2 + 1))
                nc.scalar.activation(piece((w1h, w2h), i), raw[:, i % 2, :], ACT.Copy).then_inc(raw_high, 1)
            act.wait_ge(raw_low, NPIECE)
            act.wait_ge(weights_loaded, 16 * 19)
            with act.Fori(0, B) as b:
                for j in range(NB):
                    turned_copy(b, j, 0, False)
                    if j == 0:
                        act.wait_ge(prep, per_batch(b, PREP, 3))
                    probs(b, j, 0)
                    turned_copy(b, j, 1, True)
                    act.wait_ge(routed, per_block(b, j, 1, 1))
                    nc.scalar.activation(route[:, 0, :, :].rearrange("p t e -> p (t e)"), Tb[:, 0, 0:NT * NX], ACT.Exp,
                                         scale=-1.0).then_inc(odds, 1)
                    for n in range(NH + 1):
                        if n < NH:
                            act.wait_ge(hidden, per_block(b, j, NH, n + 1))
                            if n >= 2:
                                act.wait_ge(squared, per_block(b, j, NH, n - 1))
                            nc.scalar.activation(ur[:, n % 2, :], Sb[:, n % 2, :], ACT.Relu).then_inc(rectified, 1)
                        if n < NH:
                            m = n
                            act.wait_ge(squared, per_block(b, j, NH, m + 1))
                            if m >= 2:
                                act.wait_ge(down, per_block(b, j, NH, m - 1))
                            nc.scalar.activation(hh[:, m % 2, :], hf[:, m % 2, :], ACT.Copy).then_inc(high, 1)
                    turned_copy(b, j, 2, False)
                    for g in range(G):
                        act.wait_ge(q_done, per_block(b, j, G, g + 1))
                        nc.scalar.activation(qTh[:, g, :], Ob[:, g, :], ACT.Identity,
                                             bias=bq_sb[:, g:g + 1]).then_inc(q_act, 1)
                        nc.scalar.activation(qT[:, g, :], Ob[:, g, :], ACT.Identity,
                                             bias=bq_sb[:, g:g + 1]).then_inc(q_act, 1)
                    act.wait_ge(max_turned, per_block(b, j, 1, 1))
                    nc.scalar.activation(mxT, Yb[0:32, 0, :], ACT.Copy).then_inc(max_ready, 1)
                    probs(b, j, 1)
                    turned_copy(b, j, 3, False)
                    for n in range(NF):
                        act.wait_ge(inner, per_block(b, j, NF, n + 1))
                        if n >= 2:
                            act.wait_ge(low2, per_block(b, j, NF, n - 1))
                        nc.scalar.activation(gl[:, n % 2, :], Sb[:, n % 2, :], ACT.Gelu_apprx_tanh,
                                             bias=b1_sb[:, n:n + 1]).then_inc(gelu_done, 1)

        @block.gpsimd
        def _(pool):
            def rsqrt(b, j, s):
                pool.wait_ge(aggr, per_block(b, j, 4 * NT, NT * (s + 1)))
                nc.gpsimd.tensor_tensor(veps[:], mv[:, :, 1], eps_sb[:], ALU.add).then_inc(vare, 1)
                pool.wait_ge(vare, per_block(b, j, 4, s + 1))
                nc.gpsimd.tensor_tensor(rstd[:], veps[:], minus_half[:], ALU.pow).then_inc(rstd_done, 1)

            def sum_keys(b, j, a):
                for g in range(G):
                    for c in range(1, NC):
                        r = rows_of(c)
                        pool.wait_ge(prob[a], per_block(b, j, G * NC, g * NC + c + 1))
                        if c > 1:
                            pool.wait_ge(summed[a], per_block(b, j, G * (NC - 1), g * (NC - 1) + c - 1))
                        left = pr[0:r, (g * NC) % NP, :] if c == 1 else psm[0:r, g, :]
                        nc.gpsimd.tensor_tensor(psm[0:r, g, :], left, pr[0:r, (g * NC + c) % NP, :],
                                                ALU.add).then_inc(summed[a], 1)

            nc.gpsimd.memset(minus_half[:], -0.5).then_inc(pool_ready, 1)
            nc.gpsimd.memset(eps_sb[:], EPS).then_inc(pool_ready, 1)
            pool.wait_ge(gates_ready, 4)
            pool.wait_ge(weights_loaded, 16 * 19)
            pool.wait_ge(ready, 9)
            pool.wait_ge(pool_ready, 2)
            pool.wait_ge(raw_low, NPIECE)
            with pool.Fori(0, B) as b:
                for j in range(NB):
                    rows = xs[:, j * NT:(j + 1) * NT, :]
                    rsqrt(b, j, 0)
                    sum_keys(b, j, 0)
                    rsqrt(b, j, 1)
                    rsqrt(b, j, 2)
                    pool.wait_ge(xn_done, per_block(b, j, 4 * NT, 3 * NT))
                    nc.gpsimd.tensor_tensor(rows, rows, bo_rows[:].unsqueeze(1).to_broadcast([P, NT, E]),
                                            ALU.add).then_inc(biased, 1)
                    sum_keys(b, j, 1)
                    rsqrt(b, j, 3)
                    pool.wait_ge(xn_done, per_block(b, j, 4 * NT, 4 * NT))
                    nc.gpsimd.tensor_tensor(rows, rows, b2_rows[:].unsqueeze(1).to_broadcast([P, NT, E]),
                                            ALU.add).then_inc(biased, 1)

        @block.vector
        def _(dve):
            v = nc.vector

            def norm(b, j, s):
                src = xin if s == 0 else xs
                if s == 0:
                    dve.wait_ge(xin_loaded, b * 16 + 16)
                elif s == 1:
                    dve.wait_ge(added[0], per_block(b, j, NT, NT))
                elif s == 2:
                    dve.wait_ge(mixed, per_block(b, j, NX * NT, NX * NT))
                else:
                    dve.wait_ge(added[1], per_block(b, j, NT, NT))
                for t in range(NT):
                    v.bn_stats(bstat[:, t, :], src[:, j * NT + t, :]).then_inc(stat, 1)
                dve.wait_ge(stat, per_block(b, j, 4 * NT, NT * (s + 1)))
                v.memset(aside[:], 0.0)
                for t in range(NT):
                    v.bn_aggr(mv[:, t, :], bstat[:, t, :]).then_inc(aggr, 1)
                dve.wait_ge(aggr, per_block(b, j, 4 * NT, NT * (s + 1)))
                dve.wait_ge(rstd_done, per_block(b, j, 4, s + 1))
                for t in range(NT):
                    v.tensor_scalar(xn[:, t, :], src[:, j * NT + t, :], mv[:, t, 0:1], rstd[:, t:t + 1],
                                    ALU.subtract, ALU.mult).then_inc(xn_done, 1)

            def turned_copy(b, j, s, split):
                for k in (range(KE) if split else [1]):
                    dve.wait_ge(turned, per_block(b, j, 4 * KE, KE * s + k + 1))
                    if split:
                        dve.wait_ge(xT_act, per_block(b, j, 5, k + 2))
                        v.tensor_tensor(xTl[:, k, :], Tb[:, k, :], xTh[:, k, :].bitcast(F32),
                                        ALU.subtract).then_inc(xT_dve, 1)
                    else:
                        v.tensor_copy(xT[:, 1, :], Tb[:, 1, :]).then_inc(xT_dve, 1)

            def attended(b, j, a):
                for g in range(G):
                    dve.wait_ge(total[a], per_block(b, j, G, g + 1))
                    v.reciprocal(at[:, g, :], Tb[:, g, :]).then_inc(inverse[a], 1)
                    dve.wait_ge(weighed[a], per_block(b, j, G * NC, NC * (g + 1)))
                    dve.wait_ge(inverse[a], per_block(b, j, G, g + 1))
                    v.tensor_tensor(at[:, g, :], Ob[:, g, :], at[:, g, :], ALU.mult).then_inc(normed[a], 1)
                if a == 0:
                    dve.wait_ge(stored[j], b * 16 + 16)
                else:
                    dve.wait_ge(biased, per_block(b, j, 2, 1))
                for t in range(NT):
                    dve.wait_ge(projected[a], per_block(b, j, NT // 2, t // 2 + 1))
                    tt = j * NT + t
                    v.scalar_tensor_tensor(out=xs[:, tt, :], in0=tiles(Yb)[:, t, :],
                                           scalar=gate[:, (0, 2)[a]:(0, 2)[a] + 1], in1=(xin, xs)[a][:, tt, :],
                                           op0=ALU.mult, op1=ALU.add).then_inc(added[a], 1)

            def prepare(b):
                k = 0

                def step(ins):
                    ins.then_inc(prep, 1)

                dve.wait_ge(ctx_loaded, b * (16 * (2 + NC)) + 16 * (2 + NC))
                step(v.tensor_scalar(mbias[:], mask1_sb[:], 0.0, MASKED, ALU.is_equal, ALU.mult))
                step(v.tensor_copy(ctx_wide.rearrange("p k (c h) -> p k c h", h=HG),
                                   cT[:].unsqueeze(3).to_broadcast([P, KE, KEYS, HG])))
                step(v.tensor_scalar(ebias[:], mask0_sb[:], REMOVED, cap[:, 2:3], ALU.mult, ALU.add))
                heads = head_of_feature.unsqueeze(1).to_broadcast([P, KEYS, HG])
                for g in range(G):
                    step(v.tensor_tensor(kd[0][:, g, :].rearrange("p (k h) -> p k h", h=HG),
                                         cT[:, g, :].unsqueeze(2).to_broadcast([P, KEYS, HG]), heads, ALU.mult))
                dve.wait_ge(vd0_loaded, b * (16 * NC) + 16 * NC)
                vd0_v = vd[0][:].rearrange("p c (g n) -> p (c g) n", n=P)
                step(v.tensor_tensor(vd0_v, vd0_v, same_head.unsqueeze(1).to_broadcast([P, NC * G, P]), ALU.mult))
                done = 7
                dve.wait_ge(kv_done, per_batch(b, 3, 2))
                step(v.tensor_copy(mbT[:], Yb[0:KEYS, 0, :].bitcast(BF16)))
                for g in range(G):
                    step(v.tensor_scalar(k1T[:, g, :], Tb[:, g, 0:KEYS], bk_sb[:, g:g + 1], None, ALU.add))
                dve.wait_ge(prep, per_batch(b, PREP, done + G))
                for g in range(G):
                    step(v.tensor_tensor(kd[1][:, g, :].rearrange("p (k h) -> p k h", h=HG),
                                         k1T[:, g, :].unsqueeze(2).to_broadcast([P, KEYS, HG]), heads, ALU.mult))
                dve.wait_ge(prep, per_batch(b, PREP, done + 2 * G))
                step(v.tensor_copy(kd1h[:], kd[1][:]))
                dve.wait_ge(kv_done, per_batch(b, 3, 3))
                for c in range(NC):
                    r = rows_of(c)
                    o = tiles(Sb)[0:r, c, :] if c < 4 else tiles(Ob)[0:r, 0, :]
                    step(v.tensor_tensor(vd[1][0:r, c, :].rearrange("p (g n) -> p g n", n=P),
                                         o.rearrange("p (g n) -> p g n", n=P),
                                         same_head[0:r].unsqueeze(1).to_broadcast([r, G, P]), ALU.mult))
                dve.wait_ge(prep, per_batch(b, PREP, PREP - 1))
                step(v.tensor_tensor(vd[1][:], vd[1][:], bv_rows[:].unsqueeze(1).to_broadcast([P, NC, E]), ALU.add))

            def choose(b, j):
                k = [0]

                def step(ins):
                    k[0] += 1
                    ins.then_inc(route_step, 1)
                    dve.wait_ge(route_step, per_block(b, j, ROUTE, k[0]))

                def wide(a):
                    return a.unsqueeze(2).to_broadcast([P, NT, NX])

                odd, p, is1, key1, one1, p2, is2, key2, one2, both, w, _ = (route[:, i] for i in range(12))
                m1, k1, m2, k2, den, inv, ginv, _ = (rone[:, i] for i in range(8))
                lower = rank_of_expert.unsqueeze(1).to_broadcast([P, NT, NX])
                dve.wait_ge(odds, per_block(b, j, 1, 1))
                step(v.tensor_scalar(is1, odd, 1.0, None, ALU.add))
                step(v.reciprocal(p, is1))
                step(v.tensor_reduce(m1, p, AX.X, ALU.max))
                step(v.tensor_tensor(is1, p, wide(m1), ALU.is_equal))
                step(v.tensor_tensor(key1, is1, lower, ALU.mult))
                step(v.tensor_reduce(k1, key1, AX.X, ALU.max))
                step(v.tensor_tensor(one1, key1, wide(k1), ALU.is_equal))
                step(v.scalar_tensor_tensor(out=p2, in0=one1, scalar=-4.0, in1=p, op0=ALU.mult, op1=ALU.add))
                step(v.tensor_reduce(m2, p2, AX.X, ALU.max))
                step(v.tensor_tensor(is2, p2, wide(m2), ALU.is_equal))
                step(v.tensor_tensor(key2, is2, lower, ALU.mult))
                step(v.tensor_reduce(k2, key2, AX.X, ALU.max))
                step(v.tensor_tensor(one2, key2, wide(k2), ALU.is_equal))
                step(v.tensor_tensor(both, one1, one2, ALU.add))
                step(v.scalar_tensor_tensor(out=den, in0=m1, scalar=1e-20, in1=m2, op0=ALU.add, op1=ALU.add))
                step(v.reciprocal(inv, den))
                step(v.tensor_scalar(ginv, inv, gate[:, 1:2], None, ALU.mult))
                step(v.tensor_tensor(w, p, both, ALU.mult))
                step(v.tensor_tensor(comb[:], w, wide(ginv), ALU.mult))
                assert k[0] == ROUTE

            def experts(b, j):
                for n in range(NH + 1):
                    if n < NH:
                        dve.wait_ge(rectified, per_block(b, j, NH, n + 1))
                        if n >= 2:
                            dve.wait_ge(high, per_block(b, j, NH, n - 1))
                        v.tensor_tensor(hf[:, n % 2, :], Sb[:, n % 2, :], ur[:, n % 2, :], ALU.mult).then_inc(squared, 1)
                        dve.wait_ge(high, per_block(b, j, NH, n + 1))
                        if n >= 2:
                            dve.wait_ge(down, per_block(b, j, NH, n - 1))
                        v.tensor_tensor(hl[:, n % 2, :], hf[:, n % 2, :], hh[:, n % 2, :].bitcast(F32),
                                        ALU.subtract).then_inc(low, 1)
                    if n == 1:
                        choose(b, j)
                    if n >= 1 and CH[n - 1][2]:
                        e = CH[n - 1][0]
                        dve.wait_ge(down, per_block(b, j, NH, n))
                        if e:
                            dve.wait_ge(mixed, per_block(b, j, NX * NT, e * NT))
                        for t in range(NT):
                            row = xs[:, j * NT + t, :]
                            v.scalar_tensor_tensor(out=row, in0=tiles(Y2[e % 2])[:, t, :], scalar=comb[:, t, e:e + 1],
                                                   in1=row, op0=ALU.mult, op1=ALU.add).then_inc(mixed, 1)

            v.memset(mask0_sb[:], 0).then_inc(cleared, 1)
            v.memset(vd[0][:], 0.0).then_inc(cleared, 1)
            dve.wait_ge(weights_loaded, 16 * 19)
            dve.wait_ge(gates_ready, 4)
            v.tensor_copy(rth[:], rt_raw[:]).then_inc(ready, 1)
            v.tensor_copy(minus_head[:], minus_head_raw).then_inc(ready, 1)
            v.tensor_copy(rows_of_key[:], sel_raw).then_inc(ready, 1)
            v.tensor_copy(ident_b[:], ident).then_inc(ready, 1)
            bv2 = bv_rows[:].rearrange("p (g n) -> p g n", n=P)
            v.tensor_tensor(bv2, bv2, same_head.unsqueeze(1).to_broadcast([P, G, P]), ALU.mult).then_inc(ready, 1)
            v.tensor_scalar(bo_rows[:], bo_rows[:], gate[:, 2:3], None, ALU.mult).then_inc(ready, 1)
            v.tensor_scalar(b2_rows[:], b2_rows[:], gate[:, 3:4], None, ALU.mult).then_inc(ready, 1)
            dve.wait_ge(ready, 7)
            v.tensor_tensor(rtl[:], rt_raw[:], rth[:].bitcast(F32), ALU.subtract).then_inc(ready, 1)
            v.memset(vd[1][:], 0.0).then_inc(ready, 1)
            for j in range(NB):
                dve.sem_inc(stored[j], 16)
            for i in range(NPIECE):
                dve.wait_ge(raw_high, i + 1)
                v.tensor_tensor(piece((w1l, w2l), i), raw[:, i % 2, :], piece((w1h, w2h), i).bitcast(F32),
                                ALU.subtract).then_inc(raw_low, 1)
            dve.wait_ge(ready, 9)
            dve.wait_ge(raw_low, NPIECE)
            with dve.Fori(0, B) as b:
                prepare(b)
                for j in range(NB):
                    norm(b, j, 0)
                    turned_copy(b, j, 0, False)
                    attended(b, j, 0)
                    norm(b, j, 1)
                    turned_copy(b, j, 1, True)
                    experts(b, j)
                    norm(b, j, 2)
                    turned_copy(b, j, 2, False)
                    for n in range(NT * G):
                        t, g = divmod(n, G)
                        dve.wait_ge(rowscores, per_block(b, j, NT * G, n + 1))
                        bank = (Sb, Tb)[n % 2]
                        s = bank[:, :, 0:HALF * HG].rearrange("p i (k h) -> p h i k", h=HG)
                        v.tensor_reduce(mx[:, t, g * HG:(g + 1) * HG], s, AX.XY, ALU.max).then_inc(rowmax, 1)
                    dve.wait_ge(rowmax, per_block(b, j, NT * G, NT * G))
                    v.tensor_copy(mxs[:, :, 0, :].bitcast(F32R), mx[:]).then_inc(split_max, 1)
                    dve.wait_ge(split_max, per_block(b, j, 2, 1))
                    v.tensor_tensor(mxs[:, :, 1, :], mx[:], mxs[:, :, 0, :], ALU.subtract).then_inc(split_max, 1)
                    attended(b, j, 1)
                    norm(b, j, 3)
                    turned_copy(b, j, 3, False)
                    dve.wait_ge(low1, per_block(b, j, 1, 1))
                    v.tensor_copy(pT, Ob[0:RANK, 0, :]).then_inc(low1_copied, 1)
                    dve.wait_ge(low2, per_block(b, j, NF, NF))
                    v.tensor_copy(qq, Ob[0:RANK, 1, :]).then_inc(low2_copied, 1)
                    dve.wait_ge(biased, per_block(b, j, 2, 2))
                    for t in range(NT):
                        dve.wait_ge(ffn_done, per_block(b, j, NT // 2, t // 2 + 1))
                        v.scalar_tensor_tensor(out=xs[:, j * NT + t, :], in0=tiles(Yb)[:, t, :], scalar=gate[:, 3:4],
                                               in1=xs[:, j * NT + t, :], op0=ALU.mult,
                                               op1=ALU.add).then_inc(res_done, 1)


def kernel(**inputs):
    import numpy as _np
    import concourse.bacc as _bacc
    from concourse import mybir as _mybir
    from concourse.bass_utils import run_bass_kernel_spmd as _run

    a = {k: _np.asarray(v) for k, v in inputs.items()}
    hd = 2 * DH
    w_kv = a["L1_xattn_W_kv"].reshape(E, H, hd)
    b_kv = a["L1_xattn_b_kv"].reshape(H, hd)
    r = _np.arange(P)
    consts = _np.zeros((P, C_ROWS + KEYS * HG), _np.float32)
    consts[:, 0:P] = _np.eye(P)
    consts[:, P:2 * P] = (r[:, None] % HG) == (r[None, :] // DH)
    consts[:, 2 * P:2 * P + HG] = (r[:, None] // DH) == _np.arange(HG)[None, :]
    consts[:, 2 * P + HG:2 * P + 2 * HG] = NX - _np.arange(NX)
    for g in range(G):
        q = _np.arange(32)
        consts[0:32, C_MINUS + g * P:C_MINUS + (g + 1) * P] = \
            -((q[:, None] % H) == (g * HG + r[None, :] % HG)).astype(_np.float32)
    consts[0:KEYS, C_ROWS:] = _np.arange(KEYS)[:, None] == _np.arange(KEYS * HG)[None, :] // HG
    named = {
        "x": a["x"],
        "ctx_rows": a["ctx_1024"],
        "ctx_t": a["ctx_1024"].transpose(0, 2, 1),
        "mask0": a["mask_Bx1xS2_bk0"].reshape(B, KEYS),
        "mask1": a["mask_BxSxS2_ik0"],
        "gates": _np.stack([a["g_xattn"][0], a["g_ffn"][0], a["g_xattn"][1], a["g_ffn"][1]]),
        "logc": a["L0_xattn_log_C"].reshape(1),
        "scale0": a["L0_xattn_scale"].reshape(1),
        "w_out_t": a["L0_xattn_W_out"].T,
        "router_t": a["L0_ffn_router_w"].T,
        "w1": a["L0_ffn_w1"],
        "w2": a["L0_ffn_w2"],
        "wk": w_kv[:, :, :DH].reshape(E, E),
        "wv": w_kv[:, :, DH:].reshape(E, E),
        "bk": b_kv[:, :DH].reshape(G, P).T,
        "bv": b_kv[:, DH:].reshape(E),
        "wq": a["L1_xattn_W_q"],
        "bq": a["L1_xattn_b_q"].reshape(G, P).T,
        "wo": a["L1_xattn_W_o"],
        "bo": a["L1_xattn_b_o"],
        "u1": a["L1_ffn_U1"],
        "v1": a["L1_ffn_V1"],
        "b1": a["L1_ffn_b1"].reshape(NF, P).T,
        "u2": a["L1_ffn_U2"],
        "v2": a["L1_ffn_V2"],
        "b2": a["L1_ffn_b2"],
        "consts": consts,
    }
    nc = _bacc.Bacc("TRN2", target_bir_lowering=False, num_devices=1)
    arrays, args = {}, []
    for name, v in named.items():
        v = _np.ascontiguousarray(v)
        arrays[f"in_{name}"] = v
        args.append(nc.dram_tensor(f"in_{name}", v.shape, _mybir.dt.from_np(v.dtype), kind="ExternalInput").ap())
    args.append(nc.dram_tensor("out_0", (B, S, E), F32, kind="ExternalOutput").ap())
    flamingo(nc, *args)
    result = _run(nc, [arrays], core_ids=[0])
    return result.results[0]["out_0"]
```

```python
from contextlib import ExitStack

import concourse.bass as bass
from concourse import mybir

F32 = mybir.dt.float32
F32R = mybir.dt.float32r
BF16 = mybir.dt.bfloat16
I32 = mybir.dt.int32
U8 = mybir.dt.uint8
ALU = mybir.AluOpType
ACT = mybir.ActivationFunctionType
AX = mybir.AxisListType

P = 128
B, S, E = 2, 1024, 256
H, DH = 16, 16
KEYS = 77
G = 2
HG = H // G
PAIRS = HG // 2
KM = P // 2
KL = KEYS - KM
RL = KL * HG
NC = PAIRS + 1
ROWS = KEYS * HG
T = 512
NT = T // P
NB = S // T
BL = B * NB
KE = E // P
WIDTHS = [256] * 4 + [512] * 4
NX = len(WIDTHS)
TOTAL = sum(WIDTHS)
UW = 256
UNITS = TOTAL // UW
UC = UW // P
STEPS = BL * UC
RANK = 64
NF = 1024 // P
MASKED = -1e20
REMOVED = -1e30
EPS = 1e-5
CG = G * NC
SC, DEN, TURN, OUT, PRJ = (0, 1), (2, 3), 4, (5, 6), (7, 3)
HID, YB = (0, 1, 2, 3), ((5, 6), (4, 7))
C_EYE, C_SAME2, C_SAME8, C_HEAD, C_RANK, C_MINUS, C_KEY, C_END = (
    0, P, P + 32, 2 * P + 32, 2 * P + 32 + HG, 2 * P + 32 + 2 * HG, 2 * P + 32 + 2 * HG + G * ROWS,
    2 * P + 32 + 2 * HG + (G + 1) * ROWS)


def rows_of(c):
    return P if c < PAIRS else RL


def flamingo(nc, x, ctx_rows, ctx_t, mask0, mask1, gates, logc, scale0, w_out_t, router_t, w1, w2, wk, wv, bk, bv,
             wq, bq, wo, bo, u1, v1, b1, u2, v2, b2, consts, out):
    stack = ExitStack()
    with stack:
        def sb(name, shape, dt=F32):
            return stack.enter_context(nc.sbuf_tensor(name, shape, dt))

        def sem(name):
            return stack.enter_context(nc.semaphore(name))

        cst = sb("cst", [P, C_MINUS])
        ident, same2, same8 = cst[:, 0:P], cst[:, C_SAME2:C_SAME8], cst[:, C_SAME8:C_HEAD]
        head_of_feature, rank_of_expert = cst[:, C_HEAD:C_RANK], cst[:, C_RANK:C_MINUS]
        minus_head = sb("minus_head", [32, G, ROWS], F32R)
        rows_of_key = sb("rows_of_key", [KEYS, ROWS], BF16)
        ident_b = sb("ident_b", [P, P], BF16)
        minus_half, eps_sb = sb("minus_half", [P, NT]), sb("eps_sb", [P, NT])
        unit_raw = sb("unit_raw", [P, 2, KE + UC, UW])
        unit_h, unit_l = sb("unit_h", [P, 2, KE + UC, UW], F32R), sb("unit_l", [P, 2, KE + UC, UW], F32R)
        rt_raw, rth, rtl = sb("rt_raw", [P, KE, NX]), sb("rth", [P, KE, NX], F32R), sb("rtl", [P, KE, NX], F32R)
        w_out_sb, wo_sb = sb("w_out_sb", [P, KE, E]), sb("wo_sb", [P, KE, E])
        wqh, wql = sb("wqh", [P, KE, E], F32R), sb("wql", [P, KE, E], F32R)
        u1_sb, u2_sb, v2_sb = sb("u1_sb", [P, KE, RANK]), sb("u2_sb", [P, NF, RANK]), sb("v2_sb", [P, E])
        v1h, v1l = sb("v1h", [P, NF * P], F32R), sb("v1l", [P, NF * P], F32R)
        bk_sb, bq_sb, b1_sb = sb("bk_sb", [P, G]), sb("bq_sb", [P, G]), sb("b1_sb", [P, NF])
        bv_rows, bo_rows, b2_rows = sb("bv_rows", [P, E]), sb("bo_rows", [P, E]), sb("b2_rows", [P, E])
        gate_raw, gate = sb("gate_raw", [P, 4]), sb("gate", [P, 4])
        cap, scale_raw, scale_q = sb("cap", [P, 3]), sb("scale_raw", [P, 1]), sb("scale_q", [P, 1])
        cT = sb("cT", [P, B, KE, KEYS])
        kh, kl = sb("kh", [P, 2 * B, G, KEYS], F32R), sb("kl", [P, 2 * B, G, KEYS], F32R)
        k1 = sb("k1", [P, B, G, KEYS])
        ctx_wide = sb("ctx_wide", [P, KE, P + RL])
        mask0_sb = sb("mask0_sb", [P, B, 2], U8)
        ebias = sb("ebias", [P, B, 2])
        mbias = sb("mbias", [P, BL * NT, KEYS], BF16)
        mbT = sb("mbT", [KEYS, B * S], BF16)
        kdh, kdl = sb("kdh", [P, B, G, ROWS], F32R), sb("kdl", [P, B, G, ROWS], F32R)
        vd = sb("vd", [P, 2 * B, 2, E])
        xs = sb("xs", [P, BL * NT, E])
        xn = sb("xn", [P, 2, NT, E])
        xTh, xTl = sb("xTh", [P, BL, KE, T], F32R), sb("xTl", [P, BL, KE, T], F32R)
        bstat, mv = sb("bstat", [P, NT, 6]), sb("mv", [P, NT, 2])
        veps, rstd = sb("veps", [P, NT]), sb("rstd", [P, NT])
        work = sb("work", [P, CG, T])
        pr, gl = work[:], work[:, 0:4, :]
        ur, hf = work[:, 0:4, :], work[:, 4:8, :]
        wide = unit_raw[:].rearrange("p s k n -> p (s k n)")
        mask1_sb = wide[:, 0:BL * NT * KEYS].bitcast(I32).rearrange("p (t n) -> p t n", n=KEYS)
        wq_raw = wide[:, 3 * T:4 * T].rearrange("p (k n) -> p k n", k=KE)
        wide = xs[:, 2 * NT:, :].rearrange("p t n -> p (t n)")
        minus_raw, key_raw = wide[0:32, 0:G * ROWS], wide[0:KEYS, G * ROWS:(G + 1) * ROWS]
        v1_raw = work[:, 8:10, :].rearrange("p a n -> p (a n)")
        th = sb("th", [P, 2, T])
        qq = lg = th
        at = sb("at", [P, G, T])
        wk_sb, wv_sb = (xn[:, 1, g * KE:(g + 1) * KE, :] for g in range(G))
        split = sb("split", [P, 2, 2, G, T], F32R)
        qh, ql = split[:, 0], split[:, 1]
        hh, hl = (split[:, n].rearrange("p a g n -> p (a g) n") for n in range(2))
        ph, pl = split[:, 0, :, 0], split[:, 1, :, 0]
        mx, mxl, mxs = sb("mx", [P, NT, H]), sb("mxl", [P, NT, H]), sb("mxs", [P, NT, 2, H])
        mxT = sb("mxT", [32, 2, T], F32R)
        AT = BL * NT
        route_sb = sb("route_sb", [P, 6, AT, NX])
        rone = sb("rone", [P, 8, AT])
        comb, comb_now = sb("comb", [P, UNITS, AT]), sb("comb_now", [P, 2, AT])

        bank = stack.enter_context(nc.psum_tensor("bank", [P, 8, 512], F32))

        def tile_of(banks, t):
            return bank[:, banks[t // 2], (t % 2) * E:(t % 2 + 1) * E]

        gates_loaded, gates_ready = sem("gates_loaded"), sem("gates_ready")
        consts_loaded, context_loaded, weights_loaded = sem("consts_loaded"), sem("context_loaded"), sem("weights_loaded")
        vd_loaded, mask1_loaded = sem("vd_loaded"), sem("mask1_loaded")
        x_loaded = [sem(f"x_loaded{i}") for i in range(BL)]
        cleared, ready, pool_ready = sem("cleared"), sem("ready"), sem("pool_ready")
        keys_split, keys_act = sem("keys_split"), sem("keys_act")
        kd_ready, vd_ready = [sem(f"kd_ready{l}") for l in range(2 * B)], sem("vd_ready")
        carried, carried_pool, chain = sem("carried"), sem("carried_pool"), sem("chain")
        kv_done, kv_copied = sem("kv_done"), sem("kv_copied")
        unit_loaded = [sem("unit_loaded0"), sem("unit_loaded1")]
        unit_high, unit_low = sem("unit_high"), sem("unit_low")
        stat, aggr, vare, rstd_done, xn_done = sem("stat"), sem("aggr"), sem("vare"), sem("rstd_done"), sem("xn_done")
        turned, turned_high, turned_low = sem("turned"), sem("turned_high"), sem("turned_low")
        scored = [sem("scored0"), sem("scored1")]
        capped = sem("capped")
        prob = [sem("prob0"), sem("prob1")]
        weighed = [sem("weighed0"), sem("weighed1")]
        inverse = [sem("inverse0"), sem("inverse1")]
        normed = [sem("normed0"), sem("normed1")]
        projected = [sem("projected0"), sem("projected1")]
        added = [sem("added0"), sem("added1")]
        routed, logits, logits_turned = sem("routed"), sem("logits"), sem("logits_turned")
        odds, comb_ready = sem("odds"), sem("comb_ready")
        hidden, rectified, squared = sem("hidden"), sem("rectified"), sem("squared")
        high, low, down, mixed = sem("high"), sem("low"), sem("down"), sem("mixed")
        q_done, q_high, q_low = sem("q_done"), sem("q_high"), sem("q_low")
        rowscores, rowmax, rowrest, restmax = sem("rowscores"), sem("rowmax"), sem("rowrest"), sem("restmax")
        split_max, max_turned, max_ready = sem("split_max"), sem("max_turned"), sem("max_ready")
        biased = sem("biased")
        low1, low1_high, low1_low = sem("low1"), sem("low1_high"), sem("low1_low")
        inner, gelu_done, low2, low2_copied = sem("inner"), sem("gelu_done"), sem("low2"), sem("low2_copied")
        ffn_done, res_done = sem("ffn_done"), sem("res_done")
        stored = sem("stored")

        order, turns = {}, []
        turns += [(0, 0)]
        for i in range(BL):
            if i + 1 < BL:
                turns.append((0, i + 1))
            if i >= 2:
                turns.append((1, i - 2))
        turns += [(1, BL - 2), (1, BL - 1), (2, 0), (2, 1)]
        for i in range(BL):
            if i >= 2:
                turns.append((3, i - 2))
            if i + 2 < BL:
                turns.append((2, i + 2))
        turns += [(3, BL - 2), (3, BL - 1)]
        for n, key in enumerate(turns):
            order[key] = n
        norms = [(0, 0), (0, 1)]
        for i in range(BL):
            if i + 2 < BL:
                norms.append((0, i + 2))
            if i >= 1:
                norms.append((1, i - 1))
        norms += [(1, BL - 1), (2, 0), (2, 1), (2, 2)]
        for i in range(BL):
            if i >= 1:
                norms.append((3, i - 1))
            if i + 3 < BL:
                norms.append((2, i + 3))
        norms += [(3, BL - 1)]
        norm_at = {key: n for n, key in enumerate(norms)}
        slot = {key: (0 if key[0] % 2 == 0 else 1) for key in norms}

        late = [key for key in norms if key[0] >= 2]
        bias_at = {key: n + 1 for n, key in enumerate(late)}

        def spread_keys(engine, b, l):
            for g in range(G):
                for dst, src in ((kdh, kh), (kdl, kl)):
                    heads = head_of_feature.rearrange("p (c h) -> p c h", h=2).unsqueeze(2) \
                        .to_broadcast([P, PAIRS, KM, 2])
                    k = src[:, l, g, 0:KM].bitcast(F32).unsqueeze(1).unsqueeze(3).to_broadcast([P, PAIRS, KM, 2])
                    engine.tensor_tensor(dst[:, b, g, 0:PAIRS * P].rearrange("p (c k h) -> p c k h", c=PAIRS, h=2),
                                         k, heads, ALU.mult)
                    k = src[:, l, g, KM:KEYS].bitcast(F32).unsqueeze(2).to_broadcast([P, KL, HG])
                    ins = engine.tensor_tensor(dst[:, b, g, PAIRS * P:ROWS].rearrange("p (k h) -> p k h", h=HG),
                                               k, head_of_feature.unsqueeze(1).to_broadcast([P, KL, HG]), ALU.mult)
            ins.then_inc(kd_ready[l], 1)

        block = stack.enter_context(nc.Block())

        @block.sync
        def _(sp):
            xv = x.rearrange("b (t p) e -> p (b t) e", p=P)
            ov = out.rearrange("b (t p) e -> p (b t) e", p=P)

            def load_x(i):
                sp.dma_start(xs[:, i * NT:(i + 1) * NT, :], xv[:, i * NT:(i + 1) * NT, :]).then_inc(x_loaded[i], 16)

            load_x(0)
            sp.dma_start(cst[:], consts[:, 0:C_MINUS]).then_inc(consts_loaded, 16)
            for b in range(B):
                sp.dma_start(cT[:, b], ctx_t[b].rearrange("(k p) n -> p k n", p=P)).then_inc(context_loaded, 16)
            sp.dma_start(gate_raw[:], gates.partition_broadcast(P)).then_inc(gates_loaded, 16)
            sp.dma_start(cap[:, 0:1], logc.partition_broadcast(P)).then_inc(gates_loaded, 16)
            sp.dma_start(scale_raw[:], scale0.partition_broadcast(P)).then_inc(gates_loaded, 16)
            sp.wait_ge(cleared, 2)
            for b in range(B):
                for part, (k0, n, heads) in enumerate(((0, KM, 2), (KM, KL, HG))):
                    src = mask0[b, k0:k0 + n].unsqueeze(1).unsqueeze(1).to_broadcast([n, heads, 1])
                    sp.dma_start(mask0_sb[0:n * heads, b, part:part + 1], src).then_inc(context_loaded, 16)
                    src = ctx_rows[b, k0:k0 + n, :].unsqueeze(1).to_broadcast([n, heads, E])
                    sp.dma_start(vd[0:n * heads, b, part, :], src).then_inc(vd_loaded, 16)
            load_x(1)
            for dst, src in ((wk_sb, wk), (wv_sb, wv)):
                sp.dma_start(dst, src.rearrange("(k p) n -> p k n", p=P)).then_inc(weights_loaded, 16)
            sp.dma_start(bk_sb[:], bk).then_inc(weights_loaded, 16)
            sp.dma_start(bv_rows[:], bv.partition_broadcast(P)).then_inc(weights_loaded, 16)
            sp.dma_start(w_out_sb[:], w_out_t.rearrange("(k p) n -> p k n", p=P)).then_inc(weights_loaded, 16)
            sp.dma_start(mask1_sb, mask1.rearrange("b (t p) n -> p (b t) n", p=P)).then_inc(mask1_loaded, 16)
            sp.dma_start(minus_raw, consts[0:32, C_MINUS:C_KEY]).then_inc(mask1_loaded, 16)
            sp.dma_start(rt_raw[:], router_t.rearrange("(k p) n -> p k n", p=P)).then_inc(mask1_loaded, 16)
            sp.dma_start(wq_raw, wq.rearrange("(k p) n -> p k n", p=P)).then_inc(mask1_loaded, 16)
            for half in range(2):
                rs = slice(half * RANK, (half + 1) * RANK)
                sp.dma_start(v1_raw[rs], v1).then_inc(mask1_loaded, 16)
                sp.dma_start(v2_sb[rs, :], v2).then_inc(mask1_loaded, 16)
            for dst, src in ((bq_sb, bq), (b1_sb, b1)):
                sp.dma_start(dst[:], src).then_inc(mask1_loaded, 16)
            for dst, src in ((bo_rows, bo), (b2_rows, b2)):
                sp.dma_start(dst[:], src.partition_broadcast(P)).then_inc(mask1_loaded, 16)
            sp.dma_start(key_raw, consts[0:KEYS, C_KEY:C_END]).then_inc(mask1_loaded, 16)
            for dst, src in ((wo_sb, wo), (u1_sb, u1), (u2_sb, u2)):
                sp.dma_start(dst[:], src.rearrange("(k p) n -> p k n", p=P)).then_inc(mask1_loaded, 16)
            sp.wait_ge(ready, 3)
            load_x(2)
            load_x(3)
            sp.wait_ge(ready, 8)

            w1v, w2v = w1.rearrange("(k p) n -> p k n", p=P), w2.rearrange("(j p) d -> p j d", p=P)

            def load_unit(u, s):
                sp.dma_start(unit_raw[:, s, 0:KE, :], w1v[:, :, bass.ts(u, UW)]).then_inc(unit_loaded[s], 16)
                sp.dma_start(unit_raw[:, s, KE:KE + UC, :], w2v[:, bass.ts(u, UC), :]).then_inc(unit_loaded[s], 16)

            for s in range(2):
                load_unit(s, s)
            with sp.Fori(1, UNITS // 2) as v:
                for s in range(2):
                    src = sp.snap(v * 2 + s)
                    sp.wait_ge(unit_low, v * 2 + (s - 1))
                    sp.sem_inc(carried, 1)
                    load_unit(src, s)
            for i in range(BL):
                sp.wait_ge(res_done, NT * (i + 1))
                sp.dma_start(ov[:, i * NT:(i + 1) * NT, :], xs[:, i * NT:(i + 1) * NT, :]).then_inc(stored, 16)
            sp.wait_ge(stored, 16 * BL)

        @block.tensor
        def _(pe):
            def split3(o, ah, al, bh, bl, first, last):
                pe.matmul(o, ah, bl, start=first, stop=False, skip_group_check=True)
                pe.matmul(o, al, bh, start=False, stop=False, skip_group_check=True)
                return pe.matmul(o, ah, bh, start=False, stop=last, skip_group_check=True)

            def turn(s, i, k):
                if (s, i) not in order:
                    return
                pe.wait_ge(xn_done, NT * (norm_at[s, i] + 1))
                n = KE * order[s, i] + k
                if n:
                    pe.wait_ge(turned_low, n)
                if k == 0 and s == 2 and i:
                    pe.wait_ge(*((restmax, 1) if i == 1 else (max_ready, i)))
                if k == 0 and s == 3:
                    pe.wait_ge(*((restmax, G * (i + 3) + 1) if i + 3 < BL else (max_ready, BL)))
                for t in range(NT):
                    ins = pe.transpose(bank[:, TURN, t * P:(t + 1) * P],
                                       xn[:, slot[s, i], t, k * P:(k + 1) * P], ident)
                ins.then_inc(turned, 1)

            def xT_ready(s, i):
                pe.wait_ge(turned_high, KE * (order[s, i] + 1))
                pe.wait_ge(turned_low, KE * (order[s, i] + 1))

            def scores(a, i, g, c):
                b, r = i // NB, rows_of(c)
                n = CG * i + NC * g + c
                s = bank[0:r, SC[n % 2], :]
                if n >= 2:
                    pe.wait_ge(capped if a == 0 else prob[1], n - 1)
                if a == 1 and i and n % CG == 0:
                    pe.wait_ge(max_ready, i + 1)
                if a == 1 and g == 1 and c < 2 and i + 1 < BL:
                    pe.wait_ge(rowmax, G * NT * (i + 2))
                ks = slice(P * c, P * c + r)
                if a == 0:
                    ins = split3(s, kdh[:, b, g, ks], kdl[:, b, g, ks], xTh[:, i, g, :], xTl[:, i, g, :], True, True)
                else:
                    pe.matmul(s, rows_of_key[:, ks], mbT[:, i * T:(i + 1) * T], start=True, stop=False,
                              skip_group_check=True)
                    split3(s, kdh[:, b, g, ks], kdl[:, b, g, ks], qh[:, i % 2, g, :], ql[:, i % 2, g, :], False, False)
                    ins = pe.matmul(s, minus_head[:, g, ks], mxT[:, i % 2, :], start=False, stop=True,
                                    skip_group_check=True)
                ins.then_inc(scored[a], 1)

            def weigh(a, i, g):
                if i < 0:
                    return
                b = i // NB
                if i:
                    pe.wait_ge(normed[a], G * (i - 1) + g + 1)
                if i and g:
                    pe.wait_ge(added[a], NT * i)
                if (i, g) == (0, 0):
                    pe.wait_ge(vd_ready, 4 * (a + 1))
                for v in (True, False):
                    o = bank[:, (OUT if v else DEN)[g], :]
                    if v:
                        pe.wait_ge(prob[a], CG * i + NC * g + PAIRS)
                    for c in range(PAIRS):
                        ps = slice(32 * c, 32 * c + 32)
                        w = vd[:, B * a + b, 0, g * P + 32 * c:g * P + 32 * c + 32] if v else same2
                        pe.matmul(o[ps], w, pr[:, NC * g + c, :], start=True, stop=False, skip_group_check=True)
                pe.wait_ge(prob[a], CG * i + NC * (g + 1))
                for v in (True, False):
                    w = vd[0:RL, B * a + b, 1, g * P:(g + 1) * P] if v else same8[0:RL]
                    ins = pe.matmul(bank[:, (OUT if v else DEN)[g], :], w, pr[0:RL, NC * g + PAIRS, :],
                                    start=False, stop=True, skip_group_check=True)
                ins.then_inc(weighed[a], 1)

            def project(a, i):
                if i < 0:
                    return
                w = w_out_sb if a == 0 else wo_sb
                pe.wait_ge(normed[a], G * (i + 1))
                if i:
                    pe.wait_ge(added[a], NT * i)
                if a == 1:
                    pe.wait_ge(restmax, G * min(i + 3, BL))
                for t in range(NT):
                    for g in range(G):
                        ins = pe.matmul(tile_of(PRJ, t), at[:, g, t * P:(t + 1) * P], w[:, g, :],
                                        start=(g == 0), stop=(g == G - 1))
                    if t % 2:
                        ins.then_inc(projected[a], 1)

            def prepare_keys():
                pe.wait_ge(weights_loaded, 16 * 5)
                for b in range(B):
                    for g in range(G):
                        for k in range(KE):
                            ins = pe.matmul(bank[:, DEN[b], g * 128:g * 128 + KEYS], wk_sb[:, k, g * P:(g + 1) * P],
                                            cT[:, b, k, :], start=(k == 0), stop=(k == KE - 1))
                    ins.then_inc(kv_done, 1)

            def prepare_values(b):
                pe.wait_ge(keys_split, b + 1)
                for part, r in enumerate((P, RL)):
                    for k in range(KE):
                        ins = pe.matmul(bank[0:r, OUT[b], part * E:(part + 1) * E],
                                        ctx_wide[:, k, part * P:part * P + r], wv_sb[:, k, :],
                                        start=(k == 0), stop=(k == KE - 1))
                ins.then_inc(kv_done, 1)

            def prepare_mask(b):
                pe.wait_ge(ready, 4)
                pe.wait_ge(kv_copied, 2)
                for t in range(NB * NT):
                    ins = pe.transpose(bank[:, PRJ[b], :].bitcast(BF16)[0:KEYS, t * P:(t + 1) * P],
                                       mbias[:, b * NB * NT + t, :], ident_b[:])
                ins.then_inc(kv_done, 1)

            def attend0():
                for i in range(BL):
                    if i % NB == 0:
                        pe.wait_ge(kd_ready[i // NB], 1)
                    xT_ready(0, i)
                    scores(0, i, 0, 0)
                    scores(0, i, 0, 1)
                    turn(0, i + 1, 0)
                    scores(0, i, 0, 2)
                    weigh(0, i - 1, 1)
                    if i == 0:
                        prepare_keys()
                    scores(0, i, 0, 3)
                    turn(0, i + 1, 1)
                    scores(0, i, 0, 4)
                    if i == 0:
                        prepare_values(0)
                    scores(0, i, 1, 0)
                    if i == 0:
                        prepare_values(1)
                    scores(0, i, 1, 1)
                    turn(1, i - 2, 0)
                    scores(0, i, 1, 2)
                    turn(1, i - 2, 1)
                    if i == 0:
                        pe.wait_ge(kv_copied, 4)
                    weigh(0, i, 0)
                    if i == 0:
                        for b in range(B):
                            prepare_mask(b)
                    scores(0, i, 1, 3)
                    project(0, i - 1)
                    scores(0, i, 1, 4)
                    if i == 0:
                        pe.wait_ge(kv_copied, 6)

            def attend1():
                for i in range(BL):
                    last = i + 1 == BL
                    scores(1, i, 0, 0)
                    scores(1, i, 0, 1)
                    if not last:
                        queries(i + 1, 0)
                    scores(1, i, 0, 2)
                    weigh(1, i - 1, 1)
                    if not last:
                        queries(i + 1, 1)
                    scores(1, i, 0, 3)
                    scores(1, i, 0, 4)
                    if not last:
                        row_scores(i + 1)
                    scores(1, i, 1, 0)
                    turn(3, i - 2, 0)
                    scores(1, i, 1, 1)
                    scores(1, i, 1, 2)
                    turn(3, i - 2, 1)
                    weigh(1, i, 0)
                    if not last:
                        turn_max(i + 1)
                    project(1, i - 1)
                    scores(1, i, 1, 3)
                    turn(2, i + 2, 0)
                    scores(1, i, 1, 4)
                    turn(2, i + 2, 1)

            def queries(i, g):
                xT_ready(2, i)
                if g or i:
                    pe.wait_ge(q_low, G * i + g)
                for k in range(KE):
                    gs = slice(g * P, (g + 1) * P)
                    ins = split3(bank[:, TURN, :], wqh[:, k, gs], wql[:, k, gs], xTh[:, i, k, :], xTl[:, i, k, :],
                                 k == 0, k == KE - 1)
                ins.then_inc(q_done, 1)

            def row_scores(i):
                b = i // NB
                pe.wait_ge(q_high, G * (i + 1))
                pe.wait_ge(q_low, G * (i + 1))
                for g in range(G):
                    for t in range(NT):
                        m = g * NT + t
                        if m >= 2:
                            pe.wait_ge(rowmax, G * NT * i + m - 1)
                        elif i:
                            pe.wait_ge(prob[1], CG * (i - 1) + NC)
                        o = bank[:, SC[m % 2], :]
                        mb = mbias[:, i * NT + t, 0:KM].unsqueeze(1).unsqueeze(3).to_broadcast([P, PAIRS, KM, 2])
                        pe.matmul(o.rearrange("p (c k h) -> p c k h", c=PAIRS, h=2), ident_b[:], mb,
                                  start=True, stop=False)
                        pe.matmul(o, qh[:, i % 2, g, t * P:(t + 1) * P], kdh[:, b, g, 0:PAIRS * P],
                                  start=False, stop=True).then_inc(rowscores, 1)
                    if g == 1 and i >= 2:
                        pe.wait_ge(added[1], NT * (i - 2))
                    for t in range(NT):
                        o = bank[:, (TURN, PRJ[0])[g], t * RL:(t + 1) * RL]
                        mb = mbias[:, i * NT + t, KM:KEYS].unsqueeze(2).to_broadcast([P, KL, HG])
                        pe.matmul(o.rearrange("p (k h) -> p k h", h=HG), ident_b[:], mb, start=True, stop=False)
                        ins = pe.matmul(o, qh[:, i % 2, g, t * P:(t + 1) * P], kdh[:, b, g, PAIRS * P:ROWS],
                                        start=False, stop=True)
                    ins.then_inc(rowrest, 1)

            def turn_max(i):
                pe.wait_ge(split_max, 2 * (i + 1))
                if i == 0 or i >= 3:
                    xT_ready(*((2, 1) if i == 0 else (3, i - 3)))
                for t in range(NT):
                    ins = pe.transpose(bank[0:32, TURN, t * P:(t + 1) * P],
                                       mxs[:, t, :, :].rearrange("p a h -> p (a h)"), ident)
                ins.then_inc(max_turned, 1)

            def finish(a):
                turn(2 * a + 1, BL - 2, 0)
                turn(2 * a + 1, BL - 2, 1)
                weigh(a, BL - 1, 1)

            def first_product(s, q, n):
                i, c = divmod(q, UC)
                for k in range(KE):
                    ws = slice(c * P, (c + 1) * P)
                    ins = split3(bank[:, HID[n % 4], :], unit_h[:, s, k, ws], unit_l[:, s, k, ws],
                                 xTh[:, i, k, :], xTl[:, i, k, :], k == 0, k == KE - 1)
                ins.then_inc(hidden, 1)

            def route(i):
                xT_ready(1, max(i, BL - 2))
                if i:
                    pe.wait_ge(odds, i)
                for k in range(KE):
                    ins = split3(bank[0:NX, TURN, :], rth[:, k, :], rtl[:, k, :], xTh[:, i, k, :], xTl[:, i, k, :],
                                 k == 0, k == KE - 1)
                ins.then_inc(routed, 1)
                pe.wait_ge(logits, i + 1)
                for t in range(NT):
                    ins = pe.transpose(bank[:, TURN, t * NX:(t + 1) * NX], lg[0:NX, i % 2, t * P:(t + 1) * P],
                                       ident[0:NX, 0:NX])
                ins.then_inc(logits_turned, 1)

            def expert_units(v, last):
                for step in range(2 * STEPS):
                    ahead = step + 3
                    if ahead < 2 * STEPS or not last:
                        unit, q = divmod(ahead, STEPS)
                        if q == 0:
                            pe.wait_ge(unit_low, v * 2 + (unit + 1))
                        pe.wait_ge(squared, v * (2 * STEPS) + (step + 1))
                        first_product(unit % 2, q, ahead)
                    s, q = divmod(step, STEPS)
                    pair, c = divmod(step, UC)
                    pe.wait_ge(low, v * (2 * STEPS) + (step + 1))
                    if c == 0:
                        pe.wait_ge(mixed, v * (2 * BL * NT) + (pair + 1) * NT)
                    for t in range(NT):
                        ts = slice(t * P, (t + 1) * P)
                        ins = split3(tile_of(YB[pair % 2], t), hh[:, step % 4, ts], hl[:, step % 4, ts],
                                     unit_h[:, s, KE + c, :], unit_l[:, s, KE + c, :],
                                     c == 0 and t % 2 == 0, c == UC - 1)
                    ins.then_inc(down, 1)

            def low_rank_in(i):
                if i >= BL:
                    return
                xT_ready(3, i)
                if i:
                    pe.wait_ge(low1_low, i)
                for k in range(KE):
                    xf = (xTh[:, i, k, :], xTl[:, i, k, :])
                    for m, part in enumerate(xf):
                        ins = pe.matmul(bank[k * RANK:(k + 1) * RANK, DEN[0], :], u1_sb[:, k, :], part.bitcast(F32),
                                        start=(m == 0), stop=(m == 1), skip_group_check=True)
                ins.then_inc(low1, 1)

            def low_rank_out(i):
                if i < 0:
                    return
                pe.wait_ge(low2_copied, i + 1)
                if i:
                    pe.wait_ge(res_done, NT * i)
                else:
                    pe.wait_ge(added[1], NT * BL)
                for t in range(NT):
                    ins = pe.matmul(tile_of(PRJ, t), qq[:, i % 2, t * P:(t + 1) * P], v2_sb[:], start=True, stop=True)
                    if t % 2:
                        ins.then_inc(ffn_done, 1)

            def low_rank(i):
                for n in range(NF + 2):
                    m = NF * i + n
                    if n < NF:
                        if m >= 2:
                            pe.wait_ge(gelu_done, m - 1)
                        if n == 0:
                            pe.wait_ge(low1_high, i + 1)
                            pe.wait_ge(low1_low, i + 1)
                        ns = slice(n * P, (n + 1) * P)
                        split3(bank[:, SC[n % 2], :], v1h[:, ns], v1l[:, ns], ph[:, i % 2, :], pl[:, i % 2, :],
                               True, True).then_inc(inner, 1)
                    if n >= 3 and n % 2:
                        pe.wait_ge(gelu_done, NF * i + n - 1)
                        for j in (n - 3, n - 2):
                            rs = slice(RANK * (j % 2), RANK * (j % 2) + RANK)
                            ins = pe.matmul(bank[rs, OUT[i % 2], :], u2_sb[:, j, :], gl[:, j % 4, :],
                                            start=(j < 2), stop=(j >= NF - 2), skip_group_check=True)
                        ins.then_inc(low2, 1)
                    if n == 3:
                        low_rank_out(i - 1)
                    if n == 5:
                        low_rank_in(i + 1)

            pe.wait_ge(consts_loaded, 16)
            turn(0, 0, 0)
            turn(0, 0, 1)
            attend0()
            turn(1, BL - 2, 0)
            turn(1, BL - 2, 1)
            weigh(0, BL - 1, 1)
            pe.wait_ge(ready, 9)
            pe.wait_ge(prob[0], CG * BL)
            route(0)
            route(1)
            project(0, BL - 1)
            route(2)
            pe.wait_ge(unit_low, 1)
            for q in range(3):
                first_product(0, q, q)
            pe.wait_ge(odds, BL - 1)
            turn(1, BL - 1, 0)
            turn(1, BL - 1, 1)
            route(BL - 1)
            pe.wait_ge(odds, BL)
            pe.wait_ge(added[0], NT * BL)
            with pe.Fori(0, UNITS // 2 - 1) as v:
                expert_units(v, False)
            expert_units(UNITS // 2 - 1, True)
            turn(2, 0, 0)
            turn(2, 0, 1)
            for g in range(G):
                queries(0, g)
            pe.wait_ge(kd_ready[B], 1)
            pe.wait_ge(kd_ready[B + 1], 1)
            row_scores(0)
            turn(2, 1, 0)
            turn(2, 1, 1)
            turn_max(0)
            pe.wait_ge(max_ready, 1)
            attend1()
            finish(1)
            low_rank_in(0)
            project(1, BL - 1)
            for i in range(BL):
                low_rank(i)
                if i == 0:
                    turn(3, BL - 1, 0)
                    turn(3, BL - 1, 1)
            low_rank_out(BL - 1)

        @block.scalar
        def _(act):
            def turned_high_copy(s, i, k):
                if (s, i) not in order:
                    return
                n = KE * order[s, i] + k
                act.wait_ge(turned, n + 1)
                nc.scalar.activation(xTh[:, i, k, :], bank[:, TURN, :], ACT.Copy).then_inc(turned_high, 1)

            def cap_scores(i, n):
                g, c = divmod(n, NC)
                r = rows_of(c)
                act.wait_ge(scored[0], CG * i + n + 1)
                if CG * i + n >= 2:
                    act.wait_ge(prob[0], CG * i + n - 1)
                nc.scalar.activation(th[0:r, n % 2, :], bank[0:r, SC[n % 2], :], ACT.Tanh,
                                     scale=scale_q[0:r, :]).then_inc(capped, 1)

            def exponent(a, i, n):
                if n < 0:
                    i, n = i - 1, n + CG
                if i < 0:
                    return
                g, c = divmod(n, NC)
                r = rows_of(c)
                if i:
                    act.wait_ge(weighed[a], G * (i - 1) + g + 1)
                if a == 0:
                    act.wait_ge(capped, CG * i + n + 1)
                    part = c // PAIRS
                    nc.scalar.activation(pr[0:r, n, :], th[0:r, n % 2, :], ACT.Exp, scale=cap[0:r, 1:2],
                                         bias=ebias[0:r, i // NB, part:part + 1]).then_inc(prob[0], 1)
                else:
                    act.wait_ge(scored[1], CG * i + n + 1)
                    nc.scalar.activation(pr[0:r, n, :], bank[0:r, SC[n % 2], :], ACT.Exp,
                                         scale=DH ** -0.5).then_inc(prob[1], 1)

            def queries_high(i, g):
                act.wait_ge(q_done, G * i + g + 1)
                nc.scalar.activation(qh[:, i % 2, g, :], bank[:, TURN, :], ACT.Identity,
                                     bias=bq_sb[:, g:g + 1]).then_inc(q_high, 1)

            def copy_max(i):
                act.wait_ge(max_turned, i + 1)
                nc.scalar.activation(mxT[:, i % 2, :], bank[0:32, TURN, :], ACT.Copy).then_inc(max_ready, 1)

            def route_odds(i):
                act.wait_ge(routed, i + 1)
                nc.scalar.activation(lg[0:NX, i % 2, :], bank[0:NX, TURN, :], ACT.Copy).then_inc(logits, 1)
                act.wait_ge(logits_turned, i + 1)
                nc.scalar.activation(route_sb[:, 0, i * NT:(i + 1) * NT, :].rearrange("p t e -> p (t e)"),
                                     bank[:, TURN, 0:NT * NX], ACT.Exp, scale=-1.0).then_inc(odds, 1)

            def rectify(n, at_step):
                act.wait_ge(hidden, at_step)
                nc.scalar.activation(ur[:, n % 4, :], bank[:, HID[n % 4], :], ACT.Relu).then_inc(rectified, 1)

            def hidden_high(n, at_step):
                act.wait_ge(squared, at_step)
                nc.scalar.activation(hh[:, n % 4, :], hf[:, n % 4, :], ACT.Copy).then_inc(high, 1)

            def expert_units(v, last):
                for step in range(2 * STEPS):
                    if step + 2 < 2 * STEPS or not last:
                        rectify(step + 2, v * (2 * STEPS) + (step + 3))
                    if step + 1 < 2 * STEPS or not last:
                        hidden_high(step + 1, v * (2 * STEPS) + (step + 2))

            def low_rank_high(i):
                if i >= BL:
                    return
                act.wait_ge(low1, i + 1)
                nc.scalar.activation(ph[:, i % 2, :], bank[:, DEN[0], :], ACT.Copy).then_inc(low1_high, 1)

            act.wait_ge(gates_loaded, 48)
            nc.scalar.activation(gate[:], gate_raw[:], ACT.Tanh).then_inc(gates_ready, 1)
            nc.scalar.activation(cap[:, 1:2], cap[:, 0:1], ACT.Exp).then_inc(gates_ready, 1)
            act.wait_ge(gates_ready, 2)
            nc.scalar.mul(cap[:, 2:3], cap[:, 1:2], -1.0).then_inc(gates_ready, 1)
            nc.scalar.mul(scale_q[:], scale_raw[:], DH ** -0.5).then_inc(gates_ready, 1)
            turned_high_copy(0, 0, 0)
            turned_high_copy(0, 0, 1)
            act.wait_ge(gates_ready, 4)
            act.wait_ge(chain, 1)
            for i in range(BL):
                for n in range(CG):
                    cap_scores(i, n)
                    if (i, n) == (0, 9):
                        act.wait_ge(ready, 10)
                    exponent(0, i, n - 1)
                    if n in (2, 4):
                        turned_high_copy(0, i + 1, n // 2 - 1)
                    if n in (7, 8):
                        turned_high_copy(1, i - 2, n - 7)
            turned_high_copy(1, BL - 2, 0)
            turned_high_copy(1, BL - 2, 1)
            exponent(0, BL - 1, CG - 1)
            act.wait_ge(weighed[0], G * BL)
            for i in range(BL - 1):
                route_odds(i)
            rectify(0, 1)
            rectify(1, 2)
            hidden_high(0, 1)
            turned_high_copy(1, BL - 1, 0)
            turned_high_copy(1, BL - 1, 1)
            route_odds(BL - 1)
            with act.Fori(0, UNITS // 2 - 1) as v:
                expert_units(v, False)
            expert_units(UNITS // 2 - 1, True)
            turned_high_copy(2, 0, 0)
            turned_high_copy(2, 0, 1)
            queries_high(0, 0)
            queries_high(0, 1)
            turned_high_copy(2, 1, 0)
            turned_high_copy(2, 1, 1)
            copy_max(0)
            for i in range(BL):
                last = i + 1 == BL
                for n in range(CG):
                    exponent(1, i, n)
                    if n in (5, 6):
                        turned_high_copy(3, i - 2, n - 5)
                    if n in (1, 2) and not last:
                        queries_high(i + 1, n - 1)
                    if n == 7 and not last:
                        copy_max(i + 1)
                    if n >= 8:
                        turned_high_copy(2, i + 2, n - 8)
            turned_high_copy(3, BL - 2, 0)
            turned_high_copy(3, BL - 2, 1)
            low_rank_high(0)
            act.wait_ge(weighed[1], G * BL)
            for i in range(BL):
                for n in range(NF):
                    m = NF * i + n
                    act.wait_ge(inner, m + 1)
                    if m >= 4:
                        act.wait_ge(low2, (m - 4) // 2 + 1)
                    nc.scalar.activation(gl[:, n % 4, :], bank[:, SC[n % 2], :], ACT.Gelu_apprx_tanh,
                                         bias=b1_sb[:, n:n + 1]).then_inc(gelu_done, 1)
                    if n == 5:
                        low_rank_high(i + 1)
                if i == 0:
                    turned_high_copy(3, BL - 1, 0)
                    turned_high_copy(3, BL - 1, 1)

        @block.gpsimd
        def _(pool):
            def rsqrt(s, i):
                n = norm_at[s, i]
                pool.wait_ge(aggr, NT * (n + 1))
                if n:
                    pool.wait_ge(rstd_done, n)
                    pool.wait_ge(xn_done, NT * n)
                nc.gpsimd.tensor_tensor(veps[:], mv[:, :, 1], eps_sb[:], ALU.add).then_inc(vare, 1)
                pool.wait_ge(vare, n + 1)
                nc.gpsimd.tensor_tensor(rstd[:], veps[:], minus_half[:], ALU.pow).then_inc(rstd_done, 1)
                if s >= 2:
                    rows = xs[:, i * NT:(i + 1) * NT, :]
                    pool.wait_ge(xn_done, NT * (n + 1))
                    bias = (bo_rows, b2_rows)[s - 2]
                    nc.gpsimd.tensor_tensor(rows, rows, bias[:].unsqueeze(1).to_broadcast([P, NT, E]),
                                            ALU.add).then_inc(biased, 1)

            def mask_values(l):
                for b in range(B):
                    main = vd[:, B * l + b, 0, :].rearrange("p (c n) -> p c n", n=32)
                    nc.gpsimd.tensor_tensor(main, main, same2.unsqueeze(1).to_broadcast([P, E // 32, 32]),
                                            ALU.mult).then_inc(vd_ready, 1)
                    rest = vd[:, B * l + b, 1, :].rearrange("p (g n) -> p g n", n=P)
                    nc.gpsimd.tensor_tensor(rest, rest, same8.unsqueeze(1).to_broadcast([P, G, P]),
                                            ALU.mult).then_inc(vd_ready, 1)

            def split_unit(s):
                nc.gpsimd.tensor_copy(unit_h[:, s], unit_raw[:, s]).then_inc(unit_high, 1)

            def split_unit_low(s):
                nc.gpsimd.tensor_tensor(unit_l[:, s], unit_raw[:, s], unit_h[:, s].bitcast(F32),
                                        ALU.subtract).then_inc(unit_low, 1)

            nc.gpsimd.memset(minus_half[:], -0.5).then_inc(pool_ready, 1)
            nc.gpsimd.memset(eps_sb[:], EPS).then_inc(pool_ready, 1)
            pool.wait_ge(pool_ready, 2)
            rsqrt(0, 0)
            pool.wait_ge(vd_loaded, 64)
            pool.wait_ge(consts_loaded, 16)
            mask_values(0)
            rsqrt(0, 1)
            pool.wait_ge(keys_act, 2)
            spread_keys(nc.gpsimd, 1, 1)
            for key in norms[2:]:
                if key == (2, 0):
                    pool.wait_ge(kv_copied, 4)
                    mask_values(1)
                    for b in range(B):
                        pool.wait_ge(scored[0], CG * NB * (b + 1))
                        spread_keys(nc.gpsimd, b, B + b)
                    with pool.Fori(1, UNITS // 2) as v:
                        for s in range(2):
                            pool.wait_ge(unit_loaded[s], v * 32 + 32)
                            pool.wait_ge(down, v * (2 * STEPS) + (s - 1) * STEPS)
                            pool.sem_inc(carried_pool, 1)
                            split_unit(s)
                            pool.wait_ge(unit_high, v * 2 + (s + 1))
                            split_unit_low(s)
                rsqrt(*key)
                if key == (1, 1):
                    for s in range(2):
                        pool.wait_ge(unit_loaded[s], 32)
                        split_unit(s)
                        pool.wait_ge(unit_high, s + 1)
                        split_unit_low(s)

        @block.vector
        def _(dve):
            v = nc.vector
            chained = [0]

            def link(ins):
                chained[0] += 1
                ins.then_inc(chain, 1)
                dve.wait_ge(chain, chained[0])

            def norm(s, i):
                if (s, i) not in norm_at:
                    return
                n = norm_at[s, i]
                if s == 0:
                    dve.wait_ge(x_loaded[i], 16)
                elif s == 2:
                    dve.wait_ge(mixed, 2 * NT + NT * (BL * (UNITS - 1) + i + 1))
                else:
                    dve.wait_ge(added[s // 2], NT * (i + 1))
                if n:
                    dve.wait_ge(aggr, NT * n)
                    dve.wait_ge(rstd_done, n)
                for t in range(NT):
                    v.bn_stats(bstat[:, t, :], xs[:, i * NT + t, :]).then_inc(stat, 1)
                dve.wait_ge(stat, NT * (n + 1))
                if n:
                    dve.wait_ge(xn_done, NT * n)
                for t in range(NT):
                    v.bn_aggr(mv[:, t, :], bstat[:, t, :]).then_inc(aggr, 1)
                dve.wait_ge(aggr, NT * (n + 1))
                dve.wait_ge(rstd_done, n + 1)
                last = [m for m in norms[:n] if slot[m] == slot[s, i]]
                if last:
                    dve.wait_ge(turned, KE * (order[last[-1]] + 1))
                for t in range(NT):
                    v.tensor_scalar(xn[:, slot[s, i], t, :], xs[:, i * NT + t, :], mv[:, t, 0:1], rstd[:, t:t + 1],
                                    ALU.subtract, ALU.mult).then_inc(xn_done, 1)

            def turned_low_part(s, i, k):
                if (s, i) not in order:
                    return
                dve.wait_ge(turned_high, KE * order[s, i] + k + 1)
                v.tensor_tensor(xTl[:, i, k, :], bank[:, TURN, :], xTh[:, i, k, :].bitcast(F32),
                                ALU.subtract).then_inc(turned_low, 1)

            def normalise(a, i, g):
                if i < 0:
                    return
                dve.wait_ge(weighed[a], G * i + g + 1)
                if i:
                    dve.wait_ge(projected[a], NT // 2 * i)
                v.reciprocal(at[:, g, :], bank[:, DEN[g], :]).then_inc(inverse[a], 1)
                dve.wait_ge(inverse[a], G * i + g + 1)
                v.tensor_tensor(at[:, g, :], bank[:, OUT[g], :], at[:, g, :], ALU.mult).then_inc(normed[a], 1)

            def add(a, i):
                if i < 0:
                    return
                if a == 1:
                    dve.wait_ge(biased, bias_at[2, i])
                for t in range(NT):
                    dve.wait_ge(projected[a], NT // 2 * i + t // 2 + 1)
                    row = xs[:, i * NT + t, :]
                    v.scalar_tensor_tensor(out=row, in0=tile_of(PRJ, t), scalar=gate[:, 2 * a:2 * a + 1], in1=row,
                                           op0=ALU.mult, op1=ALU.add).then_inc(added[a], 1)

            def square(n, at_step):
                dve.wait_ge(rectified, at_step)
                v.tensor_tensor(hf[:, n % 4, :], bank[:, HID[n % 4], :], ur[:, n % 4, :], ALU.mult).then_inc(squared, 1)

            def hidden_low(n, at_step):
                dve.wait_ge(high, at_step)
                v.tensor_tensor(hl[:, n % 4, :], hf[:, n % 4, :], hh[:, n % 4, :].bitcast(F32),
                                ALU.subtract).then_inc(low, 1)

            def choose():
                def wide_(a):
                    return a.unsqueeze(2).to_broadcast([P, AT, NX])

                odd, p, key, one1, one2, w = (route_sb[:, i] for i in range(6))
                m1, k1, m2, k2, den, inv, ginv, _ = (rone[:, i] for i in range(8))
                lower = rank_of_expert.unsqueeze(1).to_broadcast([P, AT, NX])
                dve.wait_ge(odds, BL)
                link(v.tensor_scalar(w, odd, 1.0, None, ALU.add))
                link(v.reciprocal(p, w))
                link(v.tensor_reduce(m1, p, AX.X, ALU.max))
                link(v.tensor_tensor(key, p, wide_(m1), ALU.is_equal))
                link(v.tensor_tensor(key, key, lower, ALU.mult))
                link(v.tensor_reduce(k1, key, AX.X, ALU.max))
                link(v.tensor_tensor(one1, key, wide_(k1), ALU.is_equal))
                link(v.scalar_tensor_tensor(out=w, in0=one1, scalar=-4.0, in1=p, op0=ALU.mult, op1=ALU.add))
                link(v.tensor_reduce(m2, w, AX.X, ALU.max))
                link(v.tensor_tensor(key, w, wide_(m2), ALU.is_equal))
                link(v.tensor_tensor(key, key, lower, ALU.mult))
                link(v.tensor_reduce(k2, key, AX.X, ALU.max))
                link(v.tensor_tensor(one2, key, wide_(k2), ALU.is_equal))
                link(v.tensor_tensor(one1, one1, one2, ALU.add))
                link(v.scalar_tensor_tensor(out=den, in0=m1, scalar=1e-20, in1=m2, op0=ALU.add, op1=ALU.add))
                link(v.reciprocal(inv, den))
                link(v.tensor_scalar(ginv, inv, gate[:, 1:2], None, ALU.mult))
                link(v.tensor_tensor(w, p, one1, ALU.mult))
                link(v.tensor_tensor(w, w, wide_(ginv), ALU.mult))
                wt = w.rearrange("p t e -> p e t")
                narrow = sum(x_ == UW for x_ in WIDTHS)
                per = WIDTHS[-1] // UW
                link(v.tensor_copy(comb[:, 0:narrow, :], wt[:, 0:narrow, :]))
                link(v.tensor_copy(comb[:, narrow:, :].rearrange("p (e r) t -> p e r t", r=per),
                                   wt[:, narrow:, :].unsqueeze(2).to_broadcast([P, NX - narrow, per, AT])))

            def expert_units(v_, last):
                dve.wait_ge(mixed, v_ * (2 * BL * NT) + 2 * NT)
                v.tensor_copy(comb_now[:], comb[:, bass.ts(v_, 2), :]).then_inc(comb_ready, 1)
                for step in range(2 * STEPS):
                    if step + 2 < 2 * STEPS or not last:
                        square(step + 2, v_ * (2 * STEPS) + (step + 3))
                    if step + 1 < 2 * STEPS or not last:
                        hidden_low(step + 1, v_ * (2 * STEPS) + (step + 2))
                    pair, c = divmod(step, UC)
                    if c == UC - 1:
                        s, i = divmod(pair, BL)
                        if pair == 0:
                            dve.wait_ge(comb_ready, v_ + 1)
                        dve.wait_ge(mixed, v_ * (2 * BL * NT) + (pair + 2) * NT)
                        dve.wait_ge(down, v_ * (2 * STEPS) + (step + 1))
                        for t in range(NT):
                            tt = i * NT + t
                            v.scalar_tensor_tensor(out=xs[:, tt, :], in0=tile_of(YB[pair % 2], t),
                                                   scalar=comb_now[:, s, tt:tt + 1], in1=xs[:, tt, :],
                                                   op0=ALU.mult, op1=ALU.add).then_inc(mixed, 1)

            def queries_low(i, g):
                dve.wait_ge(q_high, G * i + g + 1)
                v.scalar_tensor_tensor(out=ql[:, i % 2, g, :], in0=bank[:, TURN, :], scalar=bq_sb[:, g:g + 1],
                                       in1=qh[:, i % 2, g, :].bitcast(F32), op0=ALU.add,
                                       op1=ALU.subtract).then_inc(q_low, 1)

            def row_max(i):
                if i:
                    dve.wait_ge(max_turned, i)
                    dve.wait_ge(split_max, 2 * i)
                for g in range(G):
                    for t in range(NT):
                        m = g * NT + t
                        dve.wait_ge(rowscores, G * NT * i + m + 1)
                        v.tensor_reduce(mx[:, t, g * HG:(g + 1) * HG],
                                        bank[:, SC[m % 2], :].rearrange("p (c k h) -> p c h k", c=PAIRS, h=2),
                                        AX.X, ALU.max).then_inc(rowmax, 1)
                    dve.wait_ge(rowrest, G * i + g + 1)
                    v.tensor_reduce(mxl[:, :, g * HG:(g + 1) * HG],
                                    bank[:, (TURN, PRJ[0])[g], 0:NT * RL].rearrange("p (t k h) -> p t h k", t=NT, h=HG),
                                    AX.X, ALU.max).then_inc(restmax, 1)
                dve.wait_ge(rowmax, G * NT * (i + 1))
                dve.wait_ge(restmax, G * (i + 1))
                link(v.tensor_tensor(mx[:], mx[:], mxl[:], ALU.max))
                v.tensor_copy(mxs[:, :, 0, :].bitcast(F32R), mx[:]).then_inc(split_max, 1)
                dve.wait_ge(split_max, 2 * i + 1)
                v.tensor_tensor(mxs[:, :, 1, :], mx[:], mxs[:, :, 0, :], ALU.subtract).then_inc(split_max, 1)

            def low_rank_low(i):
                if i >= BL:
                    return
                dve.wait_ge(low1_high, i + 1)
                v.tensor_tensor(pl[:, i % 2, :], bank[:, DEN[0], :], ph[:, i % 2, :].bitcast(F32),
                                ALU.subtract).then_inc(low1_low, 1)

            def result(i):
                if i < 0:
                    return
                dve.wait_ge(biased, bias_at[3, i])
                for t in range(NT):
                    dve.wait_ge(ffn_done, NT // 2 * i + t // 2 + 1)
                    row = xs[:, i * NT + t, :]
                    v.scalar_tensor_tensor(out=row, in0=tile_of(PRJ, t), scalar=gate[:, 3:4], in1=row,
                                           op0=ALU.mult, op1=ALU.add).then_inc(res_done, 1)

            def widen(b):
                link(v.tensor_copy(ctx_wide[:, :, 0:P].rearrange("p k (n h) -> p k n h", h=2),
                                   cT[:, b, :, 0:KM].unsqueeze(3).to_broadcast([P, KE, KM, 2])))
                v.tensor_copy(ctx_wide[:, :, P:P + RL].rearrange("p k (n h) -> p k n h", h=HG),
                              cT[:, b, :, KM:KEYS].unsqueeze(3).to_broadcast([P, KE, KL, HG])).then_inc(keys_split, 1)

            def layer1_context():
                dve.wait_ge(mask1_loaded, 16 * 16)
                v.tensor_copy(ident_b[:], ident).then_inc(ready, 1)
                v.tensor_copy(rows_of_key[:], key_raw).then_inc(ready, 1)
                v.tensor_copy(minus_head[:].rearrange("p g n -> p (g n)"), minus_raw).then_inc(ready, 1)
                v.tensor_scalar(mbias[:], mask1_sb, 0.0, MASKED, ALU.is_equal, ALU.mult).then_inc(ready, 1)
                for b in range(B):
                    dve.wait_ge(kv_done, b + 1)
                    for g in range(G):
                        link(v.tensor_scalar(k1[:, b, g, :], bank[:, DEN[b], g * 128:g * 128 + KEYS],
                                             bk_sb[:, g:g + 1], None, ALU.add))
                    link(v.tensor_copy(kh[:, B + b], k1[:, b]))
                    v.tensor_tensor(kl[:, B + b], k1[:, b], kh[:, B + b].bitcast(F32),
                                    ALU.subtract).then_inc(kv_copied, 1)
                for b in range(B):
                    dve.wait_ge(kv_done, B + b + 1)
                    link(v.tensor_tensor(vd[:, B + b, 0, :], bank[:, OUT[b], 0:E], bv_rows[:], ALU.add))
                    v.tensor_tensor(vd[0:RL, B + b, 1, :], bank[0:RL, OUT[b], E:2 * E], bv_rows[0:RL],
                                    ALU.add).then_inc(kv_copied, 1)
                    if b + 1 < B:
                        widen(b + 1)
                v.tensor_copy(rth[:], rt_raw[:]).then_inc(ready, 1)
                v.tensor_copy(wqh[:], wq_raw).then_inc(ready, 1)
                v.tensor_copy(v1h[:], v1_raw).then_inc(ready, 1)
                dve.wait_ge(ready, 7)
                v.tensor_tensor(wql[:], wq_raw, wqh[:].bitcast(F32), ALU.subtract).then_inc(ready, 1)
                v.tensor_tensor(rtl[:], rt_raw[:], rth[:].bitcast(F32), ALU.subtract).then_inc(ready, 1)
                v.tensor_tensor(v1l[:], v1_raw, v1h[:].bitcast(F32), ALU.subtract).then_inc(ready, 1)
                link(v.tensor_scalar(bo_rows[:], bo_rows[:], gate[:, 2:3], None, ALU.mult))
                link(v.tensor_scalar(b2_rows[:], b2_rows[:], gate[:, 3:4], None, ALU.mult))

            v.memset(mask0_sb[:], 0).then_inc(cleared, 1)
            v.memset(vd[:], 0.0).then_inc(cleared, 1)
            norm(0, 0)
            dve.wait_ge(consts_loaded, 16)
            dve.wait_ge(context_loaded, 16 * 3 * B)
            v.tensor_copy(kh[:, 0:B], cT[:]).then_inc(keys_act, 1)
            dve.wait_ge(keys_act, 1)
            v.tensor_tensor(kl[:, 0:B], cT[:], kh[:, 0:B].bitcast(F32), ALU.subtract).then_inc(keys_act, 1)
            dve.wait_ge(keys_act, 2)
            spread_keys(v, 0, 0)
            turned_low_part(0, 0, 0)
            turned_low_part(0, 0, 1)
            dve.wait_ge(gates_ready, 4)
            link(v.tensor_scalar(ebias[:], mask0_sb[:], REMOVED, cap[:, 2:3], ALU.mult, ALU.add))
            norm(0, 1)
            for i in range(BL):
                turned_low_part(0, i + 1, 0)
                if i == 0:
                    dve.wait_ge(weights_loaded, 16 * 5)
                    widen(0)
                normalise(0, i - 1, 1)
                turned_low_part(0, i + 1, 1)
                if i == 0:
                    layer1_context()
                norm(0, i + 2)
                turned_low_part(1, i - 2, 0)
                turned_low_part(1, i - 2, 1)
                normalise(0, i, 0)
                if i == 0:
                    for b in range(B):
                        dve.wait_ge(kv_done, 2 * B + b + 1)
                        v.tensor_copy(mbT[:, b * S:(b + 1) * S],
                                      bank[0:KEYS, PRJ[b], :].bitcast(BF16)).then_inc(kv_copied, 1)
                add(0, i - 1)
                norm(1, i - 1)
            turned_low_part(1, BL - 2, 0)
            turned_low_part(1, BL - 2, 1)
            normalise(0, BL - 1, 1)
            add(0, BL - 1)
            norm(1, BL - 1)
            square(0, 1)
            square(1, 2)
            hidden_low(0, 1)
            turned_low_part(1, BL - 1, 0)
            turned_low_part(1, BL - 1, 1)
            choose()
            dve.sem_inc(mixed, 2 * NT)
            with dve.Fori(0, UNITS // 2 - 1) as v_:
                expert_units(v_, False)
            expert_units(UNITS // 2 - 1, True)
            norm(2, 0)
            turned_low_part(2, 0, 0)
            turned_low_part(2, 0, 1)
            norm(2, 1)
            queries_low(0, 0)
            queries_low(0, 1)
            row_max(0)
            turned_low_part(2, 1, 0)
            turned_low_part(2, 1, 1)
            norm(2, 2)
            for i in range(BL):
                last = i + 1 == BL
                if not last:
                    queries_low(i + 1, 0)
                normalise(1, i - 1, 1)
                if not last:
                    queries_low(i + 1, 1)
                    row_max(i + 1)
                turned_low_part(3, i - 2, 0)
                turned_low_part(3, i - 2, 1)
                normalise(1, i, 0)
                turned_low_part(2, i + 2, 0)
                add(1, i - 1)
                turned_low_part(2, i + 2, 1)
                norm(3, i - 1)
                norm(2, i + 3)
            turned_low_part(3, BL - 2, 0)
            turned_low_part(3, BL - 2, 1)
            normalise(1, BL - 1, 1)
            low_rank_low(0)
            add(1, BL - 1)
            norm(3, BL - 1)
            for i in range(BL):
                result(i - 1)
                low_rank_low(i + 1)
                dve.wait_ge(low2, NF // 2 * (i + 1))
                v.tensor_copy(qq[:, i % 2, :], bank[:, OUT[i % 2], :]).then_inc(low2_copied, 1)
                if i == 0:
                    turned_low_part(3, BL - 1, 0)
                    turned_low_part(3, BL - 1, 1)
            result(BL - 1)


def kernel(**inputs):
    import numpy as _np
    import concourse.bacc as _bacc
    from concourse import mybir as _mybir
    from concourse.bass_utils import run_bass_kernel_spmd as _run

    a = {k: _np.asarray(v) for k, v in inputs.items()}
    hd = 2 * DH
    w_kv = a["L1_xattn_W_kv"].reshape(E, H, hd)
    b_kv = a["L1_xattn_b_kv"].reshape(H, hd)
    r = _np.arange(P)
    row = _np.arange(ROWS)
    main = row < PAIRS * P
    key_of_row = _np.where(main, row % P // 2, KM + (row - PAIRS * P) // HG)
    head_of_row = _np.where(main, row // P * 2 + row % 2, (row - PAIRS * P) % HG)
    consts = _np.zeros((P, C_END), _np.float32)
    consts[:, C_EYE:C_SAME2] = _np.eye(P)
    consts[:, C_SAME2:C_SAME8] = (r[:, None] % 2) == (_np.arange(32)[None, :] // DH)
    consts[:, C_SAME8:C_HEAD] = (r[:, None] % HG) == (r[None, :] // DH)
    consts[:, C_HEAD:C_RANK] = (r[:, None] // DH) == _np.arange(HG)[None, :]
    consts[:, C_RANK:C_MINUS] = NX - _np.arange(NX)
    for g in range(G):
        consts[0:32, C_MINUS + g * ROWS:C_MINUS + (g + 1) * ROWS] = \
            -((_np.arange(32)[:, None] % H) == (g * HG + head_of_row[None, :])).astype(_np.float32)
    consts[0:KEYS, C_KEY:C_END] = _np.arange(KEYS)[:, None] == key_of_row[None, :]
    named = {
        "x": a["x"],
        "ctx_rows": a["ctx_1024"],
        "ctx_t": a["ctx_1024"].transpose(0, 2, 1),
        "mask0": a["mask_Bx1xS2_bk0"].reshape(B, KEYS),
        "mask1": a["mask_BxSxS2_ik0"],
        "gates": _np.stack([a["g_xattn"][0], a["g_ffn"][0], a["g_xattn"][1], a["g_ffn"][1]]),
        "logc": a["L0_xattn_log_C"].reshape(1),
        "scale0": a["L0_xattn_scale"].reshape(1),
        "w_out_t": a["L0_xattn_W_out"].T,
        "router_t": a["L0_ffn_router_w"].T,
        "w1": a["L0_ffn_w1"],
        "w2": a["L0_ffn_w2"],
        "wk": w_kv[:, :, :DH].reshape(E, E),
        "wv": w_kv[:, :, DH:].reshape(E, E),
        "bk": b_kv[:, :DH].reshape(G, P).T,
        "bv": b_kv[:, DH:].reshape(E),
        "wq": a["L1_xattn_W_q"],
        "bq": a["L1_xattn_b_q"].reshape(G, P).T,
        "wo": a["L1_xattn_W_o"],
        "bo": a["L1_xattn_b_o"],
        "u1": a["L1_ffn_U1"],
        "v1": a["L1_ffn_V1"],
        "b1": a["L1_ffn_b1"].reshape(NF, P).T,
        "u2": a["L1_ffn_U2"],
        "v2": a["L1_ffn_V2"],
        "b2": a["L1_ffn_b2"],
        "consts": consts,
    }
    nc = _bacc.Bacc("TRN2", target_bir_lowering=False, num_devices=1)
    arrays, args = {}, []
    for name, v in named.items():
        v = _np.ascontiguousarray(v)
        arrays[f"in_{name}"] = v
        args.append(nc.dram_tensor(f"in_{name}", v.shape, _mybir.dt.from_np(v.dtype), kind="ExternalInput").ap())
    args.append(nc.dram_tensor("out_0", (B, S, E), F32, kind="ExternalOutput").ap())
    flamingo(nc, *args)
    result = _run(nc, [arrays], core_ids=[0])
    return result.results[0]["out_0"]
```

```python
from contextlib import ExitStack

import numpy as np

import concourse.bass as bass
from concourse import mybir

F32 = mybir.dt.float32
F32R = mybir.dt.float32r
BF16 = mybir.dt.bfloat16
I32 = mybir.dt.int32
U8 = mybir.dt.uint8
ALU = mybir.AluOpType
ACT = mybir.ActivationFunctionType
AX = mybir.AxisListType

P = 128
B, S, E = 2, 1024, 256
H, DH = 16, 16
KEYS = 77
G = 2
HG = H // G
PAIRS = HG // 2
KM = P // 2
KL = KEYS - KM
RL = KL * HG
NC = PAIRS + 1
ROWS = KEYS * HG
T = 512
NT = T // P
NB = S // T
BL = B * NB
KE = E // P
WIDTHS = [256] * 4 + [512] * 4
NX = len(WIDTHS)
TOTAL = sum(WIDTHS)
UW = 256
UNITS = TOTAL // UW
UC = UW // P
STEPS = BL * UC
RANK = 64
NF = 1024 // P
MASKED = -1e20
REMOVED = -1e30
EPS = 1e-5
CG = G * NC
SC, DEN, TURN, OUT, PRJ = (0, 1), (2, 3), 4, (5, 6), (7, 3)
REST = (TURN, OUT[0])
FIRST, MIDDLE, LAST = range(3)
SPAN = 2 * STEPS
AHEAD = 3
ORDER = [[(0, 0), (0, 1), (1, 0), (0, 2), (0, 3), (1, 1), (1, 2), (1, 3)],
         [(s, i) for s in range(2) for i in range(BL)]]
ORDER.append([(0, 0), (0, 1), (0, 2), (1, 0), (0, 3), (1, 1), (1, 2), (1, 3)])
EARLY = 10
FREED = UC * (1 + max(n for n, (s, i) in enumerate(ORDER[FIRST]) if s == 0))
C_EYE, C_SAME2, C_SAME8, C_HEAD, C_RANK, C_SUM2, C_SUM8, C_SPREAD, C_MINUS, C_KEY, C_END = (
    int(n) for n in np.cumsum([0, P, 32, P, HG, HG, 32 + HG - 2, 32, T, G * ROWS, ROWS]))


def hidden_bank(part, n):
    if part == FIRST and n < SPAN:
        return n % 3
    return (1, 2, 0)[n % 3] if part == LAST else (1, 2, 0, 3)[n % 4]


def output_banks(part, n):
    return (5, 6) if n % 2 == 0 else (7, 3) if part == LAST or (part == FIRST and n < 5) else (4, 7)


def turned_bank(s, i, k):
    return OUT[0] if (s, i, k) == (0, 0, 1) else TURN


def max_bank(i):
    return TURN if i else DEN[1]


def hidden_slot(part, n):
    return 2 + n % 2 if part == LAST and n >= STEPS else n % 4


def rows_of(c):
    return P if c < PAIRS else RL


def flamingo(nc, x, ctx_rows, ctx_t, mask0, mask1, gates, logc, scale0, w_out_t, router_t, w1, w2, wk, wv, bk, bv,
             wq, bq, wo, bo, u1, v1, b1, u2, v2, b2, consts, out):
    stack = ExitStack()
    with stack:
        def sb(name, shape, dt=F32):
            return stack.enter_context(nc.sbuf_tensor(name, shape, dt))

        def sem(name):
            return stack.enter_context(nc.semaphore(name))

        cst = sb("cst", [P, C_MINUS])
        ident, same2, same8 = cst[:, 0:P], cst[:, C_SAME2:C_SAME8], cst[:, C_SAME8:C_HEAD]
        head_of_feature, rank_of_expert = cst[:, C_HEAD:C_RANK], cst[:, C_RANK:C_SUM2]
        sum2, sum8, spread_head = cst[:, C_SUM2:C_SUM8], cst[:, C_SUM8:C_SPREAD], cst[:, C_SPREAD:C_MINUS]
        minus_head = sb("minus_head", [32, G, ROWS], F32R)
        rows_of_key = sb("rows_of_key", [KEYS, ROWS], BF16)
        ident_b = sb("ident_b", [P, P], BF16)
        minus_half, eps_sb = sb("minus_half", [P, NT]), sb("eps_sb", [P, NT])
        unit_raw = sb("unit_raw", [P, 2, KE + UC, UW])
        unit_h, unit_l = sb("unit_h", [P, 2, KE + UC, UW], F32R), sb("unit_l", [P, 2, KE + UC, UW], F32R)
        rt_raw, rth, rtl = sb("rt_raw", [P, KE, NX]), sb("rth", [P, KE, NX], F32R), sb("rtl", [P, KE, NX], F32R)
        w_out_sb, wo_sb = sb("w_out_sb", [P, KE, E]), sb("wo_sb", [P, KE, E])
        wqh, wql = sb("wqh", [P, KE, E], F32R), sb("wql", [P, KE, E], F32R)
        u1h, u1l = sb("u1h", [P, KE, RANK], F32R), sb("u1l", [P, KE, RANK], F32R)
        u2_sb, v2_sb = sb("u2_sb", [P, NF, RANK]), sb("v2_sb", [P, E])
        v1h, v1l = sb("v1h", [RANK, NF * P], F32R), sb("v1l", [RANK, NF * P], F32R)
        bk_sb, bq_sb, b1_sb = sb("bk_sb", [P, G]), sb("bq_sb", [P, G]), sb("b1_sb", [P, NF])
        bo_rows, b2_rows = sb("bo_rows", [P, E]), sb("b2_rows", [P, E])
        gate_raw, gate = sb("gate_raw", [P, 4]), sb("gate", [P, 4])
        cap, scale_raw, scale_q = sb("cap", [P, 3]), sb("scale_raw", [P, 1]), sb("scale_q", [P, 1])
        cT = sb("cT", [P, B, KE, KEYS])
        kh, kl = sb("kh", [P, 2 * B, G, KEYS], F32R), sb("kl", [P, 2 * B, G, KEYS], F32R)
        ctx_wide_flat = sb("ctx_wide", [P, T])
        ctx_wide = ctx_wide_flat[:, 0:KE * (P + RL)].rearrange("p (k n) -> p k n", k=KE)
        mask0_sb = sb("mask0_sb", [P, B, 2], U8)
        ebias = sb("ebias", [P, B, 2])
        mbias = sb("mbias", [P, BL * NT, KEYS], BF16)
        mbT = sb("mbT", [KEYS, B * S], BF16)
        kdh, kdl = sb("kdh", [P, B, G, ROWS], F32R), sb("kdl", [P, B, G, ROWS], F32R)
        vd = sb("vd", [P, 2 * B, 2, E])
        xs = sb("xs", [P, BL * NT, E])
        xn = sb("xn", [P, 2, NT, E])
        xTh, xTl = sb("xTh", [P, BL, KE, T], F32R), sb("xTl", [P, BL, KE, T], F32R)
        bstat, mv = sb("bstat", [P, NT, 6]), sb("mv", [P, NT, 2])
        veps, rstd = sb("veps", [P, NT]), sb("rstd", [P, NT])
        work = sb("work", [P, CG, T])
        pr, gl = work[:], work[:, 0:4, :]
        ur, hf = work[:, 0:4, :], work[:, 4:8, :]
        wide = unit_raw[:].rearrange("p s k n -> p (s k n)")
        mask1_sb = wide[:, 0:BL * NT * KEYS].bitcast(I32).rearrange("p (t n) -> p t n", n=KEYS)
        v1_raw = wide[0:RANK, 0:NF * P]
        wq_raw = wide[:, 3 * T:4 * T].rearrange("p (k n) -> p k n", k=KE)
        wide = xs[:, 2 * NT:, :].rearrange("p t n -> p (t n)")
        minus_raw, key_raw = wide[0:32, 0:G * ROWS], wide[0:KEYS, G * ROWS:(G + 1) * ROWS]
        th = sb("th", [P, 2, T])
        qq = th
        lg = ctx_wide_flat
        at, inv_sb = sb("at", [P, G, T]), sb("inv_sb", [P, P])
        wk_sb, wv_sb = (xn[:, 1, g * KE:(g + 1) * KE, :] for g in range(G))
        split = sb("split", [P, 2, 2, G, T], F32R)
        qh, ql = split[:, 0], split[:, 1]
        hh, hl = (split[:, n].rearrange("p a g n -> p (a g) n") for n in range(2))
        ph, pl = split[0:RANK, 0, :, 0], split[0:RANK, 1, :, 0]
        mxs = sb("mxs", [P, NT, 2, H])
        mxT = sb("mxT", [32, 2, T], F32R)
        AT = BL * NT
        route_sb = sb("route_sb", [P, 6, AT, NX])
        early = route_sb[:].rearrange("p a t n -> p (a t n)")
        bv_rows = early[:, 0:E]
        k1 = early[:, E:E + B * G * KEYS].rearrange("p (b g n) -> p b g n", b=B, g=G)
        at_u1 = E + B * G * KEYS
        u1_raw = early[:, at_u1:at_u1 + KE * RANK].rearrange("p (k n) -> p k n", k=KE)
        rone = sb("rone", [P, 8, AT])
        comb, comb_now = sb("comb", [P, UNITS, AT]), sb("comb_now", [P, 2, AT])
        mx, mxl = comb[:, 0:NT, :], comb[:, NT:2 * NT, :]

        bank = stack.enter_context(nc.psum_tensor("bank", [P, 8, 512], F32))

        def tile_of(banks, t):
            return bank[:, banks[t // 2], (t % 2) * E:(t % 2 + 1) * E]

        gates_loaded, gates_ready = sem("gates_loaded"), sem("gates_ready")
        consts_loaded, context_loaded, weights_loaded = sem("consts_loaded"), sem("context_loaded"), sem("weights_loaded")
        vd_loaded, mask0_loaded, mask1_loaded = sem("vd_loaded"), sem("mask0_loaded"), sem("mask1_loaded")
        v1_loaded, v1_split, u1_split = sem("v1_loaded"), sem("v1_split"), sem("u1_split")
        x_loaded = [sem(f"x_loaded{i}") for i in range(BL)]
        cleared, ready, pool_ready = sem("cleared"), sem("ready"), sem("pool_ready")
        keys_split, keys_act = sem("keys_split"), sem("keys_act")
        kd_ready, vd_ready = [sem(f"kd_ready{l}") for l in range(2 * B)], sem("vd_ready")
        carried, carried_pool, chain = sem("carried"), sem("carried_pool"), sem("chain")
        kv_done, kv_copied = sem("kv_done"), sem("kv_copied")
        unit_loaded = [sem("unit_loaded0"), sem("unit_loaded1")]
        unit_high, unit_low = sem("unit_high"), sem("unit_low")
        stat, aggr, vare, rstd_done, xn_done = sem("stat"), sem("aggr"), sem("vare"), sem("rstd_done"), sem("xn_done")
        turned, turned_high, turned_low = sem("turned"), sem("turned_high"), sem("turned_low")
        scored = [sem("scored0"), sem("scored1")]
        capped = sem("capped")
        prob = [sem("prob0"), sem("prob1")]
        weighed = [sem("weighed0"), sem("weighed1")]
        spreaded = [sem("spreaded0"), sem("spreaded1")]
        weighed_copied = [sem("weighed_copied0"), sem("weighed_copied1")]
        inverse = [sem("inverse0"), sem("inverse1")]
        normed = [sem("normed0"), sem("normed1")]
        projected = [sem("projected0"), sem("projected1")]
        added = [sem("added0"), sem("added1")]
        routed, logits, logits_turned = sem("routed"), sem("logits"), sem("logits_turned")
        odds, comb_ready = sem("odds"), sem("comb_ready")
        hidden, rectified, squared = sem("hidden"), sem("rectified"), sem("squared")
        high, low, low_early, low_late = sem("high"), sem("low"), sem("low_early"), sem("low_late")
        down, mixed = sem("down"), sem("mixed")
        q_done, q_high, q_low = sem("q_done"), sem("q_high"), sem("q_low")
        rowscores, rowmax, rowrest, restmax = sem("rowscores"), sem("rowmax"), sem("rowrest"), sem("restmax")
        split_max, max_turned, max_ready = sem("split_max"), sem("max_turned"), sem("max_ready")
        biased = sem("biased")
        low1, low1_high, low1_low = sem("low1"), sem("low1_high"), sem("low1_low")
        inner, gelu_done, low2, low2_copied = sem("inner"), sem("gelu_done"), sem("low2"), sem("low2_copied")
        ffn_done, res_done = sem("ffn_done"), sem("res_done")
        stored = sem("stored")

        order, turns = {}, []
        turns += [(0, 0)]
        for i in range(BL):
            if i + 1 < BL:
                turns.append((0, i + 1))
            if i >= 2:
                turns.append((1, i - 2))
        turns += [(1, BL - 2), (1, BL - 1), (2, 0), (2, 1)]
        for i in range(BL):
            if i >= 2:
                turns.append((3, i - 2))
            if i + 2 < BL:
                turns.append((2, i + 2))
        turns += [(3, BL - 2), (3, BL - 1)]
        for n, key in enumerate(turns):
            order[key] = n
        norms = [(0, 0), (0, 1)]
        for i in range(BL):
            if i + 2 < BL:
                norms.append((0, i + 2))
            if i >= 1:
                norms.append((1, i - 1))
        norms += [(1, BL - 1), (2, 0), (2, 1), (2, 2)]
        for i in range(BL):
            if i >= 1:
                norms.append((3, i - 1))
            if i + 3 < BL:
                norms.append((2, i + 3))
        norms += [(3, BL - 1)]
        norm_at = {key: n for n, key in enumerate(norms)}
        slot = {key: (0 if key[0] % 2 == 0 else 1) for key in norms}

        late = [key for key in norms if key[0] >= 2]
        bias_at = {key: n + 1 for n, key in enumerate(late)}

        def spread_keys(engine, b, l, g):
            for dst, src in ((kdh, kh), (kdl, kl)):
                heads = head_of_feature.rearrange("p (c h) -> p c h", h=2).unsqueeze(2) \
                    .to_broadcast([P, PAIRS, KM, 2])
                k = src[:, l, g, 0:KM].bitcast(F32).unsqueeze(1).unsqueeze(3).to_broadcast([P, PAIRS, KM, 2])
                engine.tensor_tensor(dst[:, b, g, 0:PAIRS * P].rearrange("p (c k h) -> p c k h", c=PAIRS, h=2),
                                     k, heads, ALU.mult).then_inc(kd_ready[l], 1)
                k = src[:, l, g, KM:KEYS].bitcast(F32).unsqueeze(2).to_broadcast([P, KL, HG])
                engine.tensor_tensor(dst[:, b, g, PAIRS * P:ROWS].rearrange("p (k h) -> p k h", h=HG),
                                     k, head_of_feature.unsqueeze(1).to_broadcast([P, KL, HG]),
                                     ALU.mult).then_inc(kd_ready[l], 1)

        def wait_low(engine, v, part, step):
            if part == FIRST and step < EARLY:
                engine.wait_ge(low_early, step + 1)
            elif part == LAST and step >= STEPS:
                engine.wait_ge(low_late, step - STEPS + 1)
            else:
                engine.wait_ge(low, v * SPAN + (step + 1 - EARLY))

        block = stack.enter_context(nc.Block())

        @block.sync
        def _(sp):
            xv = x.rearrange("b (t p) e -> p (b t) e", p=P)
            ov = out.rearrange("b (t p) e -> p (b t) e", p=P)

            def load_x(i):
                sp.dma_start(xs[:, i * NT:(i + 1) * NT, :], xv[:, i * NT:(i + 1) * NT, :]).then_inc(x_loaded[i], 16)

            load_x(0)
            sp.dma_start(cst[:], consts[:, 0:C_MINUS]).then_inc(consts_loaded, 16)
            for b in range(B):
                sp.dma_start(cT[:, b], ctx_t[b].rearrange("(k p) n -> p k n", p=P)).then_inc(context_loaded, 16)
            sp.dma_start(gate_raw[:], gates.partition_broadcast(P)).then_inc(gates_loaded, 16)
            sp.dma_start(cap[:, 0:1], logc.partition_broadcast(P)).then_inc(gates_loaded, 16)
            sp.dma_start(scale_raw[:], scale0.partition_broadcast(P)).then_inc(gates_loaded, 16)
            sp.wait_ge(cleared, 2)
            for b in range(B):
                for part, (k0, n, heads) in enumerate(((0, KM, 2), (KM, KL, HG))):
                    src = mask0[b, k0:k0 + n].unsqueeze(1).unsqueeze(1).to_broadcast([n, heads, 1])
                    sp.dma_start(mask0_sb[0:n * heads, b, part:part + 1], src).then_inc(mask0_loaded, 16)
                    src = ctx_rows[b, k0:k0 + n, :].unsqueeze(1).to_broadcast([n, heads, E])
                    sp.dma_start(vd[0:n * heads, b, part, :], src).then_inc(vd_loaded, 16)
            load_x(1)
            for dst, src in ((wk_sb, wk), (wv_sb, wv)):
                sp.dma_start(dst, src.rearrange("(k p) n -> p k n", p=P)).then_inc(weights_loaded, 16)
            sp.dma_start(bk_sb[:], bk).then_inc(weights_loaded, 16)
            sp.dma_start(bv_rows, bv.partition_broadcast(P)).then_inc(weights_loaded, 16)
            sp.dma_start(w_out_sb[:], w_out_t.rearrange("(k p) n -> p k n", p=P)).then_inc(weights_loaded, 16)
            sp.dma_start(mask1_sb, mask1.rearrange("b (t p) n -> p (b t) n", p=P)).then_inc(mask1_loaded, 16)
            sp.dma_start(minus_raw, consts[0:32, C_MINUS:C_KEY]).then_inc(mask1_loaded, 16)
            sp.dma_start(rt_raw[:], router_t.rearrange("(k p) n -> p k n", p=P)).then_inc(mask1_loaded, 16)
            sp.dma_start(wq_raw, wq.rearrange("(k p) n -> p k n", p=P)).then_inc(mask1_loaded, 16)
            for half in range(2):
                rs = slice(half * RANK, (half + 1) * RANK)
                sp.dma_start(v2_sb[rs, :], v2).then_inc(mask1_loaded, 16)
            for dst, src in ((bq_sb, bq), (b1_sb, b1)):
                sp.dma_start(dst[:], src).then_inc(mask1_loaded, 16)
            for dst, src in ((bo_rows, bo), (b2_rows, b2)):
                sp.dma_start(dst[:], src.partition_broadcast(P)).then_inc(mask1_loaded, 16)
            sp.dma_start(key_raw, consts[0:KEYS, C_KEY:C_END]).then_inc(mask1_loaded, 16)
            for dst, src in ((wo_sb[:], wo), (u1_raw, u1), (u2_sb[:], u2)):
                sp.dma_start(dst, src.rearrange("(k p) n -> p k n", p=P)).then_inc(mask1_loaded, 16)
            sp.wait_ge(ready, 3)
            load_x(2)
            load_x(3)
            sp.wait_ge(ready, 7)

            w1v, w2v = w1.rearrange("(k p) n -> p k n", p=P), w2.rearrange("(j p) d -> p j d", p=P)

            def load_unit(u, s):
                sp.dma_start(unit_raw[:, s, 0:KE, :], w1v[:, :, bass.ts(u, UW)]).then_inc(unit_loaded[s], 16)
                sp.dma_start(unit_raw[:, s, KE:KE + UC, :], w2v[:, bass.ts(u, UC), :]).then_inc(unit_loaded[s], 16)

            for s in range(2):
                load_unit(s, s)
            with sp.Fori(1, UNITS // 2) as v:
                for s in range(2):
                    src = sp.snap(v * 2 + s)
                    sp.wait_ge(unit_low, v * 2 + (s - 1))
                    sp.sem_inc(carried, 1)
                    load_unit(src, s)
            sp.wait_ge(unit_low, UNITS - 1)
            sp.dma_start(v1_raw, v1).then_inc(v1_loaded, 16)
            for n in range(2 * BL):
                tiles = slice(n * NT // 2, (n + 1) * NT // 2)
                sp.wait_ge(res_done, tiles.stop)
                sp.dma_start(ov[:, tiles, :], xs[:, tiles, :]).then_inc(stored, 16)
            sp.wait_ge(stored, 16 * 2 * BL)

        @block.tensor
        def _(pe):
            def split3(o, ah, al, bh, bl, first, last):
                pe.matmul(o, ah, bl, start=first, stop=False, skip_group_check=True)
                pe.matmul(o, al, bh, start=False, stop=False, skip_group_check=True)
                return pe.matmul(o, ah, bh, start=False, stop=last, skip_group_check=True)

            def turn(s, i, k):
                if (s, i) not in order:
                    return
                pe.wait_ge(xn_done, NT * (norm_at[s, i] + 1))
                n = KE * order[s, i] + k
                if n >= 2:
                    pe.wait_ge(turned_low, n)
                if k == 0 and s == 2 and i:
                    pe.wait_ge(*((q_low, G) if i == 1 else (max_ready, i)))
                if k == 0 and s == 3:
                    pe.wait_ge(*((restmax, G * (i + 3) + 1) if i + 3 < BL else (max_ready, BL)))
                for t in range(NT):
                    ins = pe.transpose(bank[:, turned_bank(s, i, k), t * P:(t + 1) * P],
                                       xn[:, slot[s, i], t, k * P:(k + 1) * P], ident)
                ins.then_inc(turned, 1)

            def xT_ready(s, i):
                pe.wait_ge(turned_high, KE * (order[s, i] + 1))
                pe.wait_ge(turned_low, KE * (order[s, i] + 1))

            def scores(a, i, g, c):
                b, r = i // NB, rows_of(c)
                n = CG * i + NC * g + c
                s = bank[0:r, SC[n % 2], :]
                if n >= 2:
                    pe.wait_ge(capped if a == 0 else prob[1], n - 1)
                if a == 1 and i and n % CG == 0:
                    pe.wait_ge(max_ready, i + 1)
                if a == 1 and g == 1 and c < 2 and i + 1 < BL:
                    pe.wait_ge(rowmax, G * NT * (i + 2))
                ks = slice(P * c, P * c + r)
                if a == 0:
                    ins = split3(s, kdh[:, b, g, ks], kdl[:, b, g, ks], xTh[:, i, g, :], xTl[:, i, g, :], True, True)
                else:
                    pe.matmul(s, rows_of_key[:, ks], mbT[:, i * T:(i + 1) * T], start=True, stop=False,
                              skip_group_check=True)
                    split3(s, kdh[:, b, g, ks], kdl[:, b, g, ks], qh[:, i % 2, g, :], ql[:, i % 2, g, :], False, False)
                    ins = pe.matmul(s, minus_head[:, g, ks], mxT[:, i % 2, :], start=False, stop=True,
                                    skip_group_check=True)
                ins.then_inc(scored[a], 1)

            def weigh(a, i, g):
                weigh_pairs(a, i, g)
                weigh_rest(a, i, g)

            def weigh_pairs(a, i, g):
                if i < 0:
                    return
                b = i // NB
                if i:
                    pe.wait_ge(normed[a], G * (i - 1) + g + 1)
                if i and g:
                    pe.wait_ge(added[a], NT * i)
                if (i, g) == (0, 0):
                    pe.wait_ge(vd_ready, 4 * (a + 1))
                if a == 1 and g == 0:
                    pe.wait_ge(restmax, G * min(i + 2, BL))
                pe.wait_ge(prob[a], CG * i + NC * g + PAIRS)
                for c in range(PAIRS):
                    ps = slice(32 * c, 32 * c + 32)
                    pe.matmul(bank[ps, OUT[g], :], vd[:, B * a + b, 0, g * P + 32 * c:g * P + 32 * c + 32],
                              pr[:, NC * g + c, :], start=True, stop=False, skip_group_check=True)
                for c in range(PAIRS):
                    for t in range(NT):
                        pe.matmul(bank[32 * t:32 * t + 32, DEN[g], 0:P], sum2[:, HG - 2 - 2 * c:HG - 2 - 2 * c + 32],
                                  pr[:, NC * g + c, t * P:(t + 1) * P], start=(c == 0), stop=False,
                                  skip_group_check=True)

            def weigh_rest(a, i, g):
                if i < 0:
                    return
                b = i // NB
                pe.wait_ge(prob[a], CG * i + NC * (g + 1))
                for t in range(NT):
                    pe.matmul(bank[32 * t:32 * t + 32, DEN[g], 0:P], sum8[0:RL],
                              pr[0:RL, NC * g + PAIRS, t * P:(t + 1) * P], start=False, stop=True,
                              skip_group_check=True)
                pe.matmul(bank[:, OUT[g], :], vd[0:RL, B * a + b, 1, g * P:(g + 1) * P], pr[0:RL, NC * g + PAIRS, :],
                          start=False, stop=True, skip_group_check=True).then_inc(weighed[a], 1)

            def spread(a, i, g):
                if i < 0:
                    return
                pe.wait_ge(inverse[a], G * i + g + 1)
                for t in range(NT):
                    ins = pe.matmul(bank[:, DEN[g], t * P:(t + 1) * P], spread_head[:, t * P:(t + 1) * P], inv_sb[:],
                                    start=True, stop=True)
                ins.then_inc(spreaded[a], 1)

            def project(a, i, tiles=range(NT)):
                if i < 0:
                    return
                w = w_out_sb if a == 0 else wo_sb
                pe.wait_ge(normed[a], G * (i + 1))
                if i:
                    pe.wait_ge(added[a], NT * i)
                for t in tiles:
                    for g in range(G):
                        ins = pe.matmul(tile_of(PRJ, t), at[:, g, t * P:(t + 1) * P], w[:, g, :],
                                        start=(g == 0), stop=(g == G - 1))
                    if t % 2:
                        ins.then_inc(projected[a], 1)

            def prepare_keys():
                pe.wait_ge(weights_loaded, 16 * 5)
                for b in range(B):
                    for g in range(G):
                        for k in range(KE):
                            ins = pe.matmul(bank[:, DEN[b], g * 128:g * 128 + KEYS], wk_sb[:, k, g * P:(g + 1) * P],
                                            cT[:, b, k, :], start=(k == 0), stop=(k == KE - 1))
                    ins.then_inc(kv_done, 1)

            def prepare_values(b):
                pe.wait_ge(keys_split, b + 1)
                for part, r in enumerate((P, RL)):
                    for k in range(KE):
                        ins = pe.matmul(bank[0:r, OUT[b], part * E:(part + 1) * E],
                                        ctx_wide[:, k, part * P:part * P + r], wv_sb[:, k, :],
                                        start=(k == 0), stop=(k == KE - 1))
                ins.then_inc(kv_done, 1)

            def prepare_mask(b):
                pe.wait_ge(ready, 4)
                if b:
                    pe.wait_ge(kv_copied, 5)
                for t in range(NB * NT):
                    ins = pe.transpose(bank[:, PRJ[0], :].bitcast(BF16)[0:KEYS, t * P:(t + 1) * P],
                                       mbias[:, b * NB * NT + t, :], ident_b[:])
                ins.then_inc(kv_done, 1)

            def attend0():
                for i in range(BL):
                    if i % NB == 0:
                        pe.wait_ge(kd_ready[i // NB], 4 if i == 0 else 4 * G)
                    xT_ready(0, i)
                    scores(0, i, 0, 0)
                    if i >= 2:
                        turn(0, i + 1, 0)
                    if i == BL - 1:
                        pe.wait_ge(ready, 8)
                        route(0)
                    scores(0, i, 0, 1)
                    if i == BL - 1:
                        turn_logits(0)
                    if i == 1:
                        prepare_mask(0)
                    weigh_pairs(0, i - 1, 1)
                    scores(0, i, 0, 2)
                    if i == 1:
                        turn(0, 2, 0)
                    spread(0, i - 1, 0)
                    weigh_rest(0, i - 1, 1)
                    if i == 0:
                        prepare_keys()
                    scores(0, i, 0, 3)
                    turn(0, i + 1, 1 if i else 0)
                    scores(0, i, 0, 4)
                    if i == 1:
                        prepare_mask(1)
                    if i == 0:
                        prepare_values(0)
                        pe.wait_ge(kd_ready[0], 4 * G)
                    scores(0, i, 1, 0)
                    if i == 0:
                        turn(0, 1, 1)
                        prepare_values(1)
                    spread(0, i - 1, 1)
                    turn(1, i - 2, 0)
                    scores(0, i, 1, 1)
                    if i == 1:
                        pe.wait_ge(kv_copied, 6)
                    project(0, i - 1, range(0, NT // 2))
                    turn(1, i - 2, 1)
                    scores(0, i, 1, 2)
                    project(0, i - 1, range(NT // 2, NT))
                    scores(0, i, 1, 3)
                    if i == 0:
                        pe.wait_ge(kv_copied, 4)
                    weigh_pairs(0, i, 0)
                    scores(0, i, 1, 4)
                    weigh_rest(0, i, 0)

            def attend1():
                for i in range(BL):
                    last = i + 1 == BL
                    scores(1, i, 0, 0)
                    scores(1, i, 0, 1)
                    if i and not last:
                        queries(i + 1, 0)
                    scores(1, i, 0, 2)
                    weigh_pairs(1, i - 1, 1)
                    if i and not last:
                        queries(i + 1, 1)
                    scores(1, i, 0, 3)
                    weigh_rest(1, i - 1, 1)
                    scores(1, i, 0, 4)
                    spread(1, i - 1, 1)
                    if last:
                        scores(1, i, 1, 0)
                    row_scores(i + 1, 0)
                    project(1, i - 1, range(0, NT // 2))
                    row_scores(i + 1, 1)
                    project(1, i - 1, range(NT // 2, NT))
                    if not last:
                        scores(1, i, 1, 0)
                    turn(3, i - 2, 0)
                    scores(1, i, 1, 1)
                    scores(1, i, 1, 2)
                    turn(3, i - 2, 1)
                    weigh(1, i, 0)
                    if not last:
                        turn_max(i + 1)
                    scores(1, i, 1, 3)
                    spread(1, i, 0)
                    turn(2, i + 2, 0)
                    scores(1, i, 1, 4)
                    turn(2, i + 2, 1)

            def queries(i, g):
                xT_ready(2, i)
                if g or i:
                    pe.wait_ge(q_low, G * i + g)
                for k in range(KE):
                    gs = slice(g * P, (g + 1) * P)
                    ins = split3(bank[:, TURN, :], wqh[:, k, gs], wql[:, k, gs], xTh[:, i, k, :], xTl[:, i, k, :],
                                 k == 0, k == KE - 1)
                ins.then_inc(q_done, 1)

            def row_scores(i, g):
                if i >= BL:
                    return
                b = i // NB
                pe.wait_ge(q_high, G * (i + 1))
                pe.wait_ge(q_low, G * (i + 1))
                for t in range(NT):
                    m = g * NT + t
                    if m >= 2:
                        pe.wait_ge(rowmax, G * NT * i + m - 1)
                    elif i:
                        pe.wait_ge(prob[1], CG * (i - 1) + NC)
                    o = bank[:, SC[m % 2], :]
                    mb = mbias[:, i * NT + t, 0:KM].unsqueeze(1).unsqueeze(3).to_broadcast([P, PAIRS, KM, 2])
                    pe.matmul(o.rearrange("p (c k h) -> p c k h", c=PAIRS, h=2), ident_b[:], mb,
                              start=True, stop=False)
                    pe.matmul(o, qh[:, i % 2, g, t * P:(t + 1) * P], kdh[:, b, g, 0:PAIRS * P],
                              start=False, stop=True).then_inc(rowscores, 1)
                if i == 0:
                    pe.wait_ge(*((mixed, 2 * NT + UNITS * BL * NT) if g else (turned_low, KE * (order[2, 1] + 1))))
                elif g and i >= 2:
                    pe.wait_ge(normed[1], G * (i - 2) + 1)
                for t in range(NT):
                    o = bank[:, REST[g], t * RL:(t + 1) * RL]
                    mb = mbias[:, i * NT + t, KM:KEYS].unsqueeze(2).to_broadcast([P, KL, HG])
                    pe.matmul(o.rearrange("p (k h) -> p k h", h=HG), ident_b[:], mb, start=True, stop=False)
                    ins = pe.matmul(o, qh[:, i % 2, g, t * P:(t + 1) * P], kdh[:, b, g, PAIRS * P:ROWS],
                                    start=False, stop=True)
                ins.then_inc(rowrest, 1)

            def turn_max(i):
                pe.wait_ge(split_max, 2 * (i + 1))
                if i >= 3:
                    xT_ready(3, i - 3)
                for t in range(NT):
                    ins = pe.transpose(bank[0:32, max_bank(i), t * P:(t + 1) * P],
                                       mxs[:, t, :, :].rearrange("p a h -> p (a h)"), ident)
                ins.then_inc(max_turned, 1)

            def first_product(part, n):
                pair, c = divmod(n, UC)
                s, i = ORDER[part][pair % len(ORDER[part])]
                for k in range(KE):
                    ws = slice(c * P, (c + 1) * P)
                    ins = split3(bank[:, hidden_bank(part, n), :], unit_h[:, s, k, ws], unit_l[:, s, k, ws],
                                 xTh[:, i, k, :], xTl[:, i, k, :], k == 0, k == KE - 1)
                ins.then_inc(hidden, 1)

            def route(i):
                xT_ready(1, max(i, BL - 1) if i > 1 else i)
                if i:
                    pe.wait_ge(odds, i)
                for k in range(KE):
                    ins = split3(bank[0:NX, TURN, :], rth[:, k, :], rtl[:, k, :], xTh[:, i, k, :], xTl[:, i, k, :],
                                 k == 0, k == KE - 1)
                ins.then_inc(routed, 1)

            def turn_logits(i):
                pe.wait_ge(logits, i + 1)
                for t in range(NT):
                    ins = pe.transpose(bank[:, TURN, t * NX:(t + 1) * NX], lg[0:NX, t * P:(t + 1) * P],
                                       ident[0:NX, 0:NX])
                ins.then_inc(logits_turned, 1)

            def expert_step(v, part, step):
                first_ahead(v, part, step)
                second_product(v, part, step)

            def first_ahead(v, part, step):
                ahead = step + AHEAD
                if ahead < SPAN or part != LAST:
                    pair, c = divmod(ahead, UC)
                    s, i = ORDER[part][pair % len(ORDER[part])]
                    later = 2 * (ahead // SPAN)
                    if c == 0 and (s, i) == (s, 0):
                        pe.wait_ge(unit_low, v * 2 + (later + s + 1))
                    if part == FIRST and s == 0 and i >= BL - 2:
                        xT_ready(1, i)
                    pe.wait_ge(squared, v * SPAN + (step + 1))
                    first_product(part, ahead)

            def second_product(v, part, step):
                pair, c = divmod(step, UC)
                s, i = ORDER[part][pair]
                wait_low(pe, v, part, step)
                if c == 0:
                    pe.wait_ge(mixed, v * (2 * BL * NT) + (pair + 1) * NT)
                n = hidden_slot(part, step)
                for t in range(NT):
                    ts = slice(t * P, (t + 1) * P)
                    ins = split3(tile_of(output_banks(part, pair), t), hh[:, n, ts], hl[:, n, ts],
                                 unit_h[:, s, KE + c, :], unit_l[:, s, KE + c, :],
                                 c == 0 and t % 2 == 0, c == UC - 1)
                ins.then_inc(down, 1)

            def low_rank_in(i):
                if i >= BL:
                    return
                xT_ready(3, i)
                if i:
                    pe.wait_ge(low1_low, i)
                for k in range(KE):
                    ins = split3(bank[0:RANK, DEN[0], :], u1h[:, k, :], u1l[:, k, :],
                                 xTh[:, i, k, :], xTl[:, i, k, :], k == 0, k == KE - 1)
                ins.then_inc(low1, 1)

            def low_rank_out(i):
                if i < 0:
                    return
                pe.wait_ge(low2_copied, i + 1)
                if i:
                    pe.wait_ge(res_done, NT * i)
                else:
                    pe.wait_ge(added[1], NT * BL)
                for t in range(NT):
                    ins = pe.matmul(tile_of(PRJ, t), qq[:, i % 2, t * P:(t + 1) * P], v2_sb[:], start=True, stop=True)
                    if t % 2:
                        ins.then_inc(ffn_done, 1)

            def low_rank(i):
                for n in range(NF + 2):
                    m = NF * i + n
                    if n < NF:
                        if m >= 2:
                            pe.wait_ge(gelu_done, m - 1)
                        if n == 0:
                            pe.wait_ge(low1_high, i + 1)
                            pe.wait_ge(low1_low, i + 1)
                        ns = slice(n * P, (n + 1) * P)
                        split3(bank[:, SC[n % 2], :], v1h[:, ns], v1l[:, ns], ph[:, i % 2, :], pl[:, i % 2, :],
                               True, True).then_inc(inner, 1)
                    if n >= 3 and n % 2:
                        pe.wait_ge(gelu_done, NF * i + n - 1)
                        for j in (n - 3, n - 2):
                            rs = slice(RANK * (j % 2), RANK * (j % 2) + RANK)
                            ins = pe.matmul(bank[rs, OUT[i % 2], :], u2_sb[:, j, :], gl[:, j % 4, :],
                                            start=(j < 2), stop=(j >= NF - 2), skip_group_check=True)
                        ins.then_inc(low2, 1)
                    if n == 3:
                        low_rank_out(i - 1)
                    if n == 5:
                        low_rank_in(i + 1)
                    if (i, n) == (0, 1):
                        spread(1, BL - 1, 1)
                    if (i, n) == (0, 4):
                        project(1, BL - 1)
                    if i < 2 and n in (6, 8):
                        turn(3, BL - 2 + i, n // 2 - 3)

            pe.wait_ge(consts_loaded, 16)
            turn(0, 0, 0)
            turn(0, 0, 1)
            attend0()
            route(1)
            pe.wait_ge(unit_low, 1)
            pe.wait_ge(prob[0], CG * BL - 1)
            first_product(FIRST, 0)
            turn_logits(1)
            spread(0, BL - 1, 0)
            weigh(0, BL - 1, 1)
            first_product(FIRST, 1)
            spread(0, BL - 1, 1)
            pe.wait_ge(normed[0], G * BL - 1)
            first_product(FIRST, 2)
            project(0, BL - 1)
            for step in range(SPAN):
                if step == UC:
                    pe.wait_ge(added[0], NT * BL)
                first_ahead(0, FIRST, step)
                if step in (0, 1):
                    turn(1, BL - 2, step)
                elif step in (2, 3):
                    turn(1, BL - 1, step - 2)
                elif step in (4, 5):
                    route(step - 2)
                second_product(0, FIRST, step)
                if step in (4, 5):
                    turn_logits(step - 2)
                elif step == 8:
                    pe.wait_ge(odds, BL)
            with pe.Fori(1, UNITS // 2 - 1) as v:
                for step in range(SPAN):
                    expert_step(v, MIDDLE, step)
            for step in range(SPAN):
                first_ahead(UNITS // 2 - 1, LAST, step)
                if step in (10, 11):
                    turn(2, 0, step - 10)
                elif step in (12, 13):
                    queries(0, step - 12)
                elif step in (14, 15):
                    turn(2, 1, step - 14)
                second_product(UNITS // 2 - 1, LAST, step)
            pe.wait_ge(kd_ready[B], 4 * G)
            pe.wait_ge(kd_ready[B + 1], 4 * G)
            row_scores(0, 0)
            row_scores(0, 1)
            pe.wait_ge(restmax, 1)
            queries(1, 0)
            turn_max(0)
            queries(1, 1)
            pe.wait_ge(max_ready, 1)
            attend1()
            weigh_pairs(1, BL - 1, 1)
            pe.wait_ge(normed[1], G * BL - 1)
            pe.wait_ge(u1_split, 2)
            low_rank_in(0)
            weigh_rest(1, BL - 1, 1)
            pe.wait_ge(v1_split, 2)
            for i in range(BL):
                low_rank(i)
            low_rank_out(BL - 1)

        @block.scalar
        def _(act):
            def turned_high_copy(s, i, k):
                if (s, i) not in order:
                    return
                n = KE * order[s, i] + k
                act.wait_ge(turned, n + 1)
                nc.scalar.activation(xTh[:, i, k, :], bank[:, turned_bank(s, i, k), :], ACT.Copy).then_inc(turned_high, 1)

            def cap_scores(i, n):
                g, c = divmod(n, NC)
                r = rows_of(c)
                act.wait_ge(scored[0], CG * i + n + 1)
                if CG * i + n >= 2:
                    act.wait_ge(prob[0], CG * i + n - 1)
                nc.scalar.activation(th[0:r, n % 2, :], bank[0:r, SC[n % 2], :], ACT.Tanh,
                                     scale=scale_q[0:r, :]).then_inc(capped, 1)

            def exponent(a, i, n):
                if n < 0:
                    i, n = i - 1, n + CG
                if i < 0:
                    return
                g, c = divmod(n, NC)
                r = rows_of(c)
                if i:
                    act.wait_ge(weighed[a], G * (i - 1) + g + 1)
                if a == 0:
                    act.wait_ge(capped, CG * i + n + 1)
                    part = c // PAIRS
                    nc.scalar.activation(pr[0:r, n, :], th[0:r, n % 2, :], ACT.Exp, scale=cap[0:r, 1:2],
                                         bias=ebias[0:r, i // NB, part:part + 1]).then_inc(prob[0], 1)
                else:
                    act.wait_ge(scored[1], CG * i + n + 1)
                    nc.scalar.activation(pr[0:r, n, :], bank[0:r, SC[n % 2], :], ACT.Exp,
                                         scale=DH ** -0.5).then_inc(prob[1], 1)

            def copy_weighed(a, i, g):
                if i < 0:
                    return
                act.wait_ge(weighed[a], G * i + g + 1)
                if i:
                    act.wait_ge(projected[a], NT // 2 * i)
                nc.scalar.activation(at[:, g, :], bank[:, OUT[g], :], ACT.Copy).then_inc(weighed_copied[a], 1)

            def queries_high(i, g):
                act.wait_ge(q_done, G * i + g + 1)
                nc.scalar.activation(qh[:, i % 2, g, :], bank[:, TURN, :], ACT.Identity,
                                     bias=bq_sb[:, g:g + 1]).then_inc(q_high, 1)

            def copy_max(i):
                act.wait_ge(max_turned, i + 1)
                nc.scalar.activation(mxT[:, i % 2, :], bank[0:32, max_bank(i), :], ACT.Copy).then_inc(max_ready, 1)

            def copy_logits(i):
                act.wait_ge(routed, i + 1)
                nc.scalar.activation(lg[0:NX, :], bank[0:NX, TURN, :], ACT.Copy).then_inc(logits, 1)

            def route_odds(i):
                act.wait_ge(logits_turned, i + 1)
                nc.scalar.activation(route_sb[:, 0, i * NT:(i + 1) * NT, :].rearrange("p t e -> p (t e)"),
                                     bank[:, TURN, 0:NT * NX], ACT.Exp, scale=-1.0).then_inc(odds, 1)

            def rectify(part, n, at_step):
                act.wait_ge(hidden, at_step)
                nc.scalar.activation(ur[:, n % 4, :], bank[:, hidden_bank(part, n), :], ACT.Relu).then_inc(rectified, 1)

            def hidden_high(part, n, at_step):
                act.wait_ge(squared, at_step)
                if part != FIRST or n >= 4:
                    act.wait_ge(down, at_step - (2 if part == LAST and STEPS <= n < SPAN else 4))
                nc.scalar.activation(hh[:, hidden_slot(part, n), :], hf[:, n % 4, :], ACT.Copy).then_inc(high, 1)

            def expert_step(v, part, step):
                if step + 2 < SPAN or part != LAST:
                    rectify(part, step + 2, v * SPAN + (step + 3))
                if step + 1 < SPAN or part != LAST:
                    hidden_high(part, step + 1, v * SPAN + (step + 2))

            def low_rank_high(i):
                if i >= BL:
                    return
                act.wait_ge(low1, i + 1)
                nc.scalar.activation(ph[:, i % 2, :], bank[0:RANK, DEN[0], :], ACT.Copy).then_inc(low1_high, 1)

            act.wait_ge(gates_loaded, 48)
            nc.scalar.activation(gate[:], gate_raw[:], ACT.Tanh).then_inc(gates_ready, 1)
            nc.scalar.activation(cap[:, 1:2], cap[:, 0:1], ACT.Exp).then_inc(gates_ready, 1)
            act.wait_ge(gates_ready, 2)
            nc.scalar.mul(cap[:, 2:3], cap[:, 1:2], -1.0).then_inc(gates_ready, 1)
            nc.scalar.mul(scale_q[:], scale_raw[:], DH ** -0.5).then_inc(gates_ready, 1)
            turned_high_copy(0, 0, 0)
            turned_high_copy(0, 0, 1)
            act.wait_ge(gates_ready, 4)
            act.wait_ge(chain, 1)
            for i in range(BL):
                for n in range(CG):
                    cap_scores(i, n)
                    exponent(0, i, n - 1)
                    if n == (3, 2, 0, 0)[i]:
                        turned_high_copy(0, i + 1, 0)
                    if n == 0:
                        copy_weighed(0, i - 1, 0)
                        if i == BL - 1:
                            copy_logits(0)
                    elif (i, n) == (BL - 1, 1):
                        route_odds(0)
                    elif n == 3:
                        copy_weighed(0, i - 1, 1)
                    if n == (3 if i else 5):
                        turned_high_copy(0, i + 1, 1)
                    if n in (5, 6):
                        turned_high_copy(1, i - 2, n - 5)
            exponent(0, BL - 1, CG - 1)
            copy_logits(1)
            copy_weighed(0, BL - 1, 0)
            route_odds(1)
            act.wait_ge(weighed[0], G * BL - 1)
            rectify(FIRST, 0, 1)
            copy_weighed(0, BL - 1, 1)
            rectify(FIRST, 1, 2)
            hidden_high(FIRST, 0, 1)
            for step in range(SPAN):
                expert_step(0, FIRST, step)
                if step in (0, 1):
                    turned_high_copy(1, BL - 2, step)
                elif step in (2, 3):
                    turned_high_copy(1, BL - 1, step - 2)
                elif step in (4, 5):
                    copy_logits(step - 2)
                    route_odds(step - 2)
            with act.Fori(1, UNITS // 2 - 1) as v:
                for step in range(SPAN):
                    expert_step(v, MIDDLE, step)
            for step in range(SPAN):
                expert_step(UNITS // 2 - 1, LAST, step)
                if step in (10, 11):
                    turned_high_copy(2, 0, step - 10)
                elif step in (12, 13):
                    queries_high(0, step - 12)
                elif step in (14, 15):
                    turned_high_copy(2, 1, step - 14)
            queries_high(1, 0)
            copy_max(0)
            queries_high(1, 1)
            for i in range(BL):
                last = i + 1 == BL
                for n in range(CG):
                    exponent(1, i, n)
                    if n == 4:
                        copy_weighed(1, i - 1, 1)
                    if n == 8:
                        copy_weighed(1, i, 0)
                    if n in (5, 6):
                        turned_high_copy(3, i - 2, n - 5)
                    if n in (1, 2) and i and not last:
                        queries_high(i + 1, n - 1)
                    if n == 7 and not last:
                        copy_max(i + 1)
                    if n >= 8:
                        turned_high_copy(2, i + 2, n - 8)
            low_rank_high(0)
            copy_weighed(1, BL - 1, 1)
            for i in range(BL):
                for n in range(NF):
                    m = NF * i + n
                    act.wait_ge(inner, m + 1)
                    if m >= 4:
                        act.wait_ge(low2, (m - 4) // 2 + 1)
                    nc.scalar.activation(gl[:, n % 4, :], bank[:, SC[n % 2], :], ACT.Gelu_apprx_tanh,
                                         bias=b1_sb[:, n:n + 1]).then_inc(gelu_done, 1)
                    if n == 5:
                        low_rank_high(i + 1)
                    if n == 6 and i < 2:
                        turned_high_copy(3, BL - 2 + i, 0)
                if i < 2:
                    turned_high_copy(3, BL - 2 + i, 1)

        @block.gpsimd
        def _(pool):
            def rsqrt(s, i):
                n = norm_at[s, i]
                pool.wait_ge(aggr, NT * (n + 1))
                if n:
                    pool.wait_ge(rstd_done, n)
                    pool.wait_ge(xn_done, NT * n)
                nc.gpsimd.tensor_tensor(veps[:], mv[:, :, 1], eps_sb[:], ALU.add).then_inc(vare, 1)
                pool.wait_ge(vare, n + 1)
                nc.gpsimd.tensor_tensor(rstd[:], veps[:], minus_half[:], ALU.pow).then_inc(rstd_done, 1)

            def add_bias(s, i):
                rows = xs[:, i * NT:(i + 1) * NT, :]
                pool.wait_ge(xn_done, NT * (norm_at[s, i] + 1))
                bias = (bo_rows, b2_rows)[s - 2]
                nc.gpsimd.tensor_tensor(rows, rows, bias[:].unsqueeze(1).to_broadcast([P, NT, E]),
                                        ALU.add).then_inc(biased, 1)

            def mask_values(l):
                for b in range(B):
                    main = vd[:, B * l + b, 0, :].rearrange("p (c n) -> p c n", n=32)
                    nc.gpsimd.tensor_tensor(main, main, same2.unsqueeze(1).to_broadcast([P, E // 32, 32]),
                                            ALU.mult).then_inc(vd_ready, 1)
                    rest = vd[:, B * l + b, 1, :].rearrange("p (g n) -> p g n", n=P)
                    nc.gpsimd.tensor_tensor(rest, rest, same8.unsqueeze(1).to_broadcast([P, G, P]),
                                            ALU.mult).then_inc(vd_ready, 1)

            def split_unit(s):
                nc.gpsimd.tensor_copy(unit_h[:, s], unit_raw[:, s]).then_inc(unit_high, 1)

            def hidden_low_part(part, n, signal):
                pool.wait_ge(high, (SPAN * (UNITS // 2 - 1) if part == LAST else 0) + n + 1)
                m = hidden_slot(part, n)
                nc.gpsimd.tensor_tensor(hl[:, m, :], hf[:, n % 4, :], hh[:, m, :].bitcast(F32),
                                        ALU.subtract).then_inc(signal, 1)

            def split_unit_low(s):
                nc.gpsimd.tensor_tensor(unit_l[:, s], unit_raw[:, s], unit_h[:, s].bitcast(F32),
                                        ALU.subtract).then_inc(unit_low, 1)

            nc.gpsimd.memset(minus_half[:], -0.5).then_inc(pool_ready, 1)
            nc.gpsimd.memset(eps_sb[:], EPS).then_inc(pool_ready, 1)
            pool.wait_ge(pool_ready, 2)
            rsqrt(0, 0)
            pool.wait_ge(vd_loaded, 64)
            pool.wait_ge(consts_loaded, 16)
            mask_values(0)
            rsqrt(0, 1)
            pool.wait_ge(keys_act, 2)
            for g in range(G):
                spread_keys(nc.gpsimd, 1, 1, g)
            for key in norms[2:norm_at[1, BL - 2]]:
                rsqrt(*key)
                if key == (1, 0):
                    pool.wait_ge(kv_copied, 4)
                    mask_values(1)
                    pool.wait_ge(mask1_loaded, 16 * 14)
                    pool.wait_ge(gates_ready, 4)
                    for n, rows in enumerate((bo_rows, b2_rows)):
                        nc.gpsimd.tensor_scalar(rows[:], rows[:], gate[:, n + 2:n + 3], None,
                                                ALU.mult).then_inc(pool_ready, 1)
                    nc.gpsimd.tensor_copy(u1h[:], u1_raw).then_inc(u1_split, 1)
                    pool.wait_ge(u1_split, 1)
                    nc.gpsimd.tensor_tensor(u1l[:], u1_raw, u1h[:].bitcast(F32), ALU.subtract).then_inc(u1_split, 1)
                elif key == (1, 1):
                    for s in range(2):
                        pool.wait_ge(unit_loaded[s], 32)
                        split_unit(s)
                        pool.wait_ge(unit_high, s + 1)
                        split_unit_low(s)
            pool.wait_ge(scored[0], CG * NB)
            for g in range(G):
                spread_keys(nc.gpsimd, 0, B, g)
            rsqrt(1, BL - 2)
            hidden_low_part(FIRST, 0, low_early)
            hidden_low_part(FIRST, 1, low_early)
            hidden_low_part(FIRST, 2, low_early)
            rsqrt(1, BL - 1)
            for step in range(3, EARLY):
                hidden_low_part(FIRST, step, low_early)
            with pool.Fori(1, UNITS // 2) as v:
                for s in range(2):
                    pool.wait_ge(unit_loaded[s], v * 32 + 32)
                    pool.wait_ge(down, v * SPAN - (0 if s else SPAN - FREED))
                    pool.sem_inc(carried_pool, 1)
                    split_unit(s)
                    pool.wait_ge(unit_high, v * 2 + (s + 1))
                    split_unit_low(s)
            pool.wait_ge(scored[0], CG * BL)
            for g in range(G):
                spread_keys(nc.gpsimd, 1, B + 1, g)
            for step in range(STEPS, SPAN):
                hidden_low_part(LAST, step, low_late)
                if step == 9:
                    rsqrt(2, 0)
                elif step == 13:
                    rsqrt(2, 1)
            pool.wait_ge(pool_ready, 2)
            add_bias(2, 0)
            add_bias(2, 1)
            for key in norms[norm_at[2, 2]:]:
                rsqrt(*key)
                add_bias(*key)
                if key == (2, 2):
                    pool.wait_ge(v1_loaded, 16)
                    nc.gpsimd.tensor_copy(v1h[:], v1_raw).then_inc(v1_split, 1)
                    pool.wait_ge(v1_split, 1)
                    nc.gpsimd.tensor_tensor(v1l[:], v1_raw, v1h[:].bitcast(F32), ALU.subtract).then_inc(v1_split, 1)

        @block.vector
        def _(dve):
            v = nc.vector
            chained = [0]

            def link(ins):
                chained[0] += 1
                ins.then_inc(chain, 1)
                dve.wait_ge(chain, chained[0])

            def norm(s, i):
                if (s, i) in norm_at:
                    norm_moments(s, i)
                    normalise_rows(s, i)

            def norm_moments(s, i):
                if (s, i) not in norm_at:
                    return
                n = norm_at[s, i]
                if s == 0:
                    dve.wait_ge(x_loaded[i], 16)
                elif s == 2:
                    dve.wait_ge(mixed, 2 * NT + NT * (BL * (UNITS - 2) + ORDER[LAST].index((1, i)) + 1))
                else:
                    dve.wait_ge(added[s // 2], NT * (i + 1))
                if n:
                    dve.wait_ge(aggr, NT * n)
                    dve.wait_ge(rstd_done, n)
                for t in range(NT):
                    v.bn_stats(bstat[:, t, :], xs[:, i * NT + t, :]).then_inc(stat, 1)
                dve.wait_ge(stat, NT * (n + 1))
                if n:
                    dve.wait_ge(xn_done, NT * n)
                for t in range(NT):
                    v.bn_aggr(mv[:, t, :], bstat[:, t, :]).then_inc(aggr, 1)

            def normalise_rows(s, i):
                if (s, i) not in norm_at:
                    return
                n = norm_at[s, i]
                dve.wait_ge(aggr, NT * (n + 1))
                dve.wait_ge(rstd_done, n + 1)
                last = [m for m in norms[:n] if slot[m] == slot[s, i]]
                if last:
                    dve.wait_ge(turned, KE * (order[last[-1]] + 1))
                for t in range(NT):
                    v.tensor_scalar(xn[:, slot[s, i], t, :], xs[:, i * NT + t, :], mv[:, t, 0:1], rstd[:, t:t + 1],
                                    ALU.subtract, ALU.mult).then_inc(xn_done, 1)

            def turned_low_part(s, i, k):
                if (s, i) not in order:
                    return
                dve.wait_ge(turned_high, KE * order[s, i] + k + 1)
                v.tensor_tensor(xTl[:, i, k, :], bank[:, turned_bank(s, i, k), :], xTh[:, i, k, :].bitcast(F32),
                                ALU.subtract).then_inc(turned_low, 1)

            def invert(a, i, g):
                if i < 0:
                    return
                dve.wait_ge(weighed[a], G * i + g + 1)
                if a or i or g:
                    dve.wait_ge(*((spreaded[a], G * i + g) if i or g else (spreaded[0], G * BL)))
                v.reciprocal(inv_sb[:], bank[:, DEN[g], 0:P]).then_inc(inverse[a], 1)

            def normalise(a, i, g):
                if i < 0:
                    return
                dve.wait_ge(spreaded[a], G * i + g + 1)
                dve.wait_ge(weighed_copied[a], G * i + g + 1)
                v.tensor_tensor(at[:, g, :], at[:, g, :], bank[:, DEN[g], :], ALU.mult).then_inc(normed[a], 1)

            def add(a, i):
                if i < 0:
                    return
                if a == 1:
                    dve.wait_ge(biased, bias_at[2, i])
                for t in range(NT):
                    dve.wait_ge(projected[a], NT // 2 * i + t // 2 + 1)
                    row = xs[:, i * NT + t, :]
                    v.scalar_tensor_tensor(out=row, in0=tile_of(PRJ, t), scalar=gate[:, 2 * a:2 * a + 1], in1=row,
                                           op0=ALU.mult, op1=ALU.add).then_inc(added[a], 1)

            def square(v_, part, n):
                dve.wait_ge(rectified, v_ * SPAN + (n + 1))
                if part != FIRST or n >= 4:
                    dve.wait_ge(high, v_ * SPAN + (n - 3))
                    wait_low(dve, v_, part, n - 4)
                v.tensor_tensor(hf[:, n % 4, :], bank[:, hidden_bank(part, n), :], ur[:, n % 4, :],
                                ALU.mult).then_inc(squared, 1)

            def hidden_low(v_, part, n):
                dve.wait_ge(high, v_ * SPAN + (n + 1))
                m = hidden_slot(part, n)
                v.tensor_tensor(hl[:, m, :], hf[:, n % 4, :], hh[:, m, :].bitcast(F32), ALU.subtract).then_inc(low, 1)

            def router_views(t0, t1):
                tiles = slice(t0, t1)
                return ([route_sb[:, i, tiles] for i in range(6)] + [rone[:, i, tiles] for i in range(7)],
                        lambda column: column.unsqueeze(2).to_broadcast([P, t1 - t0, NX]),
                        rank_of_expert.unsqueeze(1).to_broadcast([P, t1 - t0, NX]))

            def choose_first(t0, t1):
                (odd, p, key, one1, one2, w, m1, k1, m2, k2, den, inv, ginv), wide, lower = router_views(t0, t1)
                dve.wait_ge(odds, t1 // NT)
                link(v.tensor_scalar(w, odd, 1.0, None, ALU.add))
                link(v.reciprocal(p, w))
                link(v.tensor_reduce(m1, p, AX.X, ALU.max))
                link(v.tensor_tensor(key, p, wide(m1), ALU.is_equal))
                link(v.tensor_tensor(key, key, lower, ALU.mult))
                link(v.tensor_reduce(k1, key, AX.X, ALU.max))
                link(v.tensor_tensor(one1, key, wide(k1), ALU.is_equal))
                link(v.scalar_tensor_tensor(out=w, in0=one1, scalar=-4.0, in1=p, op0=ALU.mult, op1=ALU.add))

            def choose_second(t0, t1):
                (odd, p, key, one1, one2, w, m1, k1, m2, k2, den, inv, ginv), wide, lower = router_views(t0, t1)
                link(v.tensor_reduce(m2, w, AX.X, ALU.max))
                link(v.tensor_tensor(key, w, wide(m2), ALU.is_equal))
                link(v.tensor_tensor(key, key, lower, ALU.mult))
                link(v.tensor_reduce(k2, key, AX.X, ALU.max))
                link(v.tensor_tensor(one2, key, wide(k2), ALU.is_equal))
                link(v.tensor_tensor(one1, one1, one2, ALU.add))
                link(v.scalar_tensor_tensor(out=den, in0=m1, scalar=1e-20, in1=m2, op0=ALU.add, op1=ALU.add))
                link(v.reciprocal(inv, den))
                link(v.tensor_scalar(ginv, inv, gate[:, 1:2], None, ALU.mult))
                link(v.tensor_tensor(w, p, one1, ALU.mult))
                link(v.tensor_tensor(w, w, wide(ginv), ALU.mult))
                tiles, wt = slice(t0, t1), w.rearrange("p t e -> p e t")
                narrow = sum(width == UW for width in WIDTHS)
                per = WIDTHS[-1] // UW
                link(v.tensor_copy(comb[:, 0:narrow, tiles], wt[:, 0:narrow, :]))
                link(v.tensor_copy(comb[:, narrow:, tiles].rearrange("p (e r) t -> p e r t", r=per),
                                   wt[:, narrow:, :].unsqueeze(2).to_broadcast([P, NX - narrow, per, t1 - t0])))
                v.tensor_copy(comb_now[:, :, tiles], comb[:, 0:2, tiles]).then_inc(comb_ready, 1)

            def prepare_hidden(v_, part, step):
                if step + 2 < SPAN or part != LAST:
                    square(v_, part, step + 2)
                if part == MIDDLE or (part == FIRST and step + 1 >= EARLY) or (part == LAST and step + 1 < STEPS):
                    hidden_low(v_, part, step + 1)

            def mix(v_, part, pair):
                s, i = ORDER[part][pair]
                if part == FIRST:
                    dve.wait_ge(comb_ready, 1 if i < 2 else 2)
                elif pair == 0:
                    dve.wait_ge(comb_ready, v_ + 2)
                dve.wait_ge(mixed, v_ * (2 * BL * NT) + (pair + 2) * NT)
                dve.wait_ge(down, v_ * SPAN + (pair + 1) * UC)
                for t in range(NT):
                    tt = i * NT + t
                    v.scalar_tensor_tensor(out=xs[:, tt, :], in0=tile_of(output_banks(part, pair), t),
                                           scalar=comb_now[:, s, tt:tt + 1], in1=xs[:, tt, :],
                                           op0=ALU.mult, op1=ALU.add).then_inc(mixed, 1)

            def weights_of_units(v_):
                dve.wait_ge(mixed, v_ * (2 * BL * NT) + 2 * NT)
                v.tensor_copy(comb_now[:], comb[:, bass.ts(v_, 2), :]).then_inc(comb_ready, 1)

            def queries_low(i, g):
                dve.wait_ge(q_high, G * i + g + 1)
                v.scalar_tensor_tensor(out=ql[:, i % 2, g, :], in0=bank[:, TURN, :], scalar=bq_sb[:, g:g + 1],
                                       in1=qh[:, i % 2, g, :].bitcast(F32), op0=ALU.add,
                                       op1=ALU.subtract).then_inc(q_low, 1)

            def row_max(i):
                if i:
                    dve.wait_ge(max_turned, i)
                    dve.wait_ge(split_max, 2 * i)
                for g in range(G):
                    for t in range(NT):
                        m = g * NT + t
                        dve.wait_ge(rowscores, G * NT * i + m + 1)
                        v.tensor_reduce(mx[:, t, g * HG:(g + 1) * HG],
                                        bank[:, SC[m % 2], :].rearrange("p (c k h) -> p c h k", c=PAIRS, h=2),
                                        AX.X, ALU.max).then_inc(rowmax, 1)
                    dve.wait_ge(rowrest, G * i + g + 1)
                    v.tensor_reduce(mxl[:, :, g * HG:(g + 1) * HG],
                                    bank[:, REST[g], 0:NT * RL].rearrange("p (t k h) -> p t h k", t=NT, h=HG),
                                    AX.X, ALU.max).then_inc(restmax, 1)
                dve.wait_ge(rowmax, G * NT * (i + 1))
                dve.wait_ge(restmax, G * (i + 1))
                link(v.tensor_tensor(mx, mx, mxl, ALU.max))
                v.tensor_copy(mxs[:, :, 0, :].bitcast(F32R), mx).then_inc(split_max, 1)
                dve.wait_ge(split_max, 2 * i + 1)
                v.tensor_tensor(mxs[:, :, 1, :], mx, mxs[:, :, 0, :], ALU.subtract).then_inc(split_max, 1)

            def low_rank_low(i):
                if i >= BL:
                    return
                dve.wait_ge(low1_high, i + 1)
                v.tensor_tensor(pl[:, i % 2, :], bank[0:RANK, DEN[0], :], ph[:, i % 2, :].bitcast(F32),
                                ALU.subtract).then_inc(low1_low, 1)

            def result(i):
                if i < 0:
                    return
                dve.wait_ge(biased, bias_at[3, i])
                for t in range(NT):
                    dve.wait_ge(ffn_done, NT // 2 * i + t // 2 + 1)
                    row = xs[:, i * NT + t, :]
                    v.scalar_tensor_tensor(out=row, in0=tile_of(PRJ, t), scalar=gate[:, 3:4], in1=row,
                                           op0=ALU.mult, op1=ALU.add).then_inc(res_done, 1)

            def widen(b):
                link(v.tensor_copy(ctx_wide[:, :, 0:P].rearrange("p k (n h) -> p k n h", h=2),
                                   cT[:, b, :, 0:KM].unsqueeze(3).to_broadcast([P, KE, KM, 2])))
                v.tensor_copy(ctx_wide[:, :, P:P + RL].rearrange("p k (n h) -> p k n h", h=HG),
                              cT[:, b, :, KM:KEYS].unsqueeze(3).to_broadcast([P, KE, KL, HG])).then_inc(keys_split, 1)

            def layer1_context():
                for b in range(B):
                    dve.wait_ge(kv_done, b + 1)
                    for g in range(G):
                        link(v.tensor_scalar(k1[:, b, g, :], bank[:, DEN[b], g * 128:g * 128 + KEYS],
                                             bk_sb[:, g:g + 1], None, ALU.add))
                    link(v.tensor_copy(kh[:, B + b], k1[:, b]))
                    v.tensor_tensor(kl[:, B + b], k1[:, b], kh[:, B + b].bitcast(F32),
                                    ALU.subtract).then_inc(kv_copied, 1)
                for b in range(B):
                    dve.wait_ge(kv_done, B + b + 1)
                    link(v.tensor_tensor(vd[:, B + b, 0, :], bank[:, OUT[b], 0:E], bv_rows, ALU.add))
                    v.tensor_tensor(vd[0:RL, B + b, 1, :], bank[0:RL, OUT[b], E:2 * E], bv_rows[0:RL],
                                    ALU.add).then_inc(kv_copied, 1)
                    if b + 1 < B:
                        widen(b + 1)
                        turned_low_part(0, 1, 1)

            def mask_copied(b):
                dve.wait_ge(kv_done, 2 * B + b + 1)
                v.tensor_copy(mbT[:, b * S:(b + 1) * S], bank[0:KEYS, PRJ[0], :].bitcast(BF16)).then_inc(kv_copied, 1)

            def layer1_mask():
                dve.wait_ge(mask1_loaded, 16 * 14)
                v.tensor_copy(ident_b[:], ident).then_inc(ready, 1)
                v.tensor_copy(rows_of_key[:], key_raw).then_inc(ready, 1)
                v.tensor_copy(minus_head[:].rearrange("p g n -> p (g n)"), minus_raw).then_inc(ready, 1)
                v.tensor_scalar(mbias[:], mask1_sb, 0.0, MASKED, ALU.is_equal, ALU.mult).then_inc(ready, 1)

            def layer1_weights():
                v.tensor_copy(rth[:], rt_raw[:]).then_inc(ready, 1)
                v.tensor_copy(wqh[:], wq_raw).then_inc(ready, 1)
                dve.wait_ge(ready, 6)
                v.tensor_tensor(wql[:], wq_raw, wqh[:].bitcast(F32), ALU.subtract).then_inc(ready, 1)
                v.tensor_tensor(rtl[:], rt_raw[:], rth[:].bitcast(F32), ALU.subtract).then_inc(ready, 1)

            v.memset(mask0_sb[:], 0).then_inc(cleared, 1)
            v.memset(vd[:], 0.0).then_inc(cleared, 1)
            norm_moments(0, 0)
            dve.wait_ge(context_loaded, 16 * B)
            v.tensor_copy(kh[:, 0:B], cT[:]).then_inc(keys_act, 1)
            dve.wait_ge(keys_act, 1)
            v.tensor_tensor(kl[:, 0:B], cT[:], kh[:, 0:B].bitcast(F32), ALU.subtract).then_inc(keys_act, 1)
            normalise_rows(0, 0)
            dve.wait_ge(consts_loaded, 16)
            dve.wait_ge(keys_act, 2)
            spread_keys(v, 0, 0, 0)
            turned_low_part(0, 0, 0)
            turned_low_part(0, 0, 1)
            spread_keys(v, 0, 0, 1)
            dve.wait_ge(gates_ready, 4)
            dve.wait_ge(mask0_loaded, 16 * 2 * B)
            link(v.tensor_scalar(ebias[:], mask0_sb[:], REMOVED, cap[:, 2:3], ALU.mult, ALU.add))
            norm(0, 1)
            for i in range(BL):
                invert(0, i - 1, 0)
                if i == 1:
                    mask_copied(0)
                if i == 0:
                    dve.wait_ge(weights_loaded, 16 * 5)
                    widen(0)
                turned_low_part(0, i + 1, 0)
                if i == 0:
                    layer1_context()
                normalise(0, i - 1, 0)
                invert(0, i - 1, 1)
                if i:
                    turned_low_part(0, i + 1, 1)
                if i == 1:
                    mask_copied(1)
                if i == 0:
                    layer1_mask()
                    layer1_weights()
                norm_moments(0, i + 2)
                normalise(0, i - 1, 1)
                normalise_rows(0, i + 2)
                turned_low_part(1, i - 2, 0)
                turned_low_part(1, i - 2, 1)
                add(0, i - 1)
                norm(1, i - 1)
            invert(0, BL - 1, 0)
            normalise(0, BL - 1, 0)
            dve.wait_ge(u1_split, 2)
            choose_first(0, 2 * NT)
            square(0, FIRST, 0)
            invert(0, BL - 1, 1)
            normalise(0, BL - 1, 1)
            dve.sem_inc(mixed, 2 * NT)
            square(0, FIRST, 1)
            prepare_hidden(0, FIRST, 0)
            choose_second(0, 2 * NT)
            add(0, BL - 1)
            norm_moments(1, BL - 1)
            turned_low_part(1, BL - 2, 0)
            prepare_hidden(0, FIRST, 1)
            turned_low_part(1, BL - 2, 1)
            prepare_hidden(0, FIRST, 2)
            normalise_rows(1, BL - 1)
            mix(0, FIRST, 0)
            turned_low_part(1, BL - 1, 0)
            prepare_hidden(0, FIRST, 3)
            turned_low_part(1, BL - 1, 1)
            mix(0, FIRST, 1)
            for step in range(4, SPAN):
                prepare_hidden(0, FIRST, step)
                if step == 6:
                    choose_first(2 * NT, AT)
                elif step == 7:
                    choose_second(2 * NT, AT)
                if step % UC == UC - 1:
                    mix(0, FIRST, step // UC)
            with dve.Fori(1, UNITS // 2 - 1) as v_:
                weights_of_units(v_)
                for step in range(SPAN):
                    prepare_hidden(v_, MIDDLE, step)
                    if step % UC == UC - 1:
                        mix(v_, MIDDLE, step // UC)
            weights_of_units(UNITS // 2 - 1)
            for step in range(SPAN):
                prepare_hidden(UNITS // 2 - 1, LAST, step)
                if step == 9:
                    normalise_rows(2, 0)
                elif step in (10, 11):
                    turned_low_part(2, 0, step - 10)
                elif step in (12, 13):
                    queries_low(0, step - 12)
                elif step in (14, 15):
                    turned_low_part(2, 1, step - 14)
                if step == 13:
                    normalise_rows(2, 1)
                if step % UC == UC - 1:
                    mix(UNITS // 2 - 1, LAST, step // UC)
                if step == 7:
                    norm_moments(2, 0)
                elif step == 11:
                    norm_moments(2, 1)
            row_max(0)
            queries_low(1, 0)
            queries_low(1, 1)
            norm(2, 2)
            for i in range(BL):
                last = i + 1 == BL
                if i and not last:
                    queries_low(i + 1, 0)
                    queries_low(i + 1, 1)
                invert(1, i - 1, 1)
                normalise(1, i - 1, 1)
                if not last:
                    row_max(i + 1)
                turned_low_part(3, i - 2, 0)
                turned_low_part(3, i - 2, 1)
                add(1, i - 1)
                invert(1, i, 0)
                norm_moments(3, i - 1)
                normalise(1, i, 0)
                turned_low_part(2, i + 2, 0)
                normalise_rows(3, i - 1)
                turned_low_part(2, i + 2, 1)
                norm(2, i + 3)
            low_rank_low(0)
            invert(1, BL - 1, 1)
            normalise(1, BL - 1, 1)
            add(1, BL - 1)
            for i in range(BL):
                result(i - 1)
                low_rank_low(i + 1)
                if i < 2:
                    turned_low_part(3, BL - 2 + i, 0)
                    turned_low_part(3, BL - 2 + i, 1)
                dve.wait_ge(low2, NF // 2 * (i + 1))
                v.tensor_copy(qq[:, i % 2, :], bank[:, OUT[i % 2], :]).then_inc(low2_copied, 1)
                if i == 0:
                    norm(3, BL - 1)
            result(BL - 1)


def kernel(**inputs):
    import numpy as _np
    import concourse.bacc as _bacc
    from concourse import mybir as _mybir
    from concourse.bass_utils import run_bass_kernel_spmd as _run

    a = {k: _np.asarray(v) for k, v in inputs.items()}
    hd = 2 * DH
    w_kv = a["L1_xattn_W_kv"].reshape(E, H, hd)
    b_kv = a["L1_xattn_b_kv"].reshape(H, hd)
    r = _np.arange(P)
    row = _np.arange(ROWS)
    main = row < PAIRS * P
    key_of_row = _np.where(main, row % P // 2, KM + (row - PAIRS * P) // HG)
    head_of_row = _np.where(main, row // P * 2 + row % 2, (row - PAIRS * P) % HG)
    consts = _np.zeros((P, C_END), _np.float32)
    consts[:, C_EYE:C_SAME2] = _np.eye(P)
    consts[:, C_SAME2:C_SAME8] = (r[:, None] % 2) == (_np.arange(32)[None, :] // DH)
    consts[:, C_SAME8:C_HEAD] = (r[:, None] % HG) == (r[None, :] // DH)
    consts[:, C_HEAD:C_RANK] = (r[:, None] // DH) == _np.arange(HG)[None, :]
    consts[:, C_RANK:C_SUM2] = NX - _np.arange(NX)
    consts[:, C_SUM2:C_SUM8] = (_np.arange(32 + HG - 2)[None, :] + 2 - r[:, None] % 2) % HG == 0
    consts[:, C_SUM8:C_SPREAD] = (_np.arange(32)[None, :] % HG) == (r[:, None] % HG)
    for t in range(NT):
        consts[:, C_SPREAD + t * P:C_SPREAD + (t + 1) * P] = r[:, None] == 32 * t + r[None, :] // DH
    for g in range(G):
        consts[0:32, C_MINUS + g * ROWS:C_MINUS + (g + 1) * ROWS] = \
            -((_np.arange(32)[:, None] % H) == (g * HG + head_of_row[None, :])).astype(_np.float32)
    consts[0:KEYS, C_KEY:C_END] = _np.arange(KEYS)[:, None] == key_of_row[None, :]
    named = {
        "x": a["x"],
        "ctx_rows": a["ctx_1024"],
        "ctx_t": a["ctx_1024"].transpose(0, 2, 1),
        "mask0": a["mask_Bx1xS2_bk0"].reshape(B, KEYS),
        "mask1": a["mask_BxSxS2_ik0"],
        "gates": _np.stack([a["g_xattn"][0], a["g_ffn"][0], a["g_xattn"][1], a["g_ffn"][1]]),
        "logc": a["L0_xattn_log_C"].reshape(1),
        "scale0": a["L0_xattn_scale"].reshape(1),
        "w_out_t": a["L0_xattn_W_out"].T,
        "router_t": a["L0_ffn_router_w"].T,
        "w1": a["L0_ffn_w1"],
        "w2": a["L0_ffn_w2"],
        "wk": w_kv[:, :, :DH].reshape(E, E),
        "wv": w_kv[:, :, DH:].reshape(E, E),
        "bk": b_kv[:, :DH].reshape(G, P).T,
        "bv": b_kv[:, DH:].reshape(E),
        "wq": a["L1_xattn_W_q"],
        "bq": a["L1_xattn_b_q"].reshape(G, P).T,
        "wo": a["L1_xattn_W_o"],
        "bo": a["L1_xattn_b_o"],
        "u1": a["L1_ffn_U1"],
        "v1": a["L1_ffn_V1"],
        "b1": a["L1_ffn_b1"].reshape(NF, P).T,
        "u2": a["L1_ffn_U2"],
        "v2": a["L1_ffn_V2"],
        "b2": a["L1_ffn_b2"],
        "consts": consts,
    }
    nc = _bacc.Bacc("TRN2", target_bir_lowering=False, num_devices=1)
    arrays, args = {}, []
    for name, v in named.items():
        v = _np.ascontiguousarray(v)
        arrays[f"in_{name}"] = v
        args.append(nc.dram_tensor(f"in_{name}", v.shape, _mybir.dt.from_np(v.dtype), kind="ExternalInput").ap())
    args.append(nc.dram_tensor("out_0", (B, S, E), F32, kind="ExternalOutput").ap())
    flamingo(nc, *args)
    result = _run(nc, [arrays], core_ids=[0])
    return result.results[0]["out_0"]
```
